# Optimizing a Trainium2 kernel written in Bass

```python
import numpy as np
import jax
import jax.numpy as jnp

def _softmax(x, axis=-1):
    return jax.nn.softmax(x, axis=axis)

def _gelu(x):
    return jax.nn.gelu(x, approximate=True)

def _silu(x):
    return jax.nn.silu(x)

def _sigmoid(x):
    return jax.nn.sigmoid(x)

def _layernorm(x, axis=-1, eps=1e-05):
    m = jnp.mean(x, axis=axis, keepdims=True)
    v = jnp.var(x, axis=axis, keepdims=True)
    return (x - m) / jnp.sqrt(v + eps)

def _scatter_add(tgt, idx, src, axis=0):
    return tgt.at[idx].add(src)

def _segment_sum(src, seg, n):
    return jax.ops.segment_sum(src, seg, n)
kernel_name = 'mk_sandwich_d1_jaxref_r8_13f8a5'

def setup_inputs(seed: int=0):
    np.random.seed(seed)
    _w = jnp.asarray

    def _L0_attn_setup():
        import jax, jax.numpy as jnp
        import numpy as np
        HEADS, DIM_HEAD, LANDMARKS, PINV_ITERS = (8, 64, 32, 6)
        WQK_DIM = 32
        CONV_K = 33

        def moore_penrose_pinv(x, iters):
            I = jnp.eye(x.shape[-1], dtype=x.dtype)
            abs_x = jnp.abs(x)
            scale = jnp.max(abs_x.sum(-1)) * jnp.max(abs_x.sum(-2))
            z = jnp.swapaxes(x, -1, -2) / scale
            for _ in range(iters):
                xz = x @ z
                z = 0.25 * z @ (13 * I - xz @ (15 * I - xz @ (7 * I - xz)))
            return z

        def nystrom_attention(x, qkv_w, out_w, out_b, conv_w):
            b, n, d = x.shape
            h, dh, m = (HEADS, DIM_HEAD, LANDMARKS)
            scale = dh ** (-0.5)
            qkv = x @ qkv_w
            q, k, v = jnp.split(qkv, 3, axis=-1)
            split = lambda t: t.reshape(b, n, h, dh).transpose(0, 2, 1, 3)
            q, k, v = (split(q) * scale, split(k), split(v))
            l = n // m
            q_l = q.reshape(b, h, m, l, dh).mean(axis=3)
            k_l = k.reshape(b, h, m, l, dh).mean(axis=3)
            attn1 = jax.nn.softmax(jnp.einsum('bhid,bhjd->bhij', q, k_l), axis=-1)
            attn2 = jax.nn.softmax(jnp.einsum('bhid,bhjd->bhij', q_l, k_l), axis=-1)
            attn3 = jax.nn.softmax(jnp.einsum('bhid,bhjd->bhij', q_l, k), axis=-1)
            attn2_inv = moore_penrose_pinv(attn2, PINV_ITERS)
            out = attn1 @ (attn2_inv @ (attn3 @ v))
            pad = CONV_K // 2
            res = jax.lax.conv_general_dilated(v, conv_w, window_strides=(1, 1), padding=((pad, pad), (0, 0)), dimension_numbers=('NCHW', 'OIHW', 'NCHW'), feature_group_count=h)
            out = out + res
            out = out.transpose(0, 2, 1, 3).reshape(b, n, h * dh)
            return out @ out_w + out_b

        def _reference_tuple_inner(dense, adj_rows, adj_cols, adj_vals, wq, wk, wv_w, wv_b, qkv_w, out_w, out_b, conv_w):
            b, n, d = dense.shape
            xg = nystrom_attention(dense, qkv_w, out_w, out_b, conv_w)
            enc = xg[0] + dense
            q = enc @ wq
            k = enc @ wk
            scores = jnp.einsum('bid,bjd->bij', q, k) / jnp.sqrt(jnp.float32(WQK_DIM))
            data = scores[0]
            contrib = adj_vals * data[adj_rows, adj_cols]
            A_raw = jax.ops.segment_sum(contrib, adj_rows, num_segments=n)
            alpha = jax.nn.softmax(A_raw)
            value = dense @ wv_w + wv_b
            xl = alpha[:, None] * value
            wei = jax.nn.sigmoid(-xl)
            sw = wei * wei
            xo = xl * 2 * sw + 2 * enc * (1 - sw)
            return (xo, A_raw)
        key = jax.random.key(seed)
        ks = jax.random.split(key, 12)
        n, d, E = (1024, 128, 16384)
        inner = HEADS * DIM_HEAD
        s = lambda fan: (1.0 / np.sqrt(fan)).astype(np.float32) if isinstance(fan, np.ndarray) else np.float32(1.0 / np.sqrt(fan))
        return {'dense': jax.random.normal(ks[0], (1, n, d), jnp.float32), 'adj_rows': jax.random.randint(ks[1], (E,), 0, n), 'adj_cols': jax.random.randint(ks[2], (E,), 0, n), 'adj_vals': jax.random.uniform(ks[3], (E,), jnp.float32), 'wq': jax.random.normal(ks[4], (d, WQK_DIM), jnp.float32) * s(d), 'wk': jax.random.normal(ks[5], (d, WQK_DIM), jnp.float32) * s(d), 'wv_w': jax.random.normal(ks[6], (d, d), jnp.float32) * s(d), 'wv_b': jnp.zeros((d,), jnp.float32), 'qkv_w': jax.random.normal(ks[7], (d, 3 * inner), jnp.float32) * s(d), 'out_w': jax.random.normal(ks[8], (inner, d), jnp.float32) * s(inner), 'out_b': jnp.zeros((d,), jnp.float32), 'conv_w': jax.random.normal(ks[9], (HEADS, 1, CONV_K, 1), jnp.float32) * s(CONV_K)}
    _L0_attn_in = _L0_attn_setup()

    def _L0_ffn_setup():
        import jax, jax.numpy as jnp
        import numpy as np
        B, L, D = (4, 64, 128)
        E, TOP_K = (16, 4)
        F = 4 * D
        key = jax.random.key(seed)
        ks = jax.random.split(key, 6)
        scale = 0.02
        return {'x': jax.random.normal(ks[0], (B, L, D), jnp.float32), 'keys': jax.random.normal(ks[1], (E, D), jnp.float32), 'w1': jax.random.normal(ks[2], (E, F, D), jnp.float32) * scale, 'b1': jnp.zeros((E, F), jnp.float32), 'w2': jax.random.normal(ks[3], (E, D, F), jnp.float32) * scale, 'b2': jnp.zeros((E, D), jnp.float32), 'rw': jax.random.normal(ks[4], (E, D), jnp.float32) * scale, 'rb': jnp.zeros((E,), jnp.float32)}
    _L0_ffn_in = _L0_ffn_setup()
    _d = {'L0_attn_dense': _L0_attn_in['dense'], 'L0_attn_adj_rows': _L0_attn_in['adj_rows'], 'L0_attn_adj_cols': _L0_attn_in['adj_cols'], 'L0_attn_adj_vals': _L0_attn_in['adj_vals'], 'L0_attn_wq': _L0_attn_in['wq'], 'L0_attn_wk': _L0_attn_in['wk'], 'L0_attn_wv_w': _L0_attn_in['wv_w'], 'L0_attn_wv_b': _L0_attn_in['wv_b'], 'L0_attn_qkv_w': _L0_attn_in['qkv_w'], 'L0_attn_out_w': _L0_attn_in['out_w'], 'L0_attn_out_b': _L0_attn_in['out_b'], 'L0_attn_conv_w': _L0_attn_in['conv_w'], 'L0_ffn_keys': _L0_ffn_in['keys'], 'L0_ffn_w1': _L0_ffn_in['w1'], 'L0_ffn_b1': _L0_ffn_in['b1'], 'L0_ffn_w2': _L0_ffn_in['w2'], 'L0_ffn_b2': _L0_ffn_in['b2'], 'L0_ffn_rw': _L0_ffn_in['rw'], 'L0_ffn_rb': _L0_ffn_in['rb']}
    _x0 = _d['L0_attn_dense']
    _d['L0_attn_dense'] = jax.random.normal(jax.random.fold_in(jax.random.key(seed), 1), (8, 512, 128), dtype=_x0.dtype)
    del _x0
    return _d

def reference(L0_attn_dense, L0_attn_adj_rows, L0_attn_adj_cols, L0_attn_adj_vals, L0_attn_wq, L0_attn_wk, L0_attn_wv_w, L0_attn_wv_b, L0_attn_qkv_w, L0_attn_out_w, L0_attn_out_b, L0_attn_conv_w, L0_ffn_keys, L0_ffn_w1, L0_ffn_b1, L0_ffn_w2, L0_ffn_b2, L0_ffn_rw, L0_ffn_rb):

    def _L0_attn_ref(dense, adj_rows, adj_cols, adj_vals, wq, wk, wv_w, wv_b, qkv_w, out_w, out_b, conv_w):
        import jax, jax.numpy as jnp
        import numpy as np
        HEADS, DIM_HEAD, LANDMARKS, PINV_ITERS = (8, 64, 32, 6)
        WQK_DIM = 32
        CONV_K = 33

        def moore_penrose_pinv(x, iters):
            I = jnp.eye(x.shape[-1], dtype=x.dtype)
            abs_x = jnp.abs(x)
            scale = jnp.max(abs_x.sum(-1)) * jnp.max(abs_x.sum(-2))
            z = jnp.swapaxes(x, -1, -2) / scale
            for _ in range(iters):
                xz = x @ z
                z = 0.25 * z @ (13 * I - xz @ (15 * I - xz @ (7 * I - xz)))
            return z

        def nystrom_attention(x, qkv_w, out_w, out_b, conv_w):
            b, n, d = x.shape
            h, dh, m = (HEADS, DIM_HEAD, LANDMARKS)
            scale = dh ** (-0.5)
            qkv = x @ qkv_w
            q, k, v = jnp.split(qkv, 3, axis=-1)
            split = lambda t: t.reshape(b, n, h, dh).transpose(0, 2, 1, 3)
            q, k, v = (split(q) * scale, split(k), split(v))
            l = n // m
            q_l = q.reshape(b, h, m, l, dh).mean(axis=3)
            k_l = k.reshape(b, h, m, l, dh).mean(axis=3)
            attn1 = jax.nn.softmax(jnp.einsum('bhid,bhjd->bhij', q, k_l), axis=-1)
            attn2 = jax.nn.softmax(jnp.einsum('bhid,bhjd->bhij', q_l, k_l), axis=-1)
            attn3 = jax.nn.softmax(jnp.einsum('bhid,bhjd->bhij', q_l, k), axis=-1)
            attn2_inv = moore_penrose_pinv(attn2, PINV_ITERS)
            out = attn1 @ (attn2_inv @ (attn3 @ v))
            pad = CONV_K // 2
            res = jax.lax.conv_general_dilated(v, conv_w, window_strides=(1, 1), padding=((pad, pad), (0, 0)), dimension_numbers=('NCHW', 'OIHW', 'NCHW'), feature_group_count=h)
            out = out + res
            out = out.transpose(0, 2, 1, 3).reshape(b, n, h * dh)
            return out @ out_w + out_b

        def _reference_tuple_inner(dense, adj_rows, adj_cols, adj_vals, wq, wk, wv_w, wv_b, qkv_w, out_w, out_b, conv_w):
            b, n, d = dense.shape
            xg = nystrom_attention(dense, qkv_w, out_w, out_b, conv_w)
            enc = xg[0] + dense
            q = enc @ wq
            k = enc @ wk
            scores = jnp.einsum('bid,bjd->bij', q, k) / jnp.sqrt(jnp.float32(WQK_DIM))
            data = scores[0]
            contrib = adj_vals * data[adj_rows, adj_cols]
            A_raw = jax.ops.segment_sum(contrib, adj_rows, num_segments=n)
            alpha = jax.nn.softmax(A_raw)
            value = dense @ wv_w + wv_b
            xl = alpha[:, None] * value
            wei = jax.nn.sigmoid(-xl)
            sw = wei * wei
            xo = xl * 2 * sw + 2 * enc * (1 - sw)
            return (xo, A_raw)
        return _reference_tuple_inner(dense, adj_rows, adj_cols, adj_vals, wq, wk, wv_w, wv_b, qkv_w, out_w, out_b, conv_w)[0]

    def _L0_ffn_ref(x, keys, w1, b1, w2, b2, rw, rb):
        import jax, jax.numpy as jnp
        import numpy as np
        B, L, D = (4, 64, 128)
        E, TOP_K = (16, 4)
        F = 4 * D
        diff = x[:, :, None, :] - keys
        dist2 = jnp.sum(diff * diff, axis=-1)
        logits = -dist2 + jnp.einsum('bld,ed->ble', x, rw) + rb
        topv, topi = jax.lax.top_k(logits, TOP_K)
        w = jax.nn.softmax(topv, axis=-1)
        hidden = jax.nn.gelu(jnp.einsum('bld,efd->blef', x, w1) + b1, approximate=False)
        exp_out = jnp.einsum('blef,edf->bled', hidden, w2) + b2
        sel = jnp.take_along_axis(exp_out, topi[..., None], axis=2)
        fused = jnp.sum(w[..., None] * sel, axis=2)
        return fused
    x = L0_attn_dense
    x = x + _layernorm(_L0_attn_ref(_layernorm(x, axis=-1), L0_attn_adj_rows, L0_attn_adj_cols, L0_attn_adj_vals, L0_attn_wq, L0_attn_wk, L0_attn_wv_w, L0_attn_wv_b, L0_attn_qkv_w, L0_attn_out_w, L0_attn_out_b, L0_attn_conv_w), axis=-1)
    x = x + _layernorm(_L0_ffn_ref(_layernorm(x, axis=-1), L0_ffn_keys, L0_ffn_w1, L0_ffn_b1, L0_ffn_w2, L0_ffn_b2, L0_ffn_rw, L0_ffn_rb), axis=-1)
    return x

_drawn_inputs = setup_inputs


def setup_inputs(seed=0):
    import zlib

    import numpy as np

    out = dict(_drawn_inputs(seed))
    spreads = {'L0_attn_wv_b': (0.0, 0.8),
     'L0_attn_out_b': (0.0, 0.1),
     'L0_ffn_b1': (0.0, 0.1),
     'L0_ffn_b2': (0.0, 0.1),
     'L0_ffn_rb': (0.0, 0.8)}
    factors = {'L0_attn_adj_vals': 3.797,
     'L0_attn_wq': 4.042,
     'L0_attn_wk': 4.391,
     'L0_attn_wv_w': 3.844,
     'L0_ffn_rw': 2.833}
    for name, (base, spread) in spreads.items():
        noise = np.random.default_rng([zlib.crc32(name.encode()), seed]).standard_normal(out[name].shape)
        drawn = base * np.exp(spread * noise) if base else spread * noise
        out[name] = jnp.asarray(drawn.astype(out[name].dtype))
    for name, factor in factors.items():
        out[name] = (out[name] * factor).astype(out[name].dtype)
    return out
```

```python
import concourse.bass as bass
from concourse import mybir
from contextlib import ExitStack


def sandwich_kernel(nc, dense, adj_rows, adj_cols, adj_vals, wq, wk, wv_w, wv_b, qkv_w, wq_t, wk_t, out_w, out_b,
                    conv_pad, keys_t, w1_t, b1_t, w2_t, b2, rw_t, rb, out):
    fp32 = mybir.dt.float32
    bf16 = mybir.dt.bfloat16
    fp16 = mybir.dt.float16
    i32 = mybir.dt.int32
    ALU = mybir.AluOpType
    ACT = mybir.ActivationFunctionType
    AX = mybir.AxisListType

    P = 128
    B, N, D = dense.shape
    NT = N // P
    T = B * NT
    H, DH, L = 8, 64, 32
    LW = N // L
    HG = P // L
    G2 = H // HG
    PINV = 6
    KC = 33
    HALO = KC // 2
    WIN = P + 2 * HALO
    BAND_CUTS = [min(N, H * WIN - c) for c in range(0, H * WIN, N)]
    EDGES = adj_rows.shape[0]
    EC = EDGES // P
    EG = 8
    NG = EC // EG
    QK = wq.shape[1]
    NS = 3
    E, TOPK = keys_t.shape[1], 4
    F = w1_t.shape[2]
    FC = F // P
    EPS = 1e-5

    ctx = ExitStack()
    with ctx:
        def sb(name, shape, dt=fp32):
            return ctx.enter_context(nc.sbuf_tensor(name, shape, dt))

        def sem(name):
            return ctx.enter_context(nc.semaphore(name))

        x = sb("x", [P, T, D])
        xn = sb("xn", [P, T, D])
        xnT = sb("xnT", [P, T * P])
        value = sb("value", [P, T, D])
        wqkv_sb = sb("wqkv_sb", [P, 3 * H * DH])
        wqT_sb = sb("wqT_sb", [DH, H, D])
        wkT_sb = sb("wkT_sb", [DH, H, D])
        wv_sb = sb("wv_sb", [P, D])
        wvb_row = sb("wvb_row", [P, D])
        outw_sb = sb("outw_sb", [P, NT, D])
        outb_row = sb("outb_row", [P, D])
        wq3_sb = sb("wq3_sb", [P, NS, QK])
        wk_sb = sb("wk_sb", [P, QK])
        band = sb("band", [P, H, WIN])
        keysT = sb("keysT", [P, E])
        rwT = sb("rwT", [P, E])
        rb_row = sb("rb_row", [P, E])
        b1b = sb("b1b", [P, 2, FC])
        b2_sb = sb("b2_sb", [E, D])

        ident = sb("ident", [P, P])
        flip = sb("flip", [P, P])
        identw = sb("identw", [P, 3, G2, P])
        blk_j = sb("blk_j", [P, HG, L])
        blk_d = sb("blk_d", [P, HG, DH])
        ones = sb("ones", [P, P])
        eps_c = sb("eps_c", [P, 1])
        zeros = sb("zeros", [P, N], bf16)
        iota_e = sb("iota_e", [P, E])
        iota_c = sb("iota_c", [P, NT])
        iota_r = sb("iota_r", [P, N], fp16)

        stats = sb("stats", [P, T, 6])
        mv = sb("mv", [P, T, 2])
        std = sb("std", [P, T])
        rstd = sb("rstd", [P, T])
        xlT = sb("xlT", [P, B * L])
        EDGE_OC, EDGE_OR = EDGES // 2, EDGES // 2 + NT * EG * P
        shared = sb("shared", [P, EDGE_OR + EG * N])
        colb = shared[:, 0:EDGE_OC].bitcast(fp16)
        oh_c = shared[:, EDGE_OC:EDGE_OR].bitcast(bf16).rearrange("p (a c n) -> p a c n", a=2, c=NT)
        oh_r = shared[:, EDGE_OR:].bitcast(bf16).rearrange("p (a j n) -> p a j n", a=2, j=EG)
        qlT = shared[0:DH, EDGE_OR:EDGE_OR + H * B * L].rearrange("p (h n) -> p h n", h=H)
        klT = shared[0:DH, EDGE_OR + H * B * L:].rearrange("p (h n) -> p h n", h=H)
        p3 = shared[:, EDGE_OC:EDGE_OC + G2 * N].rearrange("p (g n) -> p g n", g=G2)
        p3T = shared[:, EDGE_OC + G2 * N:EDGE_OC + 2 * G2 * N].rearrange("p (g t n) -> p g t n", g=G2, t=NT)
        p1 = shared[:, EDGE_OC + 2 * G2 * N:EDGE_OC + 3 * G2 * N].rearrange("p (a j) -> p a j", j=L)
        band_up = shared[:, EDGE_OC:EDGE_OC + H * WIN].rearrange("p (h m) -> p h m", h=H)
        outT = shared[:, EDGE_OR:EDGE_OR + NT * N].rearrange("p (c n) -> p c n", c=NT)
        XLW = 2 * B * D
        xl = shared[:, 0:XLW].rearrange("p (a b d) -> p a b d", a=2, b=B)
        sg = shared[:, XLW:2 * XLW].rearrange("p (a b d) -> p a b d", a=2, b=B)
        hT = shared[:, 2 * XLW:2 * XLW + 2 * FC * N].rearrange("p (a c n) -> p a c n", a=2, c=FC)
        HW = 2 * XLW + 2 * FC * N
        w1b = shared[:, HW:HW + 2 * F].rearrange("p (a f) -> p a f", a=2)
        w2b = shared[:, HW + 2 * F:HW + 2 * F + 2 * FC * D].rearrange("p (a c d) -> p a c d", a=2, c=FC)
        GW = HW + 2 * F + 2 * FC * D
        gateT = shared[0:E, GW:GW + T * P]
        LW0 = GW + T * P
        logits, chosen, khot = [shared[:, LW0 + i * T * E:LW0 + (i + 1) * T * E].rearrange("p (t e) -> p t e", t=T)
                                for i in range(3)]
        TW0 = LW0 + 3 * T * E
        top8 = shared[:, TW0:TW0 + T * 8].rearrange("p (t k) -> p t k", t=T)
        topi = shared[:, TW0 + T * 8:TW0 + 2 * T * 8].bitcast(mybir.dt.uint32).rearrange("p (t k) -> p t k", t=T)
        a2 = sb("a2", [P, B * G2, L])
        a2m = sb("a2m", [P, B * G2])
        a2s = sb("a2s", [P, B * G2])
        r1 = sb("r1", [P, H * L])
        r3 = sb("r3", [P, H * L])
        p3m = sb("p3m", [P, G2])
        p3s = sb("p3s", [P, G2])
        p1m = sb("p1m", [P, NT * H])
        p1s = sb("p1s", [P, NT * H])
        p1T = sb("p1T", [P, G2, N])
        v_sb = sb("v_sb", [P, NT, H * DH])
        a3v = sb("a3v", [P, G2, HG * DH])
        m_bd = sb("m_bd", [P, G2, HG * DH])
        xbd = sb("xbd", [P, G2, P])
        xT = sb("xT", [P, G2, P])
        z = sb("z", [P, G2, P])
        zT = sb("zT", [P, G2, P])
        pzT = sb("pzT", [P, G2, P])
        tz = sb("tz", [P, G2, P])
        mx2 = sb("mx2", [P, 4])
        srow = sb("srow", [1, 4])
        sinv = sb("sinv", [P, 1])
        xgb = sb("xgb", [P, NT, D])
        encT = sb("encT", [P, N])
        q96 = sb("q96", [NS * QK, N])
        kf = sb("kf", [P, NT, QK])
        kres = sb("kres", [P, NT, QK])
        ksp = sb("ksp", [P, NT, NS, QK], bf16)

        idx_i = sb("idx_i", [P, 2, EC], i32)
        idx_f = sb("idx_f", [P, 2, EC])
        neg = sb("neg", [P, EC])
        vals = sb("vals", [P, EC])
        colT = sb("colT", [P, EC], fp16)
        col_dram = nc.dram_tensor("col_dram", [EDGES], fp16, kind="Internal").ap()
        kv, kvr = [wqkv_sb[:, i * N:(i + 1) * N].rearrange("p (a j q) -> p a j q", a=2, j=EG) for i in range(2)]
        kvs = sb("kvs", [P, 2, EG, NS, QK], bf16)
        prod = wqkv_sb[0:NS * QK, 2 * N:3 * N]
        arow = sb("arow", [1, N])
        asc = sb("asc", [1, 4])
        alpha = sb("alpha", [P, NT])

        x2n = sb("x2n", [P, T])
        comb = sb("comb", [P, E])
        ksq = sb("ksq", [P, E])
        lbias = sb("lbias", [P, E])
        topf = sb("topf", [P, T, TOPK])
        gate = wqkv_sb[:, 0:T * E].rearrange("p (t e) -> p t e", t=T)
        gsum = sb("gsum", [P, T])

        bank = [ctx.enter_context(nc.psum_tensor(f"bank{i}", [P, 512], fp32)) for i in range(8)]

        x_in = [sem(f"x_in{b}") for b in range(B)]
        wv_in, wqkv_in, wt_in, outw_in, qk_in, band_in = [sem(s) for s in (
            "wv_in", "wqkv_in", "wt_in", "outw_in", "qk_in", "band_in")]
        edge_in, colw_done, colb_in, ffnc_in = [sem(s) for s in ("edge_in", "colw_done", "colb_in", "ffnc_in")]
        w_in = [sem("w_in0"), sem("w_in1")]
        const_step, const_ready = sem("const_step"), sem("const_ready")
        dve_step, act_step = sem("dve_step"), sem("act_step")
        stat_ready, std_ready, xn_ready, xnT_ps, xnT_ready, val_ps, val_ready, xl_ready = [sem(s) for s in (
            "stat_ready", "std_ready", "xn_ready", "xnT_ps", "xnT_ready", "val_ps", "val_ready", "xl_ready")]
        ql_ps, ql_ready, kl_ps, kl_ready, v_ps, v_ready = [sem(s) for s in (
            "ql_ps", "ql_ready", "kl_ps", "kl_ready", "v_ps", "v_ready")]
        a2_ps, a2_shift, a2_exp, a2_ready = [sem(s) for s in ("a2_ps", "a2_shift", "a2_exp", "a2_ready")]
        r_ps, r1_ready, r3_ready, s3_ps, s3_max, p3_ready, p3T_ps, p3T_ready, a3v_ps, a3v_ready = [sem(s) for s in (
            "r_ps", "r1_ready", "r3_ready", "s3_ps", "s3_max", "p3_ready", "p3T_ps", "p3T_ready", "a3v_ps", "a3v_ready")]
        s1_ps, s1_shift, s1_exp, p1_ready, p1T_ps, p1T_ready = [sem(s) for s in (
            "s1_ps", "s1_shift", "s1_exp", "p1_ready", "p1T_ps", "p1T_ready")]
        xT_ready = sem("xT_ready")
        band_ps, band_ready = sem("band_ps"), sem("band_ready")
        xbd_ready, xT_ps, max_ready, max_ps, sinv_row, sinv_ps = [sem(s) for s in (
            "xbd_ready", "xT_ps", "max_ready", "max_ps", "sinv_row", "sinv_ps")]
        pz_ps, t_ready, pzT_ready, tz_ps, zn_ps, z_ready, zT_ready = [sem(s) for s in (
            "pz_ps", "t_ready", "pzT_ready", "tz_ps", "zn_ps", "z_ready", "zT_ready")]
        m_ps, m_ready, outT_ps, outT_ready, xg_ps, enc0_ready, enc_ready = [sem(s) for s in (
            "m_ps", "m_ready", "outT_ps", "outT_ready", "xg_ps", "enc0_ready", "enc_ready")]
        encT_ps, encT_ready, q_ps, q_ready, k_ps, ksp_ready = [sem(s) for s in (
            "encT_ps", "encT_ready", "q_ps", "q_ready", "k_ps", "ksp_ready")]
        colT_need, colT_ps, colT_ready = [sem(s) for s in ("colT_need", "colT_ps", "colT_ready")]
        ohc_ready, ohr_ready, kg_ps, kv_ready, kvh_ready, kvr_ready, kvm_ready, kvs_ready, g_done = [
            [sem(f"{s}{i}") for i in range(2)] for s in (
                "ohc_ready", "ohr_ready", "kg_ps", "kv_ready", "kvh_ready", "kvr_ready", "kvm_ready", "kvs_ready",
                "g_done")]
        g_ps, prod_ready, arow_ps, amax_ready, aexp_ready, arow_ready, alpha_ps = [sem(s) for s in (
            "g_ps", "prod_ready", "arow_ps", "amax_ready", "aexp_ready", "arow_ready", "alpha_ps")]
        xl_done, sw_ready, u_ready = [sem(s) for s in ("xl_done", "sw_ready", "u_ready")]
        stat2, std2, stat3, std3, xn2_ready, sq_done, xn2T_ps, xn2T_ready = [sem(s) for s in (
            "stat2", "std2", "stat3", "std3", "xn2_ready", "sq_done", "xn2T_ps", "xn2T_ready")]
        comb_ready, ksq_ps, logit_ps, lshift, lexp, gate_ready, gateT_ps, gateT_ready, y0_ps, y0_ready = [sem(s) for s in (
            "comb_ready", "ksq_ps", "logit_ps", "lshift", "lexp", "gate_ready", "gateT_ps", "gateT_ready", "y0_ps",
            "y0_ready")]
        up_ps = sem("up_ps")
        gelu_done = [sem(f"gelu_done{c}") for c in range(FC)]
        down_ps, y_done = [[sem(f"{s}{i}") for i in range(2)] for s in ("down_ps", "y_done")]
        stat4, std4, out_ready, out_done = [sem(s) for s in ("stat4", "std4", "out_ready", "out_done")]

        block = ctx.enter_context(nc.Block())

        def tok(t):
            return slice(t * P, (t + 1) * P)

        def over_b(ap, t):
            return ap[:, :, :].rearrange("p (b t) d -> p t b d", t=NT)[:, t, :, :]

        @block.sync
        def _(sp):
            for b in range(B):
                sp.dma_start(x[:, b * NT:(b + 1) * NT, :],
                             dense[b, :, :].rearrange("(t p) d -> p t d", p=P)).then_inc(x_in[b], 16)
                if b == 0:
                    sp.dma_start(wv_sb[:, :], wv_w).then_inc(wv_in, 16)
                    sp.dma_start(wvb_row[:, :], wv_b.rearrange("(a d) -> a d", a=1).broadcast_to([P, D]))\
                      .then_inc(wv_in, 16)
            sp.dma_start(b2_sb[:, :], b2).then_inc(ffnc_in, 16)
            sp.dma_start(keysT[:, :], keys_t).then_inc(ffnc_in, 16)
            sp.dma_start(rwT[:, :], rw_t).then_inc(ffnc_in, 16)
            sp.dma_start(rb_row[:, :], rb.rearrange("(a d) -> a d", a=1).broadcast_to([P, E])).then_inc(ffnc_in, 16)
            sp.wait_ge(colT_ready, 1)
            sp.dma_start(col_dram.rearrange("(c e) -> c e", e=P), colT[:, :]).then_inc(colw_done, 16)
            sp.wait_ge(colw_done, 16)
            sp.dma_start(colb[:, :], col_dram.rearrange("(a e) -> a e", a=1).broadcast_to([P, EDGES]))\
              .then_inc(colb_in, 16)
            STEPS = B // 2

            def load_expert(e, w):
                sp.dma_start(w1b[:, w, :], w1_t[:, e, :].rearrange("p a f -> p (a f)")).then_inc(w_in[w], 16)
                sp.dma_start(w2b[:, w, :, :], w2_t[:, e, :, :].rearrange("p a c d -> p (a c) d"))\
                  .then_inc(w_in[w], 16)
                sp.dma_start(b1b[:, w, :], b1_t[:, e, :].rearrange("p a c -> p (a c)")).then_inc(w_in[w], 16)

            sp.wait_ge(g_ps, 1)
            for w in range(2):
                load_expert(slice(w, w + 1), w)
            with sp.Fori(0, E // 2 - 1) as pair:
                for w in range(2):
                    sp.wait_ge(down_ps[1], STEPS * (2 * pair + w + 1) + 1)
                    load_expert(bass.ds(2 * pair + 2 + w, 1), w)
            for b in range(B):
                sp.wait_ge(out_ready, b + 1)
                sp.dma_start(out[b, :, :].rearrange("(t p) d -> p t d", p=P), x[:, b * NT:(b + 1) * NT, :])\
                  .then_inc(out_done, 16)
            sp.wait_ge(out_done, 16 * B)

        @block.gpsimd
        def _(pool):
            steps = [0]

            def step(ins):
                steps[0] += 1
                ins.then_inc(const_step, 1)
                pool.wait_ge(const_step, steps[0])

            step(pool.memset(ident[:, :], 0.0))
            step(pool.affine_select(out=ident[:, :], in_=ident[:, :], compare_op=ALU.not_equal, fill=1.0,
                                    base=0, pattern=[[-1, P]], channel_multiplier=1))
            step(pool.memset(flip[:, :], 0.0))
            pool.affine_select(out=flip[:, :], in_=flip[:, :], compare_op=ALU.not_equal, fill=1.0,
                               base=1 - P, pattern=[[1, P]], channel_multiplier=1)
            pool.memset(eps_c[:, :], EPS)
            pool.memset(zeros[:, :], 0.0)
            pool.iota(iota_e[:, :], pattern=[[1, E]], base=0, channel_multiplier=0,
                      allow_small_or_imprecise_dtypes=True)
            pool.memset(ones[:, :], 1.0).then_inc(const_ready, 1)
            for m, w in ((blk_j, L), (blk_d, DH)):
                step(pool.memset(m[:, :, :], 1.0))
                step(pool.affine_select(out=m[:, :, :], in_=m[:, :, :], compare_op=ALU.is_ge, fill=0.0,
                                        base=0, pattern=[[-L, HG], [0, w]], channel_multiplier=1))
                step(pool.affine_select(out=m[:, :, :], in_=m[:, :, :], compare_op=ALU.is_ge, fill=0.0,
                                        base=L - 1, pattern=[[L, HG], [0, w]], channel_multiplier=-1))
            step(pool.memset(identw[:, :, :, :], 0.0))
            for n, c in enumerate((7.0, 15.0, 13.0)):
                step(pool.affine_select(out=identw[:, n, :, :], in_=identw[:, n, :, :], compare_op=ALU.not_equal,
                                        fill=c, base=0, pattern=[[0, G2], [-1, P]], channel_multiplier=1))
            pool.iota(iota_c[:, :], pattern=[[P, NT]], base=0, channel_multiplier=1,
                      allow_small_or_imprecise_dtypes=True)
            pool.iota(iota_r[:, :], pattern=[[1, N]], base=0, channel_multiplier=0,
                      allow_small_or_imprecise_dtypes=True).then_inc(const_ready, 1)
            pool.wait_ge(enc0_ready, 1)
            for t in range(NT):
                e = over_b(xn, t)[:, 1:B, :]
                last = pool.tensor_tensor(out=e, in0=e, in1=xgb[:, t, :].unsqueeze(1).broadcast_to([P, B - 1, D]),
                                          op=ALU.add)
            last.then_inc(enc_ready, 1)

        @block.scalar
        def _(act):
            steps = [0]

            def step(ins):
                steps[0] += 1
                ins.then_inc(act_step, 1)
                act.wait_ge(act_step, steps[0])

            act.dma_start(wqkv_sb[:, :], qkv_w).then_inc(wqkv_in, 16)
            act.dma_start(wqT_sb[:, :, :], wq_t).then_inc(wt_in, 16)
            act.dma_start(wkT_sb[:, :, :], wk_t).then_inc(wt_in, 16)
            act.dma_start(idx_i[:, 0, :], adj_rows.rearrange("(p c) -> p c", p=P)).then_inc(edge_in, 16)
            act.dma_start(idx_i[:, 1, :], adj_cols.rearrange("(p c) -> p c", p=P)).then_inc(edge_in, 16)
            act.dma_start(vals[:, :], adj_vals.rearrange("(p c) -> p c", p=P)).then_inc(edge_in, 16)
            act.dma_start(outw_sb[:, :, :], out_w.rearrange("(c p) d -> p c d", p=P)).then_inc(outw_in, 16)
            act.dma_start(outb_row[:, :], out_b.rearrange("(a d) -> a d", a=1).broadcast_to([P, D]))\
               .then_inc(outw_in, 16)
            for s in range(NS):
                act.dma_start(wq3_sb[:, s, :], wq).then_inc(qk_in, 16)
            act.dma_start(wk_sb[:, :], wk).then_inc(qk_in, 16)
            act.dma_start(band_up[:, :, :], bass.AP(tensor=conv_pad.tensor, offset=0,
                                                    ap=[[1, P], [conv_pad.shape[1], H], [1, WIN]]))\
               .then_inc(band_in, 16)

            act.wait_ge(const_ready, 1)
            for b in range(B):
                act.wait_ge(stat_ready, b + 1)
                act.activation(std[:, b * NT:(b + 1) * NT], mv[:, b * NT:(b + 1) * NT, 1], ACT.Sqrt,
                               bias=eps_c[:, 0:1]).then_inc(std_ready, 1)
                act.wait_ge(xnT_ps, b + 1)
                act.activation(xnT[:, b * N:(b + 1) * N], bank[b % 2][:, :], ACT.Copy).then_inc(xnT_ready, 1)
            for c, w in enumerate(BAND_CUTS):
                act.wait_ge(band_ps, c + 1)
                act.activation(band[:, :, :].rearrange("p h m -> p (h m)")[:, c * N:c * N + w], bank[4 + c][:, 0:w],
                               ACT.Copy).then_inc(band_ready, 1)
            act.wait_ge(colT_ps, 1)
            act.activation(colT[:, :], bank[3][:, 0:P], ACT.Copy).then_inc(colT_ready, 1)
            for t in range(NT):
                act.wait_ge(v_ps, t + 1)
                act.activation(v_sb[:, t, :], bank[4 + t][:, :], ACT.Copy).then_inc(v_ready, 1)
            for c in range(4):
                act.wait_ge(ql_ps, c + 1)
                act.activation(qlT[:, 2 * c:2 * c + 2, :].rearrange("p h n -> p (h n)"), bank[c][0:DH, :], ACT.Copy,
                               scale=DH ** -0.5 / LW).then_inc(ql_ready, 1)
            act.wait_ge(r_ps, 2)
            act.activation(r3[:, :], bank[2][:, 0:H * L], ACT.Copy).then_inc(r3_ready, 1)
            act.wait_ge(a2_shift, 1)
            act.activation(a2[:, :, :], a2[:, :, :], ACT.Exp).then_inc(a2_exp, 1)
            for g in range(G2):
                act.wait_ge(s3_max, g + 1)
                act.activation(p3[:, g, :], bank[3 - g][:, :], ACT.Exp, bias=p3m[:, g:g + 1],
                               accum_out=p3s[:, g:g + 1]).then_inc(p3_ready, 1)
            act.wait_ge(s1_shift, 1)
            act.activation(p1[:, :, :], p1[:, :, :], ACT.Exp).then_inc(s1_exp, 1)
            for g in range(G2):
                act.wait_ge(p3T_ps, g + 1)
                act.activation(p3T[:, g, :, :].rearrange("p c n -> p (c n)"), bank[3 - g][:, :], ACT.Copy)\
                   .then_inc(p3T_ready, 1)
            for g in range(G2):
                act.wait_ge(p1T_ps, g + 1)
                act.activation(p1T[:, g, :], bank[1 - g][:, :], ACT.Copy).then_inc(p1T_ready, 1)
            with act.Fori(0, PINV) as i:
                act.wait_ge(pz_ps, 2 * i + 2)
                act.activation(pzT[:, :, :].rearrange("p g n -> p (g n)"), bank[3][:, 0:G2 * P], ACT.Copy)\
                   .then_inc(pzT_ready, 1)
                act.wait_ge(zn_ps, 2 * i + 2)
                act.activation(zT[:, :, :].rearrange("p g n -> p (g n)"), bank[3][:, 0:G2 * P], ACT.Copy,
                               scale=0.25).then_inc(zT_ready, 1)
            act.wait_ge(m_ps, 1)
            act.activation(m_bd[:, :, :].rearrange("p g n -> p (g n)"), bank[2][:, :], ACT.Copy).then_inc(m_ready, 1)
            for c in range(2):
                act.wait_ge(outT_ps, 2 * c + 1)
                act.activation(outT[:, 2 * c, :], bank[4 + 2 * c][:, :], ACT.Copy).then_inc(outT_ready, 1)
            act.wait_ge(encT_ps, 1)
            act.activation(encT[:, :], bank[1][:, :], ACT.Copy).then_inc(encT_ready, 1)
            act.wait_ge(q_ps, 1)
            act.activation(q96[:, :], bank[2][0:NS * QK, :], ACT.Copy, scale=QK ** -0.5).then_inc(q_ready, 1)
            with act.Fori(0, NG // 2) as pair:
                for s in range(2):
                    act.wait_ge(kv_ready[s], pair + 2)
                    act.activation(kvs[:, s, :, 0, :], kv[:, s, :, :], ACT.Copy).then_inc(kvh_ready[s], 1)
                    act.wait_ge(kvr_ready[s], pair + 1)
                    act.activation(kvs[:, s, :, 1, :], kvr[:, s, :, :], ACT.Copy).then_inc(kvm_ready[s], 1)
            act.wait_ge(amax_ready, 1)
            act.activation(arow[:, :], bank[5][0:1, :], ACT.Exp, bias=asc[0:1, 0:1],
                           accum_out=asc[0:1, 1:2]).then_inc(aexp_ready, 1)
            for t in range(NT):
                act.wait_ge(xl_done, t + 1)
                step(act.activation(sg[:, t % 2, :, :], xl[:, t % 2, :, :], ACT.Sigmoid, scale=-1.0))
                act.activation(sg[:, t % 2, :, :], sg[:, t % 2, :, :], ACT.Square).then_inc(sw_ready, 1)
            act.wait_ge(stat2, 1)
            act.activation(std[:, :], mv[:, :, 1], ACT.Sqrt, bias=eps_c[:, 0:1], scale=4.0).then_inc(std2, 1)
            act.wait_ge(stat3, 1)
            act.activation(std[:, :], mv[:, :, 1], ACT.Sqrt, bias=eps_c[:, 0:1]).then_inc(std3, 1)
            for b in range(B):
                act.wait_ge(xn2T_ps, b + 1)
                act.activation(xnT[:, b * N:(b + 1) * N], bank[b % 2][:, :], ACT.Copy).then_inc(xn2T_ready, 1)
                for t in range(b * NT, (b + 1) * NT):
                    last = act.activation(shared[:, t * D:(t + 1) * D], xn[:, t, :], ACT.Square, accum_out=x2n[:, t:t + 1])
            last.then_inc(sq_done, 1)
            act.wait_ge(lshift, 1)
            act.activation(gate[:, :, :], gate[:, :, :], ACT.Exp).then_inc(lexp, 1)
            for b in range(B):
                act.wait_ge(gateT_ps, b + 1)
                act.activation(gateT[:, b * N:(b + 1) * N], bank[4 + b % 2][0:E, :], ACT.Copy)\
                   .then_inc(gateT_ready, 1)
            for c in range(FC):
                act.sem_inc(gelu_done[c], 1)
            with act.Fori(0, E // 2) as pair:
                for w in range(2):
                    with act.Fori(0, B // 2) as q:
                        use = (2 * pair + w) * (B // 2) + q
                        for s in range(2):
                            act.wait_ge(w_in[w], 48 * (pair + 1))
                            act.wait_ge(down_ps[s], use + 1)
                            for c in range(FC):
                                act.wait_ge(up_ps, FC * (2 * use + s) + c + 1)
                                act.activation(hT[:, s, c, :], bank[c][:, :], ACT.Gelu,
                                               bias=b1b[:, w, c:c + 1]).then_inc(gelu_done[c], 1)
            act.wait_ge(stat4, 1)
            act.activation(std[:, :], mv[:, :, 1], ACT.Sqrt, bias=eps_c[:, 0:1]).then_inc(std4, 1)

        @block.vector
        def _(dve):
            steps = [0]
            v = nc.vector

            def step(ins):
                steps[0] += 1
                ins.then_inc(dve_step, 1)
                dve.wait_ge(dve_step, steps[0])

            def row_stats(src, t, last):
                for i in t:
                    ins = v.bn_stats(stats[:, i, :], src[:, i, :])
                step(ins)
                for i in t:
                    ins = v.bn_aggr(mv[:, i, :], stats[:, i, :])
                ins.then_inc(last, 1)

            def batch(b):
                return range(b * NT, (b + 1) * NT)

            dve.wait_ge(edge_in, 48)
            step(v.tensor_copy(idx_f[:, :, :], idx_i[:, :, :]))
            step(v.tensor_scalar(neg[:, :], idx_f[:, 1, :], 0.0, float(N), ALU.is_lt, ALU.mult))
            step(v.tensor_tensor(out=idx_f[:, 1, :], in0=idx_f[:, 1, :], in1=neg[:, :], op=ALU.add))
            v.tensor_scalar(idx_f[:, 1, :], idx_f[:, 1, :], 0.0, float(N - 1), ALU.max, ALU.min)\
             .then_inc(colT_need, 1)

            def normalise(b):
                dve.wait_ge(std_ready, b + 1)
                step(v.reciprocal(rstd[:, b * NT:(b + 1) * NT], std[:, b * NT:(b + 1) * NT]))
                for t in batch(b):
                    ins = v.tensor_scalar(xn[:, t, :], x[:, t, :], mv[:, t, 0:1], rstd[:, t:t + 1],
                                          ALU.subtract, ALU.mult)
                ins.then_inc(xn_ready, 1)

            def values(b):
                dve.wait_ge(xnT_ready, b + 1)
                v.tensor_reduce(out=xlT[:, b * L:(b + 1) * L],
                                in_=xnT[:, b * N:(b + 1) * N].rearrange("p (l w) -> p l w", w=LW),
                                axis=AX.X, op=ALU.add).then_inc(xl_ready, 1)
                if b == 0:
                    dve.wait_ge(wv_in, 32)
                dve.wait_ge(val_ps, b + 1)
                v.tensor_tensor(out=value[:, b * NT:(b + 1) * NT, :],
                                in0=bank[2 + b % 2][:, :].rearrange("p (t d) -> p t d", t=NT),
                                in1=wvb_row[:, :].unsqueeze(1).broadcast_to([P, NT, D]), op=ALU.add)\
                 .then_inc(val_ready, 1)

            for b in range(B):
                dve.wait_ge(x_in[b], 16)
                row_stats(x, batch(b), stat_ready)
                if b >= 1:
                    normalise(b - 1)
                if b >= 2:
                    values(b - 2)
            normalise(B - 1)
            values(B - 2)
            values(B - 1)

            dve.wait_ge(const_ready, 2)
            for c in range(4):
                dve.wait_ge(kl_ps, c + 1)
                v.tensor_scalar(klT[:, 2 * c:2 * c + 2, :].rearrange("p h n -> p (h n)"), bank[c][0:DH, :],
                                1.0 / LW, None, ALU.mult).then_inc(kl_ready, 1)
            dve.wait_ge(r_ps, 1)
            v.tensor_scalar(r1[:, :], bank[1][:, 0:H * L], DH ** -0.5, None, ALU.mult).then_inc(r1_ready, 1)

            def shift_max(ps, dst, mx, out_sem):
                step(v.tensor_reduce(out=mx, in_=ps, axis=AX.X, op=ALU.max))
                v.tensor_tensor(out=dst, in0=ps, in1=mx.unsqueeze(2).broadcast_to(list(dst.shape)),
                                op=ALU.subtract).then_inc(out_sem, 1)

            def normalise_rows(p, s, out_sem):
                step(v.tensor_reduce(out=s, in_=p, axis=AX.X, op=ALU.add))
                step(v.reciprocal(s, s))
                v.tensor_tensor(out=p, in0=p, in1=s.unsqueeze(2).broadcast_to(list(p.shape)), op=ALU.mult)\
                 .then_inc(out_sem, 1)

            dve.wait_ge(a2_ps, 1)
            shift_max(bank[0][:, :].rearrange("p (a j) -> p a j", j=L), a2[:, :, :], a2m[:, :], a2_shift)
            for g in range(G2):
                dve.wait_ge(s3_ps, g + 1)
                v.tensor_reduce(out=p3m[:, g:g + 1], in_=bank[3 - g][:, :], axis=AX.X, op=ALU.max, negate=True)\
                 .then_inc(s3_max, 1)
            dve.wait_ge(a2_exp, 1)
            normalise_rows(a2[:, :, :], a2s[:, :], a2_ready)
            dve.wait_ge(a2_ready, 1)
            step(v.tensor_tensor(out=xbd[:, :, :].rearrange("p g (h j) -> p g h j", h=HG),
                                 in0=a2[:, 0:G2, :].unsqueeze(2).broadcast_to([P, G2, HG, L]),
                                 in1=blk_j[:, :, :].unsqueeze(1).broadcast_to([P, G2, HG, L]), op=ALU.mult))
            step(v.tensor_reduce(out=a2s[:, :], in_=a2[:, :, :], axis=AX.X, op=ALU.add))
            v.tensor_reduce(out=mx2[:, 0:1], in_=a2s[:, :], axis=AX.X, op=ALU.max).then_inc(xbd_ready, 1)
            dve.wait_ge(s1_ps, 1)
            for h in range(2):
                sl = slice(h * 16, (h + 1) * 16)
                step(v.tensor_reduce(out=p1m[:, sl], in_=bank[1 - h][:, :].rearrange("p (a j) -> p a j", j=L),
                                     axis=AX.X, op=ALU.max))
                ins = v.tensor_tensor(out=p1[:, sl, :], in0=bank[1 - h][:, :].rearrange("p (a j) -> p a j", j=L),
                                      in1=p1m[:, sl].unsqueeze(2).broadcast_to([P, 16, L]), op=ALU.subtract)
            ins.then_inc(s1_shift, 1)
            dve.wait_ge(xT_ps, 1)
            v.tensor_reduce(out=mx2[:, 1:2], in_=bank[0][:, :], axis=AX.X, op=ALU.max).then_inc(max_ready, 1)
            v.tensor_copy(xT[:, :, :].rearrange("p g n -> p (g n)"), bank[7][:, 0:G2 * P]).then_inc(xT_ready, 1)
            dve.wait_ge(s1_exp, 1)
            normalise_rows(p1[:, :, :], p1s[:, :], p1_ready)
            dve.wait_ge(max_ps, 1)
            step(v.tensor_reduce(out=srow[0:1, 0:2], in_=bank[7][0:1, 0:2 * P].rearrange("p (a n) -> p a n", a=2),
                                 axis=AX.X, op=ALU.max))
            step(v.tensor_tensor(out=srow[0:1, 2:3], in0=srow[0:1, 0:1], in1=srow[0:1, 1:2], op=ALU.mult))
            v.reciprocal(srow[0:1, 3:4], srow[0:1, 2:3]).then_inc(sinv_row, 1)
            dve.wait_ge(sinv_ps, 1)
            step(v.tensor_copy(sinv[:, :], bank[7][:, 0:1]))
            v.tensor_scalar(z[:, :, :], xT[:, :, :], sinv[:, 0:1], None, ALU.mult).then_inc(z_ready, 1)
            v.tensor_scalar(zT[:, :, :], xbd[:, :, :], sinv[:, 0:1], None, ALU.mult).then_inc(zT_ready, 1)
            dve.wait_ge(a3v_ps, 1)
            step(v.reciprocal(p3s[:, :], p3s[:, :]))
            for g in range(G2):
                ins = v.scalar_tensor_tensor(out=a3v[:, g, :], in0=bank[3][:, g * 256:(g + 1) * 256],
                                             scalar=p3s[:, g:g + 1],
                                             in1=blk_d[:, :, :].rearrange("p h d -> p (h d)"),
                                             op0=ALU.mult, op1=ALU.mult)
            ins.then_inc(a3v_ready, 1)
            with dve.Fori(0, PINV) as i:
                for n in range(3):
                    if n == 0:
                        dve.wait_ge(pz_ps, 2 * i + 1)
                    else:
                        dve.wait_ge(tz_ps, 2 * i + n)
                    v.scalar_tensor_tensor(out=tz[:, :, :], in0=bank[2 + (n == 2)][:, 0:G2 * P]
                                           .rearrange("p (g n) -> p g n", g=G2), scalar=-1.0,
                                           in1=identw[:, n, :, :], op0=ALU.mult, op1=ALU.add).then_inc(t_ready, 1)
                dve.wait_ge(zn_ps, 2 * i + 1)
                v.tensor_scalar(z[:, :, :].rearrange("p g n -> p (g n)"), bank[2][:, 0:G2 * P], 0.25, None,
                                ALU.mult).then_inc(z_ready, 1)
            for c in range(2):
                dve.wait_ge(outT_ps, 2 * c + 2)
                v.tensor_copy(outT[:, 2 * c + 1, :], bank[5 + 2 * c][:, :]).then_inc(outT_ready, 1)
            dve.wait_ge(outw_in, 32)
            dve.wait_ge(xg_ps, 1)
            step(v.tensor_tensor(out=xgb[:, :, :], in0=bank[0][:, :].rearrange("p (t d) -> p t d", t=NT),
                                 in1=outb_row[:, :].unsqueeze(1).broadcast_to([P, NT, D]), op=ALU.add))
            v.tensor_tensor(out=xn[:, 0:NT, :], in0=xn[:, 0:NT, :], in1=xgb[:, :, :], op=ALU.add)\
             .then_inc(enc0_ready, 1)
            dve.wait_ge(k_ps, 1)
            step(v.tensor_copy(kf[:, :, :].rearrange("p c q -> p (c q)"), bank[3][:, 0:NT * QK]))
            step(v.tensor_copy(ksp[:, :, 0, :], kf[:, :, :]))
            step(v.tensor_tensor(out=kres[:, :, :], in0=kf[:, :, :], in1=ksp[:, :, 0, :], op=ALU.subtract))
            step(v.tensor_copy(ksp[:, :, 1, :], kres[:, :, :]))
            v.tensor_tensor(out=ksp[:, :, 2, :], in0=kres[:, :, :], in1=ksp[:, :, 1, :], op=ALU.subtract)\
             .then_inc(ksp_ready, 1)
            dve.wait_ge(colb_in, 16)

            def one_hots(pair, s):
                g = 2 * pair + s
                dve.wait_ge(kg_ps[s], pair + 1)
                for c in range(NT):
                    ins = v.tensor_scalar(oh_c[:, s, c, :], colb[:, bass.ds(g * (EG * P), EG * P)],
                                          iota_c[:, c:c + 1], None, ALU.is_equal)
                ins.then_inc(ohc_ready[s], 1)
                dve.wait_ge(g_done[s], pair + 1)
                for j in range(EG):
                    ins = v.tensor_scalar(oh_r[:, s, j, :], iota_r[:, :], idx_f[:, 0, bass.ds(g * EG + j, 1)], None,
                                          ALU.is_equal)
                ins.then_inc(ohr_ready[s], 1)

            def parts(pair, s):
                g = 2 * pair + s
                dve.wait_ge(kg_ps[s], pair + 2)
                v.tensor_tensor(out=kv[:, s, :, :],
                                in0=bank[s][:, 0:EG * QK].rearrange("p (j q) -> p j q", j=EG),
                                in1=vals[:, bass.ds(g * EG, EG)].unsqueeze(2).broadcast_to([P, EG, QK]),
                                op=ALU.mult).then_inc(kv_ready[s], 1)
                dve.wait_ge(kvh_ready[s], pair + 1)
                v.tensor_tensor(out=kvr[:, s, :, :], in0=kv[:, s, :, :], in1=kvs[:, s, :, 0, :], op=ALU.subtract)\
                 .then_inc(kvr_ready[s], 1)
                dve.wait_ge(kvm_ready[s], pair + 1)
                v.tensor_tensor(out=kvs[:, s, :, 2, :], in0=kvr[:, s, :, :], in1=kvs[:, s, :, 1, :],
                                op=ALU.subtract).then_inc(kvs_ready[s], 1)

            for s in range(2):
                dve.sem_inc(kv_ready[s], 1)
            with dve.Fori(0, NG // 2) as pair:
                one_hots(pair, 0)
                one_hots(pair, 1)
                parts(pair, 0)
                parts(pair, 1)
            dve.wait_ge(g_ps, 1)
            dve.wait_ge(q_ready, 1)
            v.tensor_tensor(out=prod[:, :], in0=bank[4][0:NS * QK, :], in1=q96[:, :], op=ALU.mult)\
             .then_inc(prod_ready, 1)
            dve.wait_ge(arow_ps, 1)
            v.tensor_reduce(out=asc[0:1, 0:1], in_=bank[5][0:1, :], axis=AX.X, op=ALU.max, negate=True)\
             .then_inc(amax_ready, 1)
            dve.wait_ge(aexp_ready, 1)
            step(v.reciprocal(asc[0:1, 2:3], asc[0:1, 1:2]))
            v.tensor_scalar(arow[:, :], arow[:, :], asc[0:1, 2:3], None, ALU.mult).then_inc(arow_ready, 1)
            dve.wait_ge(alpha_ps, 1)
            step(v.tensor_copy(alpha[:, :], bank[6][:, 0:NT]))
            dve.wait_ge(enc_ready, 1)

            def gated(t):
                dve.wait_ge(sw_ready, t + 1)
                step(v.tensor_tensor(out=xl[:, t % 2, :, :], in0=xl[:, t % 2, :, :], in1=over_b(xn, t),
                                     op=ALU.subtract))
                step(v.tensor_tensor(out=xl[:, t % 2, :, :], in0=xl[:, t % 2, :, :], in1=sg[:, t % 2, :, :],
                                     op=ALU.mult))
                step(v.tensor_tensor(out=over_b(xn, t), in0=over_b(xn, t), in1=xl[:, t % 2, :, :], op=ALU.add))

            for t in range(NT):
                v.tensor_scalar(xl[:, t % 2, :, :], over_b(value, t), alpha[:, t:t + 1], None, ALU.mult)\
                 .then_inc(xl_done, 1)
                if t >= 1:
                    gated(t - 1)
            gated(NT - 1)
            row_stats(xn, range(T), stat2)
            dve.wait_ge(std2, 1)
            step(v.reciprocal(rstd[:, :], std[:, :]))
            step(v.tensor_scalar(rstd[:, :], rstd[:, :], 2.0, None, ALU.mult))
            for t in range(T):
                ins = v.tensor_scalar(xn[:, t, :], xn[:, t, :], mv[:, t, 0:1], rstd[:, t:t + 1],
                                      ALU.subtract, ALU.mult)
            step(ins)
            step(v.tensor_tensor(out=x[:, :, :], in0=x[:, :, :], in1=xn[:, :, :], op=ALU.add))
            row_stats(x, range(T), stat3)
            dve.wait_ge(std3, 1)
            step(v.reciprocal(rstd[:, :], std[:, :]))
            for b in range(B):
                for t in batch(b):
                    ins = v.tensor_scalar(xn[:, t, :], x[:, t, :], mv[:, t, 0:1], rstd[:, t:t + 1],
                                          ALU.subtract, ALU.mult)
                ins.then_inc(xn2_ready, 1)
            dve.wait_ge(ffnc_in, 64)
            v.tensor_tensor(out=ksq[:, :], in0=keysT[:, :], in1=keysT[:, :], op=ALU.mult)
            v.scalar_tensor_tensor(out=comb[:, :], in0=keysT[:, :], scalar=2.0, in1=rwT[:, :],
                                   op0=ALU.mult, op1=ALU.add).then_inc(comb_ready, 1)
            dve.wait_ge(ksq_ps, 1)
            step(v.tensor_tensor(out=lbias[:, :], in0=rb_row[:, :], in1=bank[5][:, 0:E], op=ALU.subtract))
            dve.wait_ge(logit_ps, 1)
            step(v.tensor_tensor(out=logits[:, :, :], in0=bank[6][:, :].rearrange("p (t e) -> p t e", t=T),
                                 in1=lbias[:, :].unsqueeze(1).broadcast_to([P, T, E]), op=ALU.add))
            dve.wait_ge(sq_done, 1)
            step(v.tensor_tensor(out=logits[:, :, :], in0=logits[:, :, :],
                                 in1=x2n[:, :].unsqueeze(2).broadcast_to([P, T, E]), op=ALU.subtract))
            for t in range(T):
                ins = v.max(out=top8[:, t, :], in_=logits[:, t, :])
            step(ins)
            v.tensor_tensor(out=gate[:, :, :], in0=logits[:, :, :],
                            in1=top8[:, :, 0:1].broadcast_to([P, T, E]), op=ALU.subtract).then_inc(lshift, 1)
            for t in range(T):
                ins = v.max_index(out=topi[:, t, :], in_max=top8[:, t, :], in_values=logits[:, t, :])
            step(ins)
            step(v.tensor_copy(topf[:, :, :], topi[:, :, 0:TOPK]))
            for k in range(TOPK):
                hot = chosen if k == 0 else khot
                step(v.tensor_tensor(out=hot[:, :, :], in0=iota_e[:, :].unsqueeze(1).broadcast_to([P, T, E]),
                                     in1=topf[:, :, k:k + 1].broadcast_to([P, T, E]), op=ALU.is_equal))
                if k > 0:
                    step(v.tensor_tensor(out=chosen[:, :, :], in0=chosen[:, :, :], in1=khot[:, :, :], op=ALU.add))
            dve.wait_ge(lexp, 1)
            step(v.tensor_tensor(out=gate[:, :, :], in0=gate[:, :, :], in1=chosen[:, :, :], op=ALU.mult))
            normalise_rows(gate[:, :, :], gsum[:, :], gate_ready)
            for b in range(B):
                dve.wait_ge(y0_ps, b + 1)
                v.tensor_copy(value[:, b * NT:(b + 1) * NT, :].rearrange("p t d -> p (t d)"), bank[6 + b % 2][:, :])\
                 .then_inc(y0_ready, 1)
            for s in range(2):
                dve.sem_inc(y_done[s], 1)
            with dve.Fori(0, E) as e:
                with dve.Fori(0, B // 2) as q:
                    for s in range(2):
                        dve.wait_ge(down_ps[s], e * (B // 2) + q + 2)
                        for t in range(NT):
                            tile = (2 * q + s) * NT + t
                            a = value[:, bass.ds(tile, 1), :].rearrange("p a d -> p (a d)")
                            ins = v.scalar_tensor_tensor(out=a, in0=bank[4 + s][:, t * D:(t + 1) * D],
                                                         scalar=gate[:, bass.ds(tile, 1), bass.ds(e, 1)]
                                                         .rearrange("p a b -> p (a b)"),
                                                         in1=a, op0=ALU.mult, op1=ALU.add)
                        ins.then_inc(y_done[s], 1)
            for s in range(2):
                dve.wait_ge(y_done[s], E * B // 2 + 1)
            row_stats(value, range(T), stat4)
            dve.wait_ge(std4, 1)
            step(v.reciprocal(rstd[:, :], std[:, :]))
            for b in range(B):
                for t in batch(b):
                    ins = v.tensor_scalar(value[:, t, :], value[:, t, :], mv[:, t, 0:1], rstd[:, t:t + 1],
                                          ALU.subtract, ALU.mult)
                step(ins)
                sl = slice(b * NT, (b + 1) * NT)
                v.tensor_tensor(out=x[:, sl, :], in0=x[:, sl, :], in1=value[:, sl, :], op=ALU.add)\
                 .then_inc(out_ready, 1)

        @block.tensor
        def _(pe):
            mm = nc.tensor.matmul

            def transposes(dst, src, n, width=P):
                for t in range(n):
                    ins = nc.tensor.transpose(dst(t), src(t), ident[:, :])
                return ins

            pe.wait_ge(const_ready, 1)
            for b in range(B):
                pe.wait_ge(xn_ready, b + 1)
                if b >= 2:
                    pe.wait_ge(xnT_ready, b - 1)
                transposes(lambda t: bank[b % 2][:, tok(t)], lambda t: xn[:, b * NT + t, :], NT).then_inc(xnT_ps, 1)
                if b == 0:
                    pe.wait_ge(wv_in, 32)
                pe.wait_ge(xnT_ready, b + 1)
                if b >= 2:
                    pe.wait_ge(val_ready, b - 1)
                for t in range(NT):
                    ins = mm(bank[2 + b % 2][:, tok(t)], xnT[:, tok(b * NT + t)], wv_sb[:, :], start=True, stop=True)
                ins.then_inc(val_ps, 1)
            pe.wait_ge(val_ready, B)
            pe.wait_ge(colT_need, 1)
            nc.tensor.transpose(bank[3][:, 0:P], idx_f[:, 1, :], ident[:, :]).then_inc(colT_ps, 1)
            pe.wait_ge(band_in, 16)
            for c, w in enumerate(BAND_CUTS):
                mm(bank[4 + c][:, 0:w], flip[:, :], band_up[:, :, :].rearrange("p h m -> p (h m)")[:, c * N:c * N + w],
                   start=True, stop=True).then_inc(band_ps, 1)
            pe.wait_ge(wqkv_in, 16)
            pe.wait_ge(band_ready, len(BAND_CUTS))
            for t in range(NT):
                mm(bank[4 + t][:, :], xnT[:, tok(t)], wqkv_sb[:, 2 * H * DH:3 * H * DH], start=True, stop=True)\
                    .then_inc(v_ps, 1)
            pe.wait_ge(xl_ready, B)
            for c in range(4):
                if c == 3:
                    pe.wait_ge(colT_ready, 1)
                for h in (2 * c, 2 * c + 1):
                    ins = mm(bank[c][0:DH, (h % 2) * 256:(h % 2) * 256 + B * L], wqkv_sb[:, h * DH:(h + 1) * DH],
                             xlT[:, :], start=True, stop=True)
                ins.then_inc(ql_ps, 1)
            for c in range(4):
                pe.wait_ge(ql_ready, c + 1)
                for h in (2 * c, 2 * c + 1):
                    ins = mm(bank[c][0:DH, (h % 2) * 256:(h % 2) * 256 + B * L],
                             wqkv_sb[:, (H + h) * DH:(H + h + 1) * DH], xlT[:, :], start=True, stop=True)
                ins.then_inc(kl_ps, 1)
            pe.wait_ge(wt_in, 32)
            pe.wait_ge(kl_ready, 4)
            for h in range(H):
                ins = mm(bank[1][:, h * L:(h + 1) * L], wqT_sb[:, h, :], klT[:, h, 0:L], start=True, stop=True)
            ins.then_inc(r_ps, 1)
            for h in range(H):
                ins = mm(bank[2][:, h * L:(h + 1) * L], wkT_sb[:, h, :], qlT[:, h, 0:L], start=True, stop=True)
            ins.then_inc(r_ps, 1)
            for b in range(B):
                for h in range(H):
                    col = (b * G2 + h // HG) * L
                    ins = mm(bank[0][(h % HG) * L:(h % HG + 1) * L, col:col + L], qlT[:, h, b * L:(b + 1) * L],
                             klT[:, h, b * L:(b + 1) * L], start=True, stop=True)
            ins.then_inc(a2_ps, 1)
            pe.wait_ge(r3_ready, 1)
            for g in range(G2):
                mm(bank[3 - g][:, :], r3[:, g * P:(g + 1) * P], xnT[:, 0:N], start=True, stop=True)\
                    .then_inc(s3_ps, 1)
            pe.wait_ge(r1_ready, 1)
            pe.wait_ge(a2_shift, 1)
            for t in range(NT):
                ins = mm(bank[1 - t // 2][:, (t % 2) * 256:(t % 2) * 256 + H * L], xnT[:, tok(t)], r1[:, :],
                         start=True, stop=True)
            ins.then_inc(s1_ps, 1)
            pe.wait_ge(v_ready, NT)

            def conv(c):
                for h in (2 * c, 2 * c + 1):
                    lo = (h % 2) * DH
                    for o in range(NT):
                        ins = mm(bank[4 + c][lo:lo + DH, tok(o)], v_sb[:, o, h * DH:(h + 1) * DH],
                                 band[:, h, HALO:HALO + P], start=(o == 0), stop=False, skip_group_check=True)
                    for o in range(NT):
                        if o > 0:
                            ins = mm(bank[4 + c][lo:lo + DH, o * P:o * P + HALO], v_sb[:, o - 1, h * DH:(h + 1) * DH],
                                     band[:, h, HALO + P:WIN], start=False, stop=False, skip_group_check=True)
                        if o < NT - 1:
                            ins = mm(bank[4 + c][lo:lo + DH, (o + 1) * P - HALO:(o + 1) * P],
                                     v_sb[:, o + 1, h * DH:(h + 1) * DH],
                                     band[:, h, 0:HALO], start=False, stop=False, skip_group_check=True)

            for c in range(3):
                conv(c)
            pe.wait_ge(xbd_ready, 1)
            pe.wait_ge(const_ready, 2)
            pe.wait_ge(s1_shift, 1)
            mm(bank[0][:, :], blk_j[:, :, :].rearrange("p h j -> p (h j)"), a2[:, :, :].rearrange("p a j -> p (a j)"), start=True, stop=True)
            transposes(lambda g: bank[7][:, tok(g)], lambda g: xbd[:, g, :], G2).then_inc(xT_ps, 1)
            for g in range(G2):
                pe.wait_ge(p3_ready, g + 1)
                transposes(lambda t: bank[3 - g][:, tok(t)], lambda t: p3[:, g, tok(t)], NT).then_inc(p3T_ps, 1)
            pe.wait_ge(max_ready, 1)
            pe.wait_ge(xT_ready, 1)
            mm(bank[7][0:1, 0:P], mx2[:, 0:1], ident[:, :], start=True, stop=True)
            mm(bank[7][0:1, P:2 * P], mx2[:, 1:2], ident[:, :], start=True, stop=True).then_inc(max_ps, 1)
            pe.wait_ge(p1_ready, 1)
            for g in range(G2):
                transposes(lambda t: bank[1 - g][:, tok(t)],
                           lambda t: p1[:, t * H + g * HG:t * H + (g + 1) * HG, :].rearrange("p h j -> p (h j)"), NT)\
                    .then_inc(p1T_ps, 1)
            pe.wait_ge(sinv_row, 1)
            mm(bank[7][:, 0:1], ones[0:1, :], srow[0:1, 3:4], start=True, stop=True).then_inc(sinv_ps, 1)
            pe.wait_ge(p3T_ready, 2)
            for g in range(G2):
                for t in range(NT):
                    ins = mm(bank[3][:, g * 256:(g + 1) * 256], p3T[:, g, t, :],
                             v_sb[:, t, g * 256:(g + 1) * 256], start=(t == 0), stop=(t == NT - 1))
            ins.then_inc(a3v_ps, 1)
            pe.wait_ge(z_ready, 1)
            conv(3)
            pe.wait_ge(a3v_ready, 1)
            with pe.Fori(0, PINV) as i:
                pe.wait_ge(z_ready, i + 1)
                pe.wait_ge(zT_ready, i + 1)
                for g in range(G2):
                    ins = mm(bank[2][:, tok(g)], xT[:, g, :], z[:, g, :], start=True, stop=True)
                ins.then_inc(pz_ps, 1)
                for g in range(G2):
                    ins = mm(bank[3][:, tok(g)], z[:, g, :], xT[:, g, :], start=True, stop=True)
                ins.then_inc(pz_ps, 1)
                pe.wait_ge(pzT_ready, i + 1)
                for n in range(2):
                    pe.wait_ge(t_ready, 3 * i + n + 1)
                    for g in range(G2):
                        ins = mm(bank[2 + n][:, tok(g)], pzT[:, g, :], tz[:, g, :], start=True, stop=True)
                    ins.then_inc(tz_ps, 1)
                pe.wait_ge(t_ready, 3 * i + 3)
                for g in range(G2):
                    ins = mm(bank[2][:, tok(g)], zT[:, g, :], tz[:, g, :], start=True, stop=True)
                ins.then_inc(zn_ps, 1)
                for g in range(G2):
                    ins = mm(bank[3][:, tok(g)], tz[:, g, :], zT[:, g, :], start=True, stop=True)
                ins.then_inc(zn_ps, 1)
            pe.wait_ge(zT_ready, PINV + 1)
            pe.wait_ge(z_ready, PINV + 1)
            for g in range(G2):
                ins = mm(bank[2][:, g * 256:(g + 1) * 256], zT[:, g, :], a3v[:, g, :], start=True, stop=True)
            ins.then_inc(m_ps, 1)
            pe.wait_ge(p1T_ready, 2)
            pe.wait_ge(m_ready, 1)
            for c in range(4):
                mm(bank[4 + c][:, :], m_bd[:, c // 2, (c % 2) * P:(c % 2 + 1) * P], p1T[:, c // 2, :],
                   start=False, stop=True, skip_group_check=True).then_inc(outT_ps, 1)
            pe.wait_ge(outw_in, 32)
            pe.wait_ge(outT_ready, 4)
            for t in range(NT):
                for c in range(4):
                    ins = mm(bank[0][:, tok(t)], outT[:, c, tok(t)], outw_sb[:, c, :], start=(c == 0), stop=(c == 3))
            ins.then_inc(xg_ps, 1)
            pe.wait_ge(enc0_ready, 1)
            transposes(lambda t: bank[1][:, tok(t)], lambda t: xn[:, t, :], NT).then_inc(encT_ps, 1)
            pe.wait_ge(qk_in, 64)
            pe.wait_ge(encT_ready, 1)
            for t in range(NT):
                ins = mm(bank[3][:, t * QK:(t + 1) * QK], encT[:, tok(t)], wk_sb[:, :], start=True, stop=True)
            ins.then_inc(k_ps, 1)
            mm(bank[2][0:NS * QK, :], wq3_sb[:, :, :].rearrange("p s q -> p (s q)"), encT[:, :], start=True,
               stop=True).then_inc(q_ps, 1)
            for s in range(2):
                pe.sem_inc(kg_ps[s], 1)
                pe.sem_inc(g_done[s], 1)
            pe.wait_ge(ksp_ready, 1)
            mm(bank[4][0:NS * QK, :], zeros[:, 0:NS * QK], zeros[:, :], start=True, stop=False, skip_group_check=True)

            def gather(pair, s):
                pe.wait_ge(ohc_ready[s], pair + 1)
                pe.wait_ge(kv_ready[s], pair + 1)
                for j in range(EG):
                    for c in range(NT):
                        for n in range(NS):
                            ins = mm(bank[s][:, j * QK:(j + 1) * QK], oh_c[:, s, c, j * P:(j + 1) * P],
                                     ksp[:, c, n, :], start=(c == 0 and n == 0), stop=(c == NT - 1 and n == NS - 1))
                ins.then_inc(kg_ps[s], 1)

            def segment(pair, s):
                pe.wait_ge(ohr_ready[s], pair + 1)
                pe.wait_ge(kvs_ready[s], pair + 1)
                for j in range(EG):
                    ins = mm(bank[4][0:NS * QK, :], kvs[:, s, j, :, :].rearrange("p n q -> p (n q)"),
                             oh_r[:, s, j, :], start=False, stop=False, skip_group_check=True)
                ins.then_inc(g_done[s], 1)

            with pe.Fori(0, NG // 2) as pair:
                gather(pair, 0)
                gather(pair, 1)
                segment(pair, 0)
                segment(pair, 1)
            mm(bank[4][0:NS * QK, :], zeros[:, 0:NS * QK], zeros[:, :], start=False, stop=True,
               skip_group_check=True).then_inc(g_ps, 1)
            pe.wait_ge(prod_ready, 1)
            mm(bank[5][0:1, :], ones[0:NS * QK, 0:1], prod[:, :], start=True, stop=True).then_inc(arow_ps, 1)
            pe.wait_ge(arow_ready, 1)
            for t in range(NT):
                ins = mm(bank[6][:, t:t + 1], arow[0:1, tok(t)], ones[0:1, 0:1], start=True, stop=True)
            ins.then_inc(alpha_ps, 1)

            for b in range(B):
                pe.wait_ge(xn2_ready, b + 1)
                if b >= 2:
                    pe.wait_ge(xn2T_ready, b - 1)
                transposes(lambda t: bank[b % 2][:, tok(t)], lambda t: xn[:, b * NT + t, :], NT).then_inc(xn2T_ps, 1)
            pe.wait_ge(comb_ready, 1)
            mm(bank[5][:, 0:E], ones[:, :], ksq[:, :], start=True, stop=True).then_inc(ksq_ps, 1)
            pe.wait_ge(xn2T_ready, B)
            for t in range(T):
                ins = mm(bank[6][:, t * E:(t + 1) * E], xnT[:, tok(t)], comb[:, :], start=True, stop=True)
            ins.then_inc(logit_ps, 1)
            pe.wait_ge(gate_ready, 1)
            for b in range(B):
                if b >= 2:
                    pe.wait_ge(gateT_ready, b - 1)
                transposes(lambda t: bank[4 + b % 2][0:E, tok(t)], lambda t: gate[:, b * NT + t, :], NT)\
                    .then_inc(gateT_ps, 1)
            pe.wait_ge(ffnc_in, 64)
            for b in range(B):
                pe.wait_ge(gateT_ready, b + 1)
                if b >= 2:
                    pe.wait_ge(y0_ready, b - 1)
                for t in range(b * NT, (b + 1) * NT):
                    ins = mm(bank[6 + b % 2][:, tok(t % NT)], gateT[:, tok(t)], b2_sb[:, :], start=True, stop=True)
                ins.then_inc(y0_ps, 1)
            for s in range(2):
                pe.sem_inc(down_ps[s], 1)
            with pe.Fori(0, E // 2) as pair:
                for w in range(2):
                    with pe.Fori(0, B // 2) as q:
                        pe.wait_ge(w_in[w], 48 * (pair + 1))
                        use = (2 * pair + w) * (B // 2) + q
                        for s in range(2):
                            for c in range(FC):
                                pe.wait_ge(gelu_done[c], 2 * use + s + 1)
                                mm(bank[c][:, :], w1b[:, w, c * P:(c + 1) * P], xnT[:, bass.ds((2 * q + s) * N, N)],
                                   start=True, stop=True).then_inc(up_ps, 1)
                        for s in range(2):
                            pe.wait_ge(y_done[s], use + 1)
                            for c in range(FC):
                                pe.wait_ge(gelu_done[c], 2 * use + s + 2)
                            for t in range(NT):
                                for c in range(FC):
                                    ins = mm(bank[4 + s][:, tok(t)], hT[:, s, c, tok(t)], w2b[:, w, c, :],
                                             start=(c == 0), stop=(c == FC - 1))
                            ins.then_inc(down_ps[s], 1)


def kernel(**inputs):
    import numpy as np
    import concourse.bacc as bacc
    from concourse.bass_utils import run_bass_kernel_spmd

    a = {k.split("_", 2)[2]: np.asarray(v) for k, v in inputs.items()}
    E, F, D = a["w1"].shape
    P, DH = 128, 64
    H = a["qkv_w"].shape[1] // (3 * DH)
    taps = a["conv_w"].reshape(H, -1)
    K = taps.shape[1]
    conv_pad = np.zeros((H, 2 * P - 2 + K), taps.dtype)
    conv_pad[:, P - 1:P - 1 + K] = taps[:, ::-1]

    def heads(w):
        return w.reshape(D, H, DH).transpose(2, 1, 0)

    arrays = dict(
        dense=a["dense"], adj_rows=a["adj_rows"], adj_cols=a["adj_cols"], adj_vals=a["adj_vals"], wq=a["wq"],
        wk=a["wk"], wv_w=a["wv_w"], wv_b=a["wv_b"], qkv_w=a["qkv_w"], wq_t=heads(a["qkv_w"][:, :H * DH]),
        wk_t=heads(a["qkv_w"][:, H * DH:2 * H * DH]), out_w=a["out_w"], out_b=a["out_b"], conv_pad=conv_pad,
        keys_t=a["keys"].T, w1_t=a["w1"].transpose(2, 0, 1), b1_t=a["b1"].reshape(E, F // P, P).transpose(2, 0, 1),
        w2_t=a["w2"].reshape(E, D, F // P, P).transpose(3, 0, 2, 1), b2=a["b2"], rw_t=a["rw"].T, rb=a["rb"])
    arrays = {k: np.ascontiguousarray(v) for k, v in arrays.items()}
    nc = bacc.Bacc("TRN2", target_bir_lowering=False, num_devices=1)
    args = {k: nc.dram_tensor(f"in_{k}", v.shape, mybir.dt.from_np(v.dtype), kind="ExternalInput").ap()
            for k, v in arrays.items()}
    args["out"] = nc.dram_tensor("out_x", a["dense"].shape, mybir.dt.float32, kind="ExternalOutput").ap()
    sandwich_kernel(nc, **args)
    r = run_bass_kernel_spmd(nc, [{f"in_{k}": v for k, v in arrays.items()}], core_ids=[0])
    return r.results[0]["out_x"]
```

```python
import concourse.bass as bass
from concourse import mybir
from contextlib import ExitStack


def sandwich_kernel(nc, dense, adj_rows, adj_cols, adj_vals, wq, wk, wv_w, wv_b, qkv_w, wq_t, wk_t, out_w, out_b,
                    conv_pad, keys_t, w1_t, b1, w2_t, b2, rw_t, rb, out):
    fp32 = mybir.dt.float32
    bf16 = mybir.dt.bfloat16
    fp16 = mybir.dt.float16
    i32 = mybir.dt.int32
    ALU = mybir.AluOpType
    ACT = mybir.ActivationFunctionType
    AX = mybir.AxisListType

    P = 128
    B, N, D = dense.shape
    NT = N // P
    T = B * NT
    H, DH, L = 8, 64, 32
    LW = N // L
    HG = P // L
    G2 = H // HG
    PINV = 6
    KC = 33
    HALO = KC // 2
    WIN = P + 2 * HALO
    BAND_CUTS = [min(N, H * WIN - c) for c in range(0, H * WIN, N)]
    EDGES = adj_rows.shape[0]
    EC = EDGES // P
    EG = 8
    NG = EC // EG
    QK = wq.shape[1]
    NS = 3
    E, TOPK = keys_t.shape[1], 4
    F = w1_t.shape[2]
    FC = F // P
    EPS = 1e-5
    NBLK = -(-(T * P * TOPK + E * (P - 1)) // P // 4) * 4
    BG = 4
    DUMP = T * P * TOPK

    ctx = ExitStack()
    with ctx:
        def sb(name, shape, dt=fp32):
            return ctx.enter_context(nc.sbuf_tensor(name, shape, dt))

        def sem(name):
            return ctx.enter_context(nc.semaphore(name))

        x = sb("x", [P, T, D])
        xn = sb("xn", [P, T, D])
        xnT = sb("xnT", [P, T * P])
        value = sb("value", [P, T, D])
        early = sb("early", [P, 3 * H * DH + 2 * H * D + NT * D + H * WIN + NT * H * DH + G2 * N])
        b1_row = early[:, 0:E * F].rearrange("p (e f) -> p e f", e=E)
        cursor = [0]

        def of_early(parts, width):
            cursor[0] += width
            return early[0:parts, cursor[0] - width:cursor[0]]

        wqkv_sb = of_early(P, 3 * H * DH)
        wqT_sb = of_early(DH, H * D).rearrange("p (h d) -> p h d", h=H)
        wkT_sb = of_early(DH, H * D).rearrange("p (h d) -> p h d", h=H)
        outw_sb = of_early(P, NT * D).rearrange("p (c d) -> p c d", c=NT)
        band = of_early(P, H * WIN).rearrange("p (h m) -> p h m", h=H)
        v_sb = of_early(P, NT * H * DH).rearrange("p (t n) -> p t n", t=NT)
        p1T = of_early(P, G2 * N).rearrange("p (g n) -> p g n", g=G2)
        wv_sb = sb("wv_sb", [P, D])
        wvb_row = sb("wvb_row", [P, D])
        outb_row = sb("outb_row", [P, D])
        wq3_sb = sb("wq3_sb", [P, NS, QK])
        wk_sb = sb("wk_sb", [P, QK])
        keysT = sb("keysT", [P, E])
        rwT = sb("rwT", [P, E])
        rb_row = sb("rb_row", [P, E])
        b2_sb = sb("b2_sb", [P, E * D // P])
        b2_res = sb("b2_res", [P, E * D // P])
        b2_cut = sb("b2_cut", [P, NS, E * D // P], bf16)
        b2_parts = sb("b2_parts", [NS, E, D], bf16)
        b2_dram = nc.dram_tensor("b2_dram", [NS, E * D], bf16, kind="Internal").ap()

        ident = sb("ident", [P, P])
        flip = sb("flip", [P, P])
        identw = sb("identw", [P, 3, G2, P])
        blk_j = sb("blk_j", [P, HG, L])
        blk_d = sb("blk_d", [P, HG, DH])
        ones = sb("ones", [P, P])
        eps_c = sb("eps_c", [P, 1])
        zeros = sb("zeros", [P, N], bf16)
        iota_e = sb("iota_e", [P, E])
        iota_c = sb("iota_c", [P, NT])
        iota_r = sb("iota_r", [P, N], fp16)

        stats = sb("stats", [P, T, 6])
        mv = sb("mv", [P, T, 2])
        std = sb("std", [P, T])
        rstd = sb("rstd", [P, T])
        xlT = sb("xlT", [P, B * L])
        EDGE_OC, EDGE_OR = EDGES // 2, EDGES // 2 + NT * EG * P
        shared = sb("shared", [P, EDGE_OR + EG * N])
        colb = shared[:, 0:EDGE_OC].bitcast(fp16)
        oh_c = shared[:, EDGE_OC:EDGE_OR].bitcast(bf16).rearrange("p (a c n) -> p a c n", a=2, c=NT)
        oh_r = shared[:, EDGE_OR:].bitcast(bf16).rearrange("p (a j n) -> p a j n", a=2, j=EG)
        qlT = shared[0:DH, EDGE_OR:EDGE_OR + H * B * L].rearrange("p (h n) -> p h n", h=H)
        klT = shared[0:DH, EDGE_OR + H * B * L:].rearrange("p (h n) -> p h n", h=H)
        p3 = shared[:, EDGE_OC:EDGE_OC + G2 * N].rearrange("p (g n) -> p g n", g=G2)
        p3T = shared[:, EDGE_OC + G2 * N:EDGE_OC + 2 * G2 * N].rearrange("p (g t n) -> p g t n", g=G2, t=NT)
        p1 = shared[:, EDGE_OC + 2 * G2 * N:EDGE_OC + 3 * G2 * N].rearrange("p (a j) -> p a j", j=L)
        band_up = shared[:, EDGE_OC:EDGE_OC + H * WIN].rearrange("p (h m) -> p h m", h=H)
        outT = shared[:, EDGE_OR:EDGE_OR + NT * N].rearrange("p (c n) -> p c n", c=NT)
        w1_sb = shared[:, 0:E * F].rearrange("p (e f) -> p e f", e=E)
        w2_sb = shared[:, E * F:E * (F + FC * D)].rearrange("p (e c d) -> p e c d", e=E, c=FC)
        xl = xnT[:, 0:2 * B * D].rearrange("p (a b d) -> p a b d", a=2, b=B)
        sg = xnT[:, 2 * B * D:4 * B * D].rearrange("p (a b d) -> p a b d", a=2, b=B)
        TE = T * E
        logits, chosen, pos_e, tmp_e, k0, k1, k2 = [
            xnT[:, i * TE:(i + 1) * TE].rearrange("p (t e) -> p t e", t=T) for i in range(7)]
        top8 = xnT[:, 7 * TE:7 * TE + T * 8].rearrange("p (t k) -> p t k", t=T)
        topi = xnT[:, 7 * TE + T * 8:8 * TE].bitcast(mybir.dt.uint32).rearrange("p (t k) -> p t k", t=T)
        att = sb("att", [P, 7, N])
        a2 = att[:, 0, :].rearrange("p (a j) -> p a j", j=L)
        a2m = sb("a2m", [P, B * G2])
        a2s = sb("a2s", [P, B * G2])
        r1, r3 = att[:, 1, 0:H * L], att[:, 1, H * L:2 * H * L]
        p3m = sb("p3m", [P, G2])
        p3s = sb("p3s", [P, G2])
        p1m = sb("p1m", [P, NT * H])
        p1s = sb("p1s", [P, NT * H])
        a3v = att[:, 2, :].rearrange("p (g n) -> p g n", g=G2)
        m_bd = att[:, 3, :].rearrange("p (g n) -> p g n", g=G2)
        pinv = sb("pinv", [P, 6, G2 * P])
        xbd, xT, z, zT, pzT, tz = [pinv[:, i, :].rearrange("p (g n) -> p g n", g=G2) for i in range(6)]
        mx2 = sb("mx2", [P, 4])
        srow = sb("srow", [1, 4])
        sinv = sb("sinv", [P, 1])
        xgb = att[:, 4, :].rearrange("p (t d) -> p t d", t=NT)
        encT = att[:, 5, :]
        q96 = att[0:NS * QK, 6, :]
        kf = sb("kf", [P, NT, QK])
        kres = sb("kres", [P, NT, QK])
        ksp = sb("ksp", [P, NT, NS, QK], bf16)

        idx_i = sb("idx_i", [P, 2, EC], i32)
        idx_f = sb("idx_f", [P, 2, EC])
        neg = sb("neg", [P, EC])
        vals = sb("vals", [P, EC])
        colT = sb("colT", [P, EC], fp16)
        col_dram = nc.dram_tensor("col_dram", [EDGES], fp16, kind="Internal").ap()
        kv, kvr = [xnT[:, i * N:(i + 1) * N].rearrange("p (a j q) -> p a j q", a=2, j=EG) for i in range(2)]
        kvs = xnT[:, 2 * N:2 * N + EG * NS * QK].bitcast(bf16).rearrange("p (a j n q) -> p a j n q", a=2, j=EG, n=NS)
        prod = xnT[0:NS * QK, 4 * N:5 * N]
        arow = xnT[0:1, 5 * N:6 * N]
        asc = sb("asc", [1, 4])
        alpha = sb("alpha", [P, NT])

        attf = att[:, :, :].rearrange("p a n -> p (a n)")
        taken = [0]

        def of_att(width):
            taken[0] += width
            return attf[:, taken[0] - width:taken[0]]

        hb = of_att(2 * F).rearrange("p (a f) -> p a f", a=2)
        k3 = of_att(TE).rearrange("p (t e) -> p t e", t=T)
        chosen_b = of_att(TE // 2).bitcast(bf16).rearrange("p (t e) -> p t e", t=T)
        pos, lane, blk, pos_i, lane_i = [of_att(T * TOPK).rearrange("p (t k) -> p t k", t=T) for _ in range(5)]
        pos_i, lane_i = pos_i.bitcast(i32), lane_i.bitcast(i32)
        src_tok, used = of_att(NBLK), of_att(NBLK)
        part_i, part_f = [of_att(2 * NBLK).rearrange("p (a n) -> p a n", a=2) for _ in range(2)]
        part_i = part_i.bitcast(i32)
        x2n = sb("x2n", [P, T])
        comb = sb("comb", [P, E])
        ksq = sb("ksq", [P, E])
        lbias = sb("lbias", [P, E])
        upper = sb("upper", [P, P], bf16)
        ones_b = sb("ones_b", [P, P], bf16)
        tot, cum = [pinv[:, 2 * i:2 * i + 2, :].rearrange("p a n -> p (a n)").rearrange("p (e t) -> p e t", e=E)
                    for i in range(2)]
        zero_r = pinv[:, 4:6, :].rearrange("p a n -> p (a n)")
        cnt = sb("cnt", [P, E])
        cnt_i = sb("cnt_i", [P, E], i32)
        pbase = sb("pbase", [P, E])
        pend = sb("pend", [P, E])
        iota_p1 = sb("iota_p1", [P, 1])
        iota_tk = sb("iota_tk", [P, T, TOPK])
        iota_b = sb("iota_b", [P, NBLK], fp16)
        iota_b2 = sb("iota_b2", [P, 2])
        iota_d = sb("iota_d", [P, NBLK])
        blk_cmp = sb("blk_cmp", [P, 2, E])
        blk_exp = sb("blk_exp", [P, 2])
        exp_row = sb("exp_row", [1, 2 * P], i32)
        idx_src, idx_dst = [of_att(NBLK).bitcast(mybir.dt.uint32) for _ in range(2)]
        xd = nc.dram_tensor("xd", [P * T, D], fp32, kind="Internal").ap()
        yd = nc.dram_tensor("yd", [DUMP + NBLK * P, D], fp32, kind="Internal").ap()
        xnf = xn[:, :, :].rearrange("p t d -> p (t d)")
        hot_lane = xnf[:, 0:TOPK * P].bitcast(bf16).rearrange("p (a k n) -> p a k n", a=2, k=TOPK)
        hot_blk = xnf[:, TOPK * P:TOPK * P + 2 * TOPK * NBLK].bitcast(bf16)\
            .rearrange("p (a k b n) -> p a k b n", a=2, k=TOPK, b=2)
        xg = xnf[:, 0:4 * D].rearrange("p (a d) -> p a d", a=4)
        yg = xnf[:, 4 * D:8 * D].rearrange("p (a d) -> p a d", a=4)
        xgT = xnf[:, 8 * D:10 * D].rearrange("p (a d) -> p a d", a=2)
        hT = xnf[:, 10 * D:10 * D + 2 * F].rearrange("p (a f) -> p a f", a=2)
        hg = xnf[:, 10 * D + 2 * F:10 * D + 4 * F].rearrange("p (a f) -> p a f", a=2)
        CT = 4
        yk = shared[:, 0:2 * TOPK * CT * D].rearrange("p (a k n) -> p a k n", a=2, k=TOPK)
        khot = [k0, k1, k2, k3]
        gate, topf = [idx_f[:, a, :].rearrange("p (t k) -> p t k", t=T) for a in range(2)]
        gsum = p1m

        bank = [ctx.enter_context(nc.psum_tensor(f"bank{i}", [P, 512], fp32)) for i in range(8)]

        x_in = [sem(f"x_in{b}") for b in range(B)]
        wv_in, wqkv_in, wt_in, outw_in, qk_in, band_in = [sem(s) for s in (
            "wv_in", "wqkv_in", "wt_in", "outw_in", "qk_in", "band_in")]
        edge_in, colw_done, colb_in, ffnc_in = [sem(s) for s in ("edge_in", "colw_done", "colb_in", "ffnc_in")]
        w_in, b1_in, b2_in, b2_cut_ready, b2w_done, b2p_in = [sem(s) for s in (
            "w_in", "b1_in", "b2_in", "b2_cut_ready", "b2w_done", "b2p_in")]
        const_step, const_ready = sem("const_step"), sem("const_ready")
        dve_step, act_step = sem("dve_step"), sem("act_step")
        stat_ready, std_ready, xn_ready, xnT_ps, xnT_ready, val_ps, val_ready, xl_ready = [sem(s) for s in (
            "stat_ready", "std_ready", "xn_ready", "xnT_ps", "xnT_ready", "val_ps", "val_ready", "xl_ready")]
        ql_ps, ql_ready, kl_ps, kl_ready, v_ps, v_ready = [sem(s) for s in (
            "ql_ps", "ql_ready", "kl_ps", "kl_ready", "v_ps", "v_ready")]
        a2_ps, a2_shift, a2_exp, a2_ready = [sem(s) for s in ("a2_ps", "a2_shift", "a2_exp", "a2_ready")]
        r_ps, r1_ready, r3_ready, s3_ps, s3_max, p3_ready, p3T_ps, p3T_ready, a3v_ps, a3v_ready = [sem(s) for s in (
            "r_ps", "r1_ready", "r3_ready", "s3_ps", "s3_max", "p3_ready", "p3T_ps", "p3T_ready", "a3v_ps", "a3v_ready")]
        s1_ps, s1_shift, s1_exp, p1_ready, p1T_ps, p1T_ready = [sem(s) for s in (
            "s1_ps", "s1_shift", "s1_exp", "p1_ready", "p1T_ps", "p1T_ready")]
        xT_ready = sem("xT_ready")
        band_ps, band_ready = sem("band_ps"), sem("band_ready")
        xbd_ready, xT_ps, max_ready, max_ps, sinv_row, sinv_ps = [sem(s) for s in (
            "xbd_ready", "xT_ps", "max_ready", "max_ps", "sinv_row", "sinv_ps")]
        pz_ps, t_ready, pzT_ready, tz_ps, zn_ps, z_ready, zT_ready = [sem(s) for s in (
            "pz_ps", "t_ready", "pzT_ready", "tz_ps", "zn_ps", "z_ready", "zT_ready")]
        m_ps, m_ready, outT_ps, outT_ready, xg_ps, enc0_ready, enc_ready = [sem(s) for s in (
            "m_ps", "m_ready", "outT_ps", "outT_ready", "xg_ps", "enc0_ready", "enc_ready")]
        encT_ps, encT_ready, q_ps, q_ready, k_ps, ksp_ready = [sem(s) for s in (
            "encT_ps", "encT_ready", "q_ps", "q_ready", "k_ps", "ksp_ready")]
        colT_need, colT_ps, colT_ready = [sem(s) for s in ("colT_need", "colT_ps", "colT_ready")]
        ohc_ready, ohr_ready, kg_ps, kv_ready, kvh_ready, kvr_ready, kvm_ready, kvs_ready, g_done = [sem(s) for s in (
            "ohc_ready", "ohr_ready", "kg_ps", "kv_ready", "kvh_ready", "kvr_ready", "kvm_ready", "kvs_ready",
            "g_done")]
        g_ps, prod_ready, arow_ps, amax_ready, aexp_ready, arow_ready, alpha_ps = [sem(s) for s in (
            "g_ps", "prod_ready", "arow_ps", "amax_ready", "aexp_ready", "arow_ready", "alpha_ps")]
        xl_done, sw_ready = sem("xl_done"), sem("sw_ready")
        comb_ready, ksq_ps, logit_ps, lshift, lexp = [sem(s) for s in (
            "comb_ready", "ksq_ps", "logit_ps", "lshift", "lexp")]
        xd_done, chosen_ready, prefix_ps, bexp_ready, bexp_ps, exp_ready = [sem(s) for s in (
            "xd_done", "chosen_ready", "prefix_ps", "bexp_ready", "bexp_ps", "exp_ready")]
        hot_ready, hot_used = sem("hot_ready"), sem("hot_used")
        table_ps, idx_ready = sem("table_ps"), sem("idx_ready")
        xg_in, y_out = [[sem(f"{s}{i}") for i in range(4)] for s in ("xg_in", "y_out")]
        xgT_ps, xgT_ready, up_ps, hb_ready, h_ready, hT_ps, hT_ready, down_ps, y_ready = [sem(s) for s in (
            "xgT_ps", "xgT_ready", "up_ps", "hb_ready", "h_ready", "hT_ps", "hT_ready", "down_ps", "y_ready")]
        yk_in, yk_used = [[sem(f"{s}{i}") for i in range(2)] for s in ("yk_in", "yk_used")]
        out_ready, out_done = sem("out_ready"), sem("out_done")

        block = ctx.enter_context(nc.Block())

        def tok(t):
            return slice(t * P, (t + 1) * P)

        def slot(s):
            return s % 2

        def nth(g, s):
            return BG * g + s

        def freed(eng, sem, count):
            if not (isinstance(count, int) and count <= 0):
                eng.wait_ge(sem, count)

        GROUPS = NBLK // BG

        def group_loop(eng, body):
            body(0)
            body(1)
            with eng.Fori(2, GROUPS - 1) as g:
                body(g)
            body(GROUPS - 1)

        def follows(g, s):
            return not isinstance(g, int) or BG * g + s < NBLK

        def precedes(g, s):
            return not isinstance(g, int) or BG * g + s >= 0

        def experts(eng, g):
            _, e = nc.values_load_multi_w_load_instructions(
                exp_row[0:1, bass.ds(BG * g, BG)], engines=[eng.engine], min_val=0, max_val=E - 1,
                skip_runtime_bounds_check_because="the row is clamped to 0..E-1 when it is made")
            return e

        def over_b(ap, t):
            return ap[:, :, :].rearrange("p (b t) d -> p t b d", t=NT)[:, t, :, :]

        @block.sync
        def _(sp):
            for b in range(B):
                sp.dma_start(x[:, b * NT:(b + 1) * NT, :],
                             dense[b, :, :].rearrange("(t p) d -> p t d", p=P)).then_inc(x_in[b], 16)
                if b == 0:
                    sp.dma_start(wv_sb[:, :], wv_w).then_inc(wv_in, 16)
                    sp.dma_start(wvb_row[:, :], wv_b.rearrange("(a d) -> a d", a=1).broadcast_to([P, D]))\
                      .then_inc(wv_in, 16)
            sp.dma_start(b2_sb[:, :], b2.rearrange("e (c n) -> (e c) n", c=P // E))\
              .then_inc(b2_in, 16)
            sp.dma_start(keysT[:, :], keys_t).then_inc(ffnc_in, 16)
            sp.dma_start(rwT[:, :], rw_t).then_inc(ffnc_in, 16)
            sp.dma_start(rb_row[:, :], rb.rearrange("(a d) -> a d", a=1).broadcast_to([P, E])).then_inc(ffnc_in, 16)
            sp.wait_ge(colT_ready, 1)
            sp.dma_start(col_dram.rearrange("(c e) -> c e", e=P), colT[:, :]).then_inc(colw_done, 16)
            sp.wait_ge(colw_done, 16)
            sp.dma_start(colb[:, :], col_dram.rearrange("(a e) -> a e", a=1).broadcast_to([P, EDGES]))\
              .then_inc(colb_in, 16)
            sp.wait_ge(b2_cut_ready, 1)
            sp.dma_start(b2_dram.rearrange("s (p n) -> p s n", p=P), b2_cut[:, :, :]).then_inc(b2w_done, 16)
            sp.wait_ge(b2w_done, 16)
            sp.dma_start(b2_parts[:, :, :].rearrange("s e d -> s (e d)"), b2_dram).then_inc(b2p_in, 16)
            sp.wait_ge(xg_ps, 1)
            sp.dma_start(b1_row, b1.rearrange("(a e) f -> a (e f)", a=1).broadcast_to([P, E * F])
                         .rearrange("p (e f) -> p e f", e=E)).then_inc(b1_in, 16)
            sp.wait_ge(g_ps, 1)
            sp.dma_start(w1_sb, w1_t).then_inc(w_in, 16)
            sp.dma_start(w2_sb, w2_t).then_inc(w_in, 16)
            for b in range(B):
                sp.wait_ge(xn_ready, B + b + 1)
                sp.dma_start(xd.rearrange("(p t) d -> p t d", p=P)[:, b * NT:(b + 1) * NT, :],
                             xn[:, b * NT:(b + 1) * NT, :]).then_inc(xd_done, 16)
            for s in range(4):
                sp.wait_ge(y_out[s], 16 * NBLK // 4)
            for c in range(T // CT):
                if c >= 2:
                    sp.wait_ge(yk_used[c % 2], c // 2)
                sp.dma_start(yk[:, c % 2, :, :], yd[0:DUMP, :].rearrange("(k p t) d -> p k (t d)", k=TOPK, p=P)
                             [:, :, c * CT * D:(c + 1) * CT * D]).then_inc(yk_in[c % 2], 16)
            for b in range(B):
                sp.wait_ge(out_ready, b + 1)
                sp.dma_start(out[b, :, :].rearrange("(t p) d -> p t d", p=P), x[:, b * NT:(b + 1) * NT, :])\
                  .then_inc(out_done, 16)
            sp.wait_ge(out_done, 16 * B)

        @block.gpsimd
        def _(pool):
            steps = [0]

            def step(ins):
                steps[0] += 1
                ins.then_inc(const_step, 1)
                pool.wait_ge(const_step, steps[0])

            step(pool.memset(ident[:, :], 0.0))
            step(pool.affine_select(out=ident[:, :], in_=ident[:, :], compare_op=ALU.not_equal, fill=1.0,
                                    base=0, pattern=[[-1, P]], channel_multiplier=1))
            step(pool.memset(flip[:, :], 0.0))
            pool.affine_select(out=flip[:, :], in_=flip[:, :], compare_op=ALU.not_equal, fill=1.0,
                               base=1 - P, pattern=[[1, P]], channel_multiplier=1)
            pool.memset(eps_c[:, :], EPS)
            pool.memset(zeros[:, :], 0.0)
            pool.iota(iota_e[:, :], pattern=[[1, E]], base=0, channel_multiplier=0,
                      allow_small_or_imprecise_dtypes=True)
            pool.memset(ones[:, :], 1.0).then_inc(const_ready, 1)
            for m, w in ((blk_j, L), (blk_d, DH)):
                step(pool.memset(m[:, :, :], 1.0))
                step(pool.affine_select(out=m[:, :, :], in_=m[:, :, :], compare_op=ALU.is_ge, fill=0.0,
                                        base=0, pattern=[[-L, HG], [0, w]], channel_multiplier=1))
                step(pool.affine_select(out=m[:, :, :], in_=m[:, :, :], compare_op=ALU.is_ge, fill=0.0,
                                        base=L - 1, pattern=[[L, HG], [0, w]], channel_multiplier=-1))
            step(pool.memset(identw[:, :, :, :], 0.0))
            for n, c in enumerate((7.0, 15.0, 13.0)):
                step(pool.affine_select(out=identw[:, n, :, :], in_=identw[:, n, :, :], compare_op=ALU.not_equal,
                                        fill=c, base=0, pattern=[[0, G2], [-1, P]], channel_multiplier=1))
            pool.iota(iota_c[:, :], pattern=[[P, NT]], base=0, channel_multiplier=1,
                      allow_small_or_imprecise_dtypes=True)
            pool.iota(iota_r[:, :], pattern=[[1, N]], base=0, channel_multiplier=0,
                      allow_small_or_imprecise_dtypes=True).then_inc(const_ready, 1)
            step(pool.memset(upper[:, :], 1.0))
            pool.affine_select(out=upper[:, :], in_=upper[:, :], compare_op=ALU.is_gt, fill=0.0, base=0,
                               pattern=[[1, P]], channel_multiplier=-1)
            pool.memset(ones_b[:, :], 1.0)

            def iota(out, pattern, base, mult):
                return pool.iota(out, pattern=pattern, base=base, channel_multiplier=mult,
                                 allow_small_or_imprecise_dtypes=True)

            iota(iota_p1[:, :], [[0, 1]], 1, 1)
            iota(iota_tk[:, :, :], [[1, T], [T, TOPK]], 0, 0)
            iota(iota_b[:, :], [[1, NBLK]], 0, 0)
            iota(iota_b2[:, :], [[P, 2]], 0, 1)
            iota(iota_d[:, :], [[P, NBLK]], DUMP, 1).then_inc(const_ready, 1)
            pool.wait_ge(b2_in, 16)
            step(pool.tensor_copy(b2_cut[:, 0, :], b2_sb[:, :]))
            step(pool.tensor_tensor(out=b2_res[:, :], in0=b2_sb[:, :], in1=b2_cut[:, 0, :], op=ALU.subtract))
            step(pool.tensor_copy(b2_cut[:, 1, :], b2_res[:, :]))
            pool.tensor_tensor(out=b2_cut[:, 2, :], in0=b2_res[:, :], in1=b2_cut[:, 1, :], op=ALU.subtract)\
                .then_inc(b2_cut_ready, 1)
            pool.wait_ge(enc0_ready, 1)
            for t in range(NT):
                e = over_b(xn, t)[:, 1:B, :]
                last = pool.tensor_tensor(out=e, in0=e, in1=xgb[:, t, :].unsqueeze(1).broadcast_to([P, B - 1, D]),
                                          op=ALU.add)
            last.then_inc(enc_ready, 1)
            LEAD = 6
            pool.wait_ge(idx_ready, 1)
            pool.wait_ge(xd_done, 16 * B)
            for j in range(NBLK + LEAD):
                if j < NBLK:
                    if j >= 4:
                        pool.wait_ge(xgT_ps, j - 3)
                    pool.indirect_dma_start(out=xg[:, j % 4, :], out_offset=None, in_=xd[:, :],
                                            in_offset=bass.IndirectOffsetOnAxis(ap=idx_src[:, j:j + 1], axis=0))\
                        .then_inc(xg_in[j % 4], 16)
                i = j - LEAD
                if i >= 0:
                    pool.wait_ge(y_ready, i + 1)
                    pool.indirect_dma_start(out=yd[:, :],
                                            out_offset=bass.IndirectOffsetOnAxis(ap=idx_dst[:, i:i + 1], axis=0),
                                            in_=yg[:, i % 4, :], in_offset=None).then_inc(y_out[i % 4], 16)

        @block.scalar
        def _(act):
            steps = [0]

            def step(ins):
                steps[0] += 1
                ins.then_inc(act_step, 1)
                act.wait_ge(act_step, steps[0])

            act.dma_start(wqkv_sb[:, :], qkv_w).then_inc(wqkv_in, 16)
            act.dma_start(wqT_sb[:, :, :], wq_t).then_inc(wt_in, 16)
            act.dma_start(wkT_sb[:, :, :], wk_t).then_inc(wt_in, 16)
            act.dma_start(idx_i[:, 0, :], adj_rows.rearrange("(p c) -> p c", p=P)).then_inc(edge_in, 16)
            act.dma_start(idx_i[:, 1, :], adj_cols.rearrange("(p c) -> p c", p=P)).then_inc(edge_in, 16)
            act.dma_start(vals[:, :], adj_vals.rearrange("(p c) -> p c", p=P)).then_inc(edge_in, 16)
            act.dma_start(outw_sb[:, :, :], out_w.rearrange("(c p) d -> p c d", p=P)).then_inc(outw_in, 16)
            act.dma_start(outb_row[:, :], out_b.rearrange("(a d) -> a d", a=1).broadcast_to([P, D]))\
               .then_inc(outw_in, 16)
            for s in range(NS):
                act.dma_start(wq3_sb[:, s, :], wq).then_inc(qk_in, 16)
            act.dma_start(wk_sb[:, :], wk).then_inc(qk_in, 16)
            act.dma_start(band_up[:, :, :], bass.AP(tensor=conv_pad.tensor, offset=0,
                                                    ap=[[1, P], [conv_pad.shape[1], H], [1, WIN]]))\
               .then_inc(band_in, 16)

            act.wait_ge(const_ready, 1)
            for b in range(B):
                act.wait_ge(stat_ready, b + 1)
                act.activation(std[:, b * NT:(b + 1) * NT], mv[:, b * NT:(b + 1) * NT, 1], ACT.Sqrt,
                               bias=eps_c[:, 0:1]).then_inc(std_ready, 1)
                act.wait_ge(xnT_ps, b + 1)
                act.activation(xnT[:, b * N:(b + 1) * N], bank[b % 2][:, :], ACT.Copy).then_inc(xnT_ready, 1)
            for c, w in enumerate(BAND_CUTS):
                act.wait_ge(band_ps, c + 1)
                act.activation(band[:, :, :].rearrange("p h m -> p (h m)")[:, c * N:c * N + w], bank[4 + c][:, 0:w],
                               ACT.Copy).then_inc(band_ready, 1)
            act.wait_ge(colT_ps, 1)
            act.activation(colT[:, :], bank[3][:, 0:P], ACT.Copy).then_inc(colT_ready, 1)
            for t in range(NT):
                act.wait_ge(v_ps, t + 1)
                act.activation(v_sb[:, t, :], bank[4 + t][:, :], ACT.Copy).then_inc(v_ready, 1)
            for c in range(4):
                act.wait_ge(ql_ps, c + 1)
                act.activation(qlT[:, 2 * c:2 * c + 2, :].rearrange("p h n -> p (h n)"), bank[c][0:DH, :], ACT.Copy,
                               scale=DH ** -0.5 / LW).then_inc(ql_ready, 1)
            act.wait_ge(r_ps, 2)
            act.activation(r3[:, :], bank[2][:, 0:H * L], ACT.Copy).then_inc(r3_ready, 1)
            act.wait_ge(a2_shift, 1)
            act.activation(a2[:, :, :], a2[:, :, :], ACT.Exp).then_inc(a2_exp, 1)
            for g in range(G2):
                act.wait_ge(s3_max, g + 1)
                act.activation(p3[:, g, :], bank[3 - g][:, :], ACT.Exp, bias=p3m[:, g:g + 1],
                               accum_out=p3s[:, g:g + 1]).then_inc(p3_ready, 1)
            act.wait_ge(s1_shift, 1)
            act.activation(p1[:, :, :], p1[:, :, :], ACT.Exp).then_inc(s1_exp, 1)
            for g in range(G2):
                act.wait_ge(p3T_ps, g + 1)
                act.activation(p3T[:, g, :, :].rearrange("p c n -> p (c n)"), bank[3 - g][:, :], ACT.Copy)\
                   .then_inc(p3T_ready, 1)
            for g in range(G2):
                act.wait_ge(p1T_ps, g + 1)
                act.activation(p1T[:, g, :], bank[1 - g][:, :], ACT.Copy).then_inc(p1T_ready, 1)
            with act.Fori(0, PINV) as i:
                act.wait_ge(pz_ps, 2 * i + 2)
                act.activation(pzT[:, :, :].rearrange("p g n -> p (g n)"), bank[3][:, 0:G2 * P], ACT.Copy)\
                   .then_inc(pzT_ready, 1)
                act.wait_ge(zn_ps, 2 * i + 2)
                act.activation(zT[:, :, :].rearrange("p g n -> p (g n)"), bank[3][:, 0:G2 * P], ACT.Copy,
                               scale=0.25).then_inc(zT_ready, 1)
            act.wait_ge(m_ps, 1)
            act.activation(m_bd[:, :, :].rearrange("p g n -> p (g n)"), bank[2][:, :], ACT.Copy).then_inc(m_ready, 1)
            for c in range(2):
                act.wait_ge(outT_ps, 2 * c + 1)
                act.activation(outT[:, 2 * c, :], bank[4 + 2 * c][:, :], ACT.Copy).then_inc(outT_ready, 1)
            act.wait_ge(encT_ps, 1)
            act.activation(encT[:, :], bank[1][:, :], ACT.Copy).then_inc(encT_ready, 1)
            act.wait_ge(q_ps, 1)
            act.activation(q96[:, :], bank[2][0:NS * QK, :], ACT.Copy, scale=QK ** -0.5).then_inc(q_ready, 1)
            with act.Fori(0, NG // 2) as pair:
                for s in range(2):
                    act.wait_ge(kv_ready, 2 * pair + s + 3)
                    act.activation(kvs[:, s, :, 0, :], kv[:, s, :, :], ACT.Copy).then_inc(kvh_ready, 1)
                    act.wait_ge(kvr_ready, 2 * pair + s + 1)
                    act.activation(kvs[:, s, :, 1, :], kvr[:, s, :, :], ACT.Copy).then_inc(kvm_ready, 1)
            act.wait_ge(amax_ready, 1)
            act.activation(arow[:, :], bank[5][0:1, :], ACT.Exp, bias=asc[0:1, 0:1],
                           accum_out=asc[0:1, 1:2]).then_inc(aexp_ready, 1)
            for t in range(NT):
                act.wait_ge(xl_done, t + 1)
                step(act.activation(sg[:, t % 2, :, :], xl[:, t % 2, :, :], ACT.Sigmoid, scale=-1.0))
                act.activation(sg[:, t % 2, :, :], sg[:, t % 2, :, :], ACT.Square).then_inc(sw_ready, 1)
            act.wait_ge(stat_ready, B + 1)
            act.activation(std[:, :], mv[:, :, 1], ACT.Sqrt, bias=eps_c[:, 0:1], scale=4.0).then_inc(std_ready, 1)
            act.wait_ge(stat_ready, B + 2)
            act.activation(std[:, :], mv[:, :, 1], ACT.Sqrt, bias=eps_c[:, 0:1]).then_inc(std_ready, 1)
            for b in range(B):
                act.wait_ge(xnT_ps, B + b + 1)
                act.activation(xnT[:, b * N:(b + 1) * N], bank[b % 2][:, :], ACT.Copy).then_inc(xnT_ready, 1)
            act.wait_ge(lshift, 1)
            act.activation(gate[:, :, :], gate[:, :, :], ACT.Exp).then_inc(lexp, 1)

            def xT(g, s):
                act.wait_ge(xgT_ps, nth(g, s) + 1)
                act.activation(xgT[:, slot(s), :], bank[slot(s)][:, 0:P], ACT.Copy).then_inc(xgT_ready, 1)

            def gelu(g, s):
                act.wait_ge(hb_ready, nth(g, s) + 1)
                act.activation(hg[:, slot(s), :], hb[:, slot(s), :], ACT.Gelu).then_inc(h_ready, 1)

            def y(g, s):
                act.wait_ge(down_ps, nth(g, s) + 1)
                freed(act, y_out[s % 4], 16 * (g + s // 4))
                act.activation(yg[:, s % 4, :], bank[6 + slot(s)][:, 0:P], ACT.Copy).then_inc(y_ready, 1)

            def act_group(g):
                for s in range(BG):
                    gelu(g, s)
                    if precedes(g, s - 2):
                        y(g, s - 2)
                    if follows(g, s + 2):
                        xT(g, s + 2)

            xT(0, 0)
            xT(0, 1)
            group_loop(act, act_group)
            for s in (-2, -1):
                y(GROUPS, s)
            act.wait_ge(stat_ready, B + 3)
            act.activation(std[:, :], mv[:, :, 1], ACT.Sqrt, bias=eps_c[:, 0:1]).then_inc(std_ready, 1)

        @block.vector
        def _(dve):
            steps = [0]
            v = nc.vector

            def step(ins):
                steps[0] += 1
                ins.then_inc(dve_step, 1)
                dve.wait_ge(dve_step, steps[0])

            def row_stats(src, t, last):
                for i in t:
                    ins = v.bn_stats(stats[:, i, :], src[:, i, :])
                step(ins)
                for i in t:
                    ins = v.bn_aggr(mv[:, i, :], stats[:, i, :])
                ins.then_inc(last, 1)

            def batch(b):
                return range(b * NT, (b + 1) * NT)

            dve.wait_ge(edge_in, 48)
            step(v.tensor_copy(idx_f[:, :, :], idx_i[:, :, :]))
            step(v.tensor_scalar(neg[:, :], idx_f[:, 1, :], 0.0, float(N), ALU.is_lt, ALU.mult))
            step(v.tensor_tensor(out=idx_f[:, 1, :], in0=idx_f[:, 1, :], in1=neg[:, :], op=ALU.add))
            v.tensor_scalar(idx_f[:, 1, :], idx_f[:, 1, :], 0.0, float(N - 1), ALU.max, ALU.min)\
             .then_inc(colT_need, 1)

            def normalise(b):
                dve.wait_ge(std_ready, b + 1)
                step(v.reciprocal(rstd[:, b * NT:(b + 1) * NT], std[:, b * NT:(b + 1) * NT]))
                for t in batch(b):
                    ins = v.tensor_scalar(xn[:, t, :], x[:, t, :], mv[:, t, 0:1], rstd[:, t:t + 1],
                                          ALU.subtract, ALU.mult)
                ins.then_inc(xn_ready, 1)

            def values(b):
                dve.wait_ge(xnT_ready, b + 1)
                v.tensor_reduce(out=xlT[:, b * L:(b + 1) * L],
                                in_=xnT[:, b * N:(b + 1) * N].rearrange("p (l w) -> p l w", w=LW),
                                axis=AX.X, op=ALU.add).then_inc(xl_ready, 1)
                if b == 0:
                    dve.wait_ge(wv_in, 32)
                dve.wait_ge(val_ps, b + 1)
                v.tensor_tensor(out=value[:, b * NT:(b + 1) * NT, :],
                                in0=bank[2 + b % 2][:, :].rearrange("p (t d) -> p t d", t=NT),
                                in1=wvb_row[:, :].unsqueeze(1).broadcast_to([P, NT, D]), op=ALU.add)\
                 .then_inc(val_ready, 1)

            for b in range(B):
                dve.wait_ge(x_in[b], 16)
                row_stats(x, batch(b), stat_ready)
                if b >= 1:
                    normalise(b - 1)
                if b >= 2:
                    values(b - 2)
            normalise(B - 1)
            values(B - 2)
            values(B - 1)

            dve.wait_ge(const_ready, 2)
            for c in range(4):
                dve.wait_ge(kl_ps, c + 1)
                v.tensor_scalar(klT[:, 2 * c:2 * c + 2, :].rearrange("p h n -> p (h n)"), bank[c][0:DH, :],
                                1.0 / LW, None, ALU.mult).then_inc(kl_ready, 1)
            dve.wait_ge(r_ps, 1)
            v.tensor_scalar(r1[:, :], bank[1][:, 0:H * L], DH ** -0.5, None, ALU.mult).then_inc(r1_ready, 1)

            def shift_max(ps, dst, mx, out_sem):
                step(v.tensor_reduce(out=mx, in_=ps, axis=AX.X, op=ALU.max))
                v.tensor_tensor(out=dst, in0=ps, in1=mx.unsqueeze(2).broadcast_to(list(dst.shape)),
                                op=ALU.subtract).then_inc(out_sem, 1)

            def normalise_rows(p, s):
                step(v.tensor_reduce(out=s, in_=p, axis=AX.X, op=ALU.add))
                step(v.reciprocal(s, s))
                return v.tensor_tensor(out=p, in0=p, in1=s.unsqueeze(2).broadcast_to(list(p.shape)), op=ALU.mult)

            dve.wait_ge(a2_ps, 1)
            shift_max(bank[0][:, :].rearrange("p (a j) -> p a j", j=L), a2[:, :, :], a2m[:, :], a2_shift)
            for g in range(G2):
                dve.wait_ge(s3_ps, g + 1)
                v.tensor_reduce(out=p3m[:, g:g + 1], in_=bank[3 - g][:, :], axis=AX.X, op=ALU.max, negate=True)\
                 .then_inc(s3_max, 1)
            dve.wait_ge(a2_exp, 1)
            normalise_rows(a2[:, :, :], a2s[:, :]).then_inc(a2_ready, 1)
            dve.wait_ge(a2_ready, 1)
            step(v.tensor_tensor(out=xbd[:, :, :].rearrange("p g (h j) -> p g h j", h=HG),
                                 in0=a2[:, 0:G2, :].unsqueeze(2).broadcast_to([P, G2, HG, L]),
                                 in1=blk_j[:, :, :].unsqueeze(1).broadcast_to([P, G2, HG, L]), op=ALU.mult))
            step(v.tensor_reduce(out=a2s[:, :], in_=a2[:, :, :], axis=AX.X, op=ALU.add))
            v.tensor_reduce(out=mx2[:, 0:1], in_=a2s[:, :], axis=AX.X, op=ALU.max).then_inc(xbd_ready, 1)
            dve.wait_ge(s1_ps, 1)
            for h in range(2):
                sl = slice(h * 16, (h + 1) * 16)
                step(v.tensor_reduce(out=p1m[:, sl], in_=bank[1 - h][:, :].rearrange("p (a j) -> p a j", j=L),
                                     axis=AX.X, op=ALU.max))
                ins = v.tensor_tensor(out=p1[:, sl, :], in0=bank[1 - h][:, :].rearrange("p (a j) -> p a j", j=L),
                                      in1=p1m[:, sl].unsqueeze(2).broadcast_to([P, 16, L]), op=ALU.subtract)
            ins.then_inc(s1_shift, 1)
            dve.wait_ge(xT_ps, 1)
            v.tensor_reduce(out=mx2[:, 1:2], in_=bank[0][:, :], axis=AX.X, op=ALU.max).then_inc(max_ready, 1)
            v.tensor_copy(xT[:, :, :].rearrange("p g n -> p (g n)"), bank[7][:, 0:G2 * P]).then_inc(xT_ready, 1)
            dve.wait_ge(s1_exp, 1)
            normalise_rows(p1[:, :, :], p1s[:, :]).then_inc(p1_ready, 1)
            dve.wait_ge(max_ps, 1)
            step(v.tensor_reduce(out=srow[0:1, 0:2], in_=bank[7][0:1, 0:2 * P].rearrange("p (a n) -> p a n", a=2),
                                 axis=AX.X, op=ALU.max))
            step(v.tensor_tensor(out=srow[0:1, 2:3], in0=srow[0:1, 0:1], in1=srow[0:1, 1:2], op=ALU.mult))
            v.reciprocal(srow[0:1, 3:4], srow[0:1, 2:3]).then_inc(sinv_row, 1)
            dve.wait_ge(sinv_ps, 1)
            step(v.tensor_copy(sinv[:, :], bank[7][:, 0:1]))
            v.tensor_scalar(z[:, :, :], xT[:, :, :], sinv[:, 0:1], None, ALU.mult).then_inc(z_ready, 1)
            v.tensor_scalar(zT[:, :, :], xbd[:, :, :], sinv[:, 0:1], None, ALU.mult).then_inc(zT_ready, 1)
            dve.wait_ge(a3v_ps, 1)
            step(v.reciprocal(p3s[:, :], p3s[:, :]))
            for g in range(G2):
                ins = v.scalar_tensor_tensor(out=a3v[:, g, :], in0=bank[3][:, g * 256:(g + 1) * 256],
                                             scalar=p3s[:, g:g + 1],
                                             in1=blk_d[:, :, :].rearrange("p h d -> p (h d)"),
                                             op0=ALU.mult, op1=ALU.mult)
            ins.then_inc(a3v_ready, 1)
            with dve.Fori(0, PINV) as i:
                for n in range(3):
                    if n == 0:
                        dve.wait_ge(pz_ps, 2 * i + 1)
                    else:
                        dve.wait_ge(tz_ps, 2 * i + n)
                    v.scalar_tensor_tensor(out=tz[:, :, :], in0=bank[2 + (n == 2)][:, 0:G2 * P]
                                           .rearrange("p (g n) -> p g n", g=G2), scalar=-1.0,
                                           in1=identw[:, n, :, :], op0=ALU.mult, op1=ALU.add).then_inc(t_ready, 1)
                dve.wait_ge(zn_ps, 2 * i + 1)
                v.tensor_scalar(z[:, :, :].rearrange("p g n -> p (g n)"), bank[2][:, 0:G2 * P], 0.25, None,
                                ALU.mult).then_inc(z_ready, 1)
            for c in range(2):
                dve.wait_ge(outT_ps, 2 * c + 2)
                v.tensor_copy(outT[:, 2 * c + 1, :], bank[5 + 2 * c][:, :]).then_inc(outT_ready, 1)
            dve.wait_ge(outw_in, 32)
            dve.wait_ge(xg_ps, 1)
            step(v.tensor_tensor(out=xgb[:, :, :], in0=bank[0][:, :].rearrange("p (t d) -> p t d", t=NT),
                                 in1=outb_row[:, :].unsqueeze(1).broadcast_to([P, NT, D]), op=ALU.add))
            v.tensor_tensor(out=xn[:, 0:NT, :], in0=xn[:, 0:NT, :], in1=xgb[:, :, :], op=ALU.add)\
             .then_inc(enc0_ready, 1)
            dve.wait_ge(k_ps, 1)
            step(v.tensor_copy(kf[:, :, :].rearrange("p c q -> p (c q)"), bank[3][:, 0:NT * QK]))
            step(v.tensor_copy(ksp[:, :, 0, :], kf[:, :, :]))
            step(v.tensor_tensor(out=kres[:, :, :], in0=kf[:, :, :], in1=ksp[:, :, 0, :], op=ALU.subtract))
            step(v.tensor_copy(ksp[:, :, 1, :], kres[:, :, :]))
            v.tensor_tensor(out=ksp[:, :, 2, :], in0=kres[:, :, :], in1=ksp[:, :, 1, :], op=ALU.subtract)\
             .then_inc(ksp_ready, 1)
            dve.wait_ge(colb_in, 16)

            def one_hots(pair, s):
                g = 2 * pair + s
                dve.wait_ge(kg_ps, 2 * pair + s + 1)
                for c in range(NT):
                    ins = v.tensor_scalar(oh_c[:, s, c, :], colb[:, bass.ds(g * (EG * P), EG * P)],
                                          iota_c[:, c:c + 1], None, ALU.is_equal)
                ins.then_inc(ohc_ready, 1)
                dve.wait_ge(g_done, 2 * pair + s + 1)
                for j in range(EG):
                    ins = v.tensor_scalar(oh_r[:, s, j, :], iota_r[:, :], idx_f[:, 0, bass.ds(g * EG + j, 1)], None,
                                          ALU.is_equal)
                ins.then_inc(ohr_ready, 1)

            def parts(pair, s):
                g = 2 * pair + s
                dve.wait_ge(kg_ps, 2 * pair + s + 3)
                v.tensor_tensor(out=kv[:, s, :, :],
                                in0=bank[s][:, 0:EG * QK].rearrange("p (j q) -> p j q", j=EG),
                                in1=vals[:, bass.ds(g * EG, EG)].unsqueeze(2).broadcast_to([P, EG, QK]),
                                op=ALU.mult).then_inc(kv_ready, 1)
                dve.wait_ge(kvh_ready, 2 * pair + s + 1)
                v.tensor_tensor(out=kvr[:, s, :, :], in0=kv[:, s, :, :], in1=kvs[:, s, :, 0, :], op=ALU.subtract)\
                 .then_inc(kvr_ready, 1)
                dve.wait_ge(kvm_ready, 2 * pair + s + 1)
                v.tensor_tensor(out=kvs[:, s, :, 2, :], in0=kvr[:, s, :, :], in1=kvs[:, s, :, 1, :],
                                op=ALU.subtract).then_inc(kvs_ready, 1)

            dve.sem_inc(kv_ready, 2)
            with dve.Fori(0, NG // 2) as pair:
                one_hots(pair, 0)
                one_hots(pair, 1)
                parts(pair, 0)
                parts(pair, 1)
            dve.wait_ge(g_ps, 1)
            dve.wait_ge(q_ready, 1)
            v.tensor_tensor(out=prod[:, :], in0=bank[4][0:NS * QK, :], in1=q96[:, :], op=ALU.mult)\
             .then_inc(prod_ready, 1)
            dve.wait_ge(arow_ps, 1)
            v.tensor_reduce(out=asc[0:1, 0:1], in_=bank[5][0:1, :], axis=AX.X, op=ALU.max, negate=True)\
             .then_inc(amax_ready, 1)
            dve.wait_ge(aexp_ready, 1)
            step(v.reciprocal(asc[0:1, 2:3], asc[0:1, 1:2]))
            v.tensor_scalar(arow[:, :], arow[:, :], asc[0:1, 2:3], None, ALU.mult).then_inc(arow_ready, 1)
            dve.wait_ge(alpha_ps, 1)
            step(v.tensor_copy(alpha[:, :], bank[6][:, 0:NT]))
            dve.wait_ge(enc_ready, 1)

            def gated(t):
                dve.wait_ge(sw_ready, t + 1)
                step(v.tensor_tensor(out=xl[:, t % 2, :, :], in0=xl[:, t % 2, :, :], in1=over_b(xn, t),
                                     op=ALU.subtract))
                step(v.tensor_tensor(out=xl[:, t % 2, :, :], in0=xl[:, t % 2, :, :], in1=sg[:, t % 2, :, :],
                                     op=ALU.mult))
                step(v.tensor_tensor(out=over_b(xn, t), in0=over_b(xn, t), in1=xl[:, t % 2, :, :], op=ALU.add))

            for t in range(NT):
                v.tensor_scalar(xl[:, t % 2, :, :], over_b(value, t), alpha[:, t:t + 1], None, ALU.mult)\
                 .then_inc(xl_done, 1)
                if t >= 1:
                    gated(t - 1)
            gated(NT - 1)
            row_stats(xn, range(T), stat_ready)
            dve.wait_ge(std_ready, B + 1)
            step(v.reciprocal(rstd[:, :], std[:, :]))
            step(v.tensor_scalar(rstd[:, :], rstd[:, :], 2.0, None, ALU.mult))
            for t in range(T):
                ins = v.tensor_scalar(xn[:, t, :], xn[:, t, :], mv[:, t, 0:1], rstd[:, t:t + 1],
                                      ALU.subtract, ALU.mult)
            step(ins)
            step(v.tensor_tensor(out=x[:, :, :], in0=x[:, :, :], in1=xn[:, :, :], op=ALU.add))
            row_stats(x, range(T), stat_ready)
            dve.wait_ge(std_ready, B + 2)
            step(v.reciprocal(rstd[:, :], std[:, :]))
            for b in range(B):
                for t in batch(b):
                    ins = v.tensor_scalar(xn[:, t, :], x[:, t, :], mv[:, t, 0:1], rstd[:, t:t + 1],
                                          ALU.subtract, ALU.mult)
                ins.then_inc(xn_ready, 1)
            dve.wait_ge(ffnc_in, 48)
            v.tensor_tensor(out=ksq[:, :], in0=keysT[:, :], in1=keysT[:, :], op=ALU.mult)
            v.scalar_tensor_tensor(out=comb[:, :], in0=keysT[:, :], scalar=2.0, in1=rwT[:, :],
                                   op0=ALU.mult, op1=ALU.add).then_inc(comb_ready, 1)
            dve.wait_ge(ksq_ps, 1)
            step(v.tensor_tensor(out=lbias[:, :], in0=rb_row[:, :], in1=bank[5][:, 0:E], op=ALU.subtract))
            dve.wait_ge(logit_ps, 1)
            step(v.tensor_tensor(out=logits[:, :, :], in0=bank[6][:, :].rearrange("p (t e) -> p t e", t=T),
                                 in1=lbias[:, :].unsqueeze(1).broadcast_to([P, T, E]), op=ALU.add))
            step(v.tensor_tensor(out=x2n[:, :], in0=rstd[:, :], in1=rstd[:, :], op=ALU.mult))
            step(v.tensor_tensor(out=x2n[:, :], in0=x2n[:, :], in1=mv[:, :, 1], op=ALU.mult))
            step(v.tensor_scalar(x2n[:, :], x2n[:, :], float(D), None, ALU.mult))
            step(v.tensor_tensor(out=logits[:, :, :], in0=logits[:, :, :],
                                 in1=x2n[:, :].unsqueeze(2).broadcast_to([P, T, E]), op=ALU.subtract))
            for t in range(T):
                ins = v.max(out=top8[:, t, :], in_=logits[:, t, :])
            step(ins)
            v.tensor_tensor(out=gate[:, :, :], in0=top8[:, :, 0:TOPK],
                            in1=top8[:, :, 0:1].broadcast_to([P, T, TOPK]), op=ALU.subtract).then_inc(lshift, 1)
            dve.wait_ge(const_ready, 3)
            for t in range(T):
                ins = v.max_index(out=topi[:, t, :], in_max=top8[:, t, :], in_values=logits[:, t, :])
            step(ins)
            step(v.tensor_copy(topf[:, :, :], topi[:, :, 0:TOPK]))
            for k in range(TOPK):
                ins = v.tensor_tensor(out=khot[k][:, :, :], in0=iota_e[:, :].unsqueeze(1).broadcast_to([P, T, E]),
                                      in1=topf[:, :, k:k + 1].broadcast_to([P, T, E]), op=ALU.is_equal)
            step(ins)
            step(v.tensor_tensor(out=chosen[:, :, :], in0=khot[0][:, :, :], in1=khot[1][:, :, :], op=ALU.add))
            step(v.tensor_tensor(out=tmp_e[:, :, :], in0=khot[2][:, :, :], in1=khot[3][:, :, :], op=ALU.add))
            v.tensor_tensor(out=chosen_b[:, :, :], in0=chosen[:, :, :], in1=tmp_e[:, :, :], op=ALU.add)\
             .then_inc(chosen_ready, 1)
            v.memset(zero_r[:, :], 0.0)
            dve.wait_ge(prefix_ps, 2)
            step(v.tensor_copy(tot[:, :, :], bank[1][:, :].rearrange("p (t e) -> p e t", t=T)))
            step(v.tensor_tensor_scan(out=cum[:, :, :].rearrange("p e t -> p (e t)"),
                                      data0=tot[:, :, :].rearrange("p e t -> p (e t)"), data1=zero_r[:, :],
                                      initial=0.0, op0=ALU.add, op1=ALU.add))
            step(v.tensor_tensor(out=tot[:, :, :], in0=cum[:, :, :], in1=tot[:, :, :], op=ALU.subtract))
            step(v.tensor_tensor(out=cnt[:, :], in0=cum[:, :, T - 1], in1=tot[:, :, 0], op=ALU.subtract))
            step(v.tensor_scalar(cnt_i[:, :], cnt[:, :], float(P - 1), None, ALU.add))
            step(v.tensor_scalar(cnt_i[:, :], cnt_i[:, :], 7, 7, ALU.logical_shift_right, ALU.logical_shift_left))
            step(v.tensor_copy(cnt[:, :], cnt_i[:, :]))
            step(v.tensor_tensor_scan(out=pend[:, :], data0=cnt[:, :], data1=zero_r[:, 0:E], initial=0.0,
                                      op0=ALU.add, op1=ALU.add))
            step(v.tensor_tensor(out=pbase[:, :], in0=pend[:, :], in1=cnt[:, :], op=ALU.subtract))
            step(v.tensor_scalar(pend[:, :], pend[:, :], 1.0 / P, None, ALU.mult))
            step(v.tensor_tensor(out=blk_cmp[:, :, :], in0=pend[:, :].unsqueeze(1).broadcast_to([P, 2, E]),
                                 in1=iota_b2[:, :].unsqueeze(2).broadcast_to([P, 2, E]), op=ALU.is_le))
            step(v.tensor_reduce(out=blk_exp[:, :], in_=blk_cmp[:, :, :], axis=AX.X, op=ALU.add))
            v.tensor_scalar(blk_exp[:, :], blk_exp[:, :], float(E - 1), None, ALU.min).then_inc(bexp_ready, 1)
            step(v.tensor_tensor(out=pbase[:, :], in0=pbase[:, :], in1=tot[:, :, 0], op=ALU.subtract))
            step(v.tensor_tensor(out=tot[:, :, :], in0=tot[:, :, :],
                                 in1=pbase[:, :].unsqueeze(2).broadcast_to([P, E, T]), op=ALU.add))
            step(v.tensor_tensor(out=pos_e[:, :, :], in0=bank[0][:, :].rearrange("p (t e) -> p t e", t=T),
                                 in1=tot[:, :, :].rearrange("p e t -> p t e"), op=ALU.add))
            for k in range(TOPK):
                step(v.tensor_tensor(out=khot[k][:, :, :], in0=khot[k][:, :, :], in1=pos_e[:, :, :], op=ALU.mult))
                ins = v.tensor_reduce(out=pos[:, :, k], in_=khot[k][:, :, :], axis=AX.X, op=ALU.add)
            step(ins)
            step(v.tensor_copy(pos_i[:, :, :], pos[:, :, :]))
            v.tensor_scalar(lane_i[:, :, :], pos_i[:, :, :], P - 1, None, ALU.bitwise_and)
            step(v.tensor_scalar(pos_i[:, :, :], pos_i[:, :, :], 7, None, ALU.logical_shift_right))
            v.tensor_copy(lane[:, :, :], lane_i[:, :, :])
            step(v.tensor_copy(blk[:, :, :], pos_i[:, :, :]))
            lane_f, blk_f, tk_f = [a[:, :, :].rearrange("p t k -> p (t k)") for a in (lane, blk, iota_tk)]
            dve.sem_inc(hot_used, 2)
            dve.wait_ge(xd_done, 16 * B)
            with dve.Fori(0, T // 2) as i:
                for s in range(2):
                    dve.wait_ge(hot_used, 2 * i + s + 1)
                    for k in range(TOPK):
                        at = bass.ds((2 * i + s) * TOPK + k, 1)
                        v.tensor_scalar(hot_lane[:, s, k, :], iota_r[:, 0:P], lane_f[:, at], None, ALU.is_equal)
                        v.tensor_scalar(hot_blk[:, s, k, 0, :], iota_b[:, :], blk_f[:, at], iota_p1[:, 0:1],
                                        ALU.is_equal, ALU.mult)
                        ins = v.tensor_scalar(hot_blk[:, s, k, 1, :], iota_b[:, :], blk_f[:, at], tk_f[:, at],
                                              ALU.is_equal, ALU.mult)
                    ins.then_inc(hot_ready, 1)
            dve.wait_ge(bexp_ps, 1)
            v.tensor_copy(exp_row[:, :], bank[3][0:1, 0:2 * P]).then_inc(exp_ready, 1)
            dve.wait_ge(table_ps, 1)
            v.tensor_scalar(used[:, :], bank[2][:, 0:NBLK], 0.0, None, ALU.is_gt)
            v.tensor_scalar(src_tok[:, :], bank[2][:, 0:NBLK], 1.0, float(T), ALU.subtract, ALU.mult)
            step(v.tensor_copy(part_i[:, 0, :], bank[2][:, NBLK:2 * NBLK]))
            v.tensor_scalar(part_i[:, 1, :], part_i[:, 0, :], 5, 12, ALU.logical_shift_right, ALU.logical_shift_left)
            step(v.tensor_scalar(part_i[:, 0, :], part_i[:, 0, :], T - 1, None, ALU.bitwise_and))
            step(v.tensor_copy(part_f[:, :, :], part_i[:, :, :]))
            step(v.tensor_tensor(out=src_tok[:, :], in0=src_tok[:, :], in1=part_f[:, 0, :], op=ALU.add))
            step(v.tensor_tensor(out=part_f[:, 1, :], in0=src_tok[:, :], in1=part_f[:, 1, :], op=ALU.add))
            step(v.tensor_tensor(out=part_f[:, 1, :], in0=part_f[:, 1, :], in1=iota_d[:, :], op=ALU.subtract))
            step(v.tensor_tensor(out=part_f[:, 1, :], in0=part_f[:, 1, :], in1=used[:, :], op=ALU.mult))
            step(v.tensor_tensor(out=idx_dst[:, :], in0=part_f[:, 1, :], in1=iota_d[:, :], op=ALU.add))
            v.tensor_scalar(idx_src[:, :], src_tok[:, :], 0.0, None, ALU.max).then_inc(idx_ready, 1)
            dve.wait_ge(lexp, 1)
            step(normalise_rows(gate[:, :, :], gsum[:, :]))

            def bias(g, s, e):
                dve.wait_ge(up_ps, nth(g, s) + 1)
                v.tensor_tensor(out=hb[:, slot(s), :], in0=bank[2 + slot(s)][:, :], in1=e, op=ALU.add)\
                 .then_inc(hb_ready, 1)

            def hT_copy(g, s):
                dve.wait_ge(hT_ps, nth(g, s) + 1)
                v.tensor_copy(hT[:, slot(s), :], bank[4 + slot(s)][:, :]).then_inc(hT_ready, 1)

            def dve_group(g):
                e = experts(dve, g)
                for s in range(BG):
                    bias(g, s, b1_row[:, bass.ds(e[s], 1), :].rearrange("p a f -> p (a f)"))
                    if precedes(g, s - 1):
                        hT_copy(g, s - 1)

            dve.wait_ge(b1_in, 16)
            dve.wait_ge(exp_ready, 1)
            group_loop(dve, dve_group)
            hT_copy(GROUPS, -1)
            for c in range(T // CT):
                dve.wait_ge(yk_in[c % 2], 16 * (c // 2 + 1))
                for k in range(TOPK):
                    for t in range(CT):
                        tile = c * CT + t
                        src = yk[:, c % 2, k, t * D:(t + 1) * D]
                        if k == 0:
                            ins = v.tensor_scalar(value[:, tile, :], src, gate[:, tile, 0:1], None, ALU.mult)
                        else:
                            ins = v.scalar_tensor_tensor(out=value[:, tile, :], in0=src, scalar=gate[:, tile, k:k + 1],
                                                         in1=value[:, tile, :], op0=ALU.mult, op1=ALU.add)
                    if k == TOPK - 1:
                        ins.then_inc(yk_used[c % 2], 1)
                        dve.wait_ge(yk_used[c % 2], c // 2 + 1)
                    else:
                        step(ins)
            row_stats(value, range(T), stat_ready)
            dve.wait_ge(std_ready, B + 3)
            step(v.reciprocal(rstd[:, :], std[:, :]))
            for b in range(B):
                for t in batch(b):
                    ins = v.tensor_scalar(value[:, t, :], value[:, t, :], mv[:, t, 0:1], rstd[:, t:t + 1],
                                          ALU.subtract, ALU.mult)
                step(ins)
                sl = slice(b * NT, (b + 1) * NT)
                v.tensor_tensor(out=x[:, sl, :], in0=x[:, sl, :], in1=value[:, sl, :], op=ALU.add)\
                 .then_inc(out_ready, 1)

        @block.tensor
        def _(pe):
            mm = nc.tensor.matmul

            def transposes(dst, src, n, width=P):
                for t in range(n):
                    ins = nc.tensor.transpose(dst(t), src(t), ident[:, :])
                return ins

            pe.wait_ge(const_ready, 1)
            for b in range(B):
                pe.wait_ge(xn_ready, b + 1)
                if b >= 2:
                    pe.wait_ge(xnT_ready, b - 1)
                transposes(lambda t: bank[b % 2][:, tok(t)], lambda t: xn[:, b * NT + t, :], NT).then_inc(xnT_ps, 1)
                if b == 0:
                    pe.wait_ge(wv_in, 32)
                pe.wait_ge(xnT_ready, b + 1)
                if b >= 2:
                    pe.wait_ge(val_ready, b - 1)
                for t in range(NT):
                    ins = mm(bank[2 + b % 2][:, tok(t)], xnT[:, tok(b * NT + t)], wv_sb[:, :], start=True, stop=True)
                ins.then_inc(val_ps, 1)
            pe.wait_ge(val_ready, B)
            pe.wait_ge(colT_need, 1)
            nc.tensor.transpose(bank[3][:, 0:P], idx_f[:, 1, :], ident[:, :]).then_inc(colT_ps, 1)
            pe.wait_ge(band_in, 16)
            for c, w in enumerate(BAND_CUTS):
                mm(bank[4 + c][:, 0:w], flip[:, :], band_up[:, :, :].rearrange("p h m -> p (h m)")[:, c * N:c * N + w],
                   start=True, stop=True).then_inc(band_ps, 1)
            pe.wait_ge(wqkv_in, 16)
            pe.wait_ge(band_ready, len(BAND_CUTS))
            for t in range(NT):
                mm(bank[4 + t][:, :], xnT[:, tok(t)], wqkv_sb[:, 2 * H * DH:3 * H * DH], start=True, stop=True)\
                    .then_inc(v_ps, 1)
            pe.wait_ge(xl_ready, B)
            for c in range(4):
                if c == 3:
                    pe.wait_ge(colT_ready, 1)
                for h in (2 * c, 2 * c + 1):
                    ins = mm(bank[c][0:DH, (h % 2) * 256:(h % 2) * 256 + B * L], wqkv_sb[:, h * DH:(h + 1) * DH],
                             xlT[:, :], start=True, stop=True)
                ins.then_inc(ql_ps, 1)
            for c in range(4):
                pe.wait_ge(ql_ready, c + 1)
                for h in (2 * c, 2 * c + 1):
                    ins = mm(bank[c][0:DH, (h % 2) * 256:(h % 2) * 256 + B * L],
                             wqkv_sb[:, (H + h) * DH:(H + h + 1) * DH], xlT[:, :], start=True, stop=True)
                ins.then_inc(kl_ps, 1)
            pe.wait_ge(wt_in, 32)
            pe.wait_ge(kl_ready, 4)
            for h in range(H):
                ins = mm(bank[1][:, h * L:(h + 1) * L], wqT_sb[:, h, :], klT[:, h, 0:L], start=True, stop=True)
            ins.then_inc(r_ps, 1)
            for h in range(H):
                ins = mm(bank[2][:, h * L:(h + 1) * L], wkT_sb[:, h, :], qlT[:, h, 0:L], start=True, stop=True)
            ins.then_inc(r_ps, 1)
            for b in range(B):
                for h in range(H):
                    col = (b * G2 + h // HG) * L
                    ins = mm(bank[0][(h % HG) * L:(h % HG + 1) * L, col:col + L], qlT[:, h, b * L:(b + 1) * L],
                             klT[:, h, b * L:(b + 1) * L], start=True, stop=True)
            ins.then_inc(a2_ps, 1)
            pe.wait_ge(r3_ready, 1)
            for g in range(G2):
                mm(bank[3 - g][:, :], r3[:, g * P:(g + 1) * P], xnT[:, 0:N], start=True, stop=True)\
                    .then_inc(s3_ps, 1)
            pe.wait_ge(r1_ready, 1)
            pe.wait_ge(a2_shift, 1)
            for t in range(NT):
                ins = mm(bank[1 - t // 2][:, (t % 2) * 256:(t % 2) * 256 + H * L], xnT[:, tok(t)], r1[:, :],
                         start=True, stop=True)
            ins.then_inc(s1_ps, 1)
            pe.wait_ge(v_ready, NT)

            def conv(c):
                for h in (2 * c, 2 * c + 1):
                    lo = (h % 2) * DH
                    for o in range(NT):
                        ins = mm(bank[4 + c][lo:lo + DH, tok(o)], v_sb[:, o, h * DH:(h + 1) * DH],
                                 band[:, h, HALO:HALO + P], start=(o == 0), stop=False, skip_group_check=True)
                    for o in range(NT):
                        if o > 0:
                            ins = mm(bank[4 + c][lo:lo + DH, o * P:o * P + HALO], v_sb[:, o - 1, h * DH:(h + 1) * DH],
                                     band[:, h, HALO + P:WIN], start=False, stop=False, skip_group_check=True)
                        if o < NT - 1:
                            ins = mm(bank[4 + c][lo:lo + DH, (o + 1) * P - HALO:(o + 1) * P],
                                     v_sb[:, o + 1, h * DH:(h + 1) * DH],
                                     band[:, h, 0:HALO], start=False, stop=False, skip_group_check=True)

            for c in range(3):
                conv(c)
            pe.wait_ge(xbd_ready, 1)
            pe.wait_ge(const_ready, 2)
            pe.wait_ge(s1_shift, 1)
            mm(bank[0][:, :], blk_j[:, :, :].rearrange("p h j -> p (h j)"), a2[:, :, :].rearrange("p a j -> p (a j)"), start=True, stop=True)
            transposes(lambda g: bank[7][:, tok(g)], lambda g: xbd[:, g, :], G2).then_inc(xT_ps, 1)
            for g in range(G2):
                pe.wait_ge(p3_ready, g + 1)
                transposes(lambda t: bank[3 - g][:, tok(t)], lambda t: p3[:, g, tok(t)], NT).then_inc(p3T_ps, 1)
            pe.wait_ge(max_ready, 1)
            pe.wait_ge(xT_ready, 1)
            mm(bank[7][0:1, 0:P], mx2[:, 0:1], ident[:, :], start=True, stop=True)
            mm(bank[7][0:1, P:2 * P], mx2[:, 1:2], ident[:, :], start=True, stop=True).then_inc(max_ps, 1)
            pe.wait_ge(p1_ready, 1)
            for g in range(G2):
                transposes(lambda t: bank[1 - g][:, tok(t)],
                           lambda t: p1[:, t * H + g * HG:t * H + (g + 1) * HG, :].rearrange("p h j -> p (h j)"), NT)\
                    .then_inc(p1T_ps, 1)
            pe.wait_ge(sinv_row, 1)
            mm(bank[7][:, 0:1], ones[0:1, :], srow[0:1, 3:4], start=True, stop=True).then_inc(sinv_ps, 1)
            pe.wait_ge(p3T_ready, 2)
            for g in range(G2):
                for t in range(NT):
                    ins = mm(bank[3][:, g * 256:(g + 1) * 256], p3T[:, g, t, :],
                             v_sb[:, t, g * 256:(g + 1) * 256], start=(t == 0), stop=(t == NT - 1))
            ins.then_inc(a3v_ps, 1)
            pe.wait_ge(z_ready, 1)
            conv(3)
            pe.wait_ge(a3v_ready, 1)
            with pe.Fori(0, PINV) as i:
                pe.wait_ge(z_ready, i + 1)
                pe.wait_ge(zT_ready, i + 1)
                for g in range(G2):
                    ins = mm(bank[2][:, tok(g)], xT[:, g, :], z[:, g, :], start=True, stop=True)
                ins.then_inc(pz_ps, 1)
                for g in range(G2):
                    ins = mm(bank[3][:, tok(g)], z[:, g, :], xT[:, g, :], start=True, stop=True)
                ins.then_inc(pz_ps, 1)
                pe.wait_ge(pzT_ready, i + 1)
                for n in range(2):
                    pe.wait_ge(t_ready, 3 * i + n + 1)
                    for g in range(G2):
                        ins = mm(bank[2 + n][:, tok(g)], pzT[:, g, :], tz[:, g, :], start=True, stop=True)
                    ins.then_inc(tz_ps, 1)
                pe.wait_ge(t_ready, 3 * i + 3)
                for g in range(G2):
                    ins = mm(bank[2][:, tok(g)], zT[:, g, :], tz[:, g, :], start=True, stop=True)
                ins.then_inc(zn_ps, 1)
                for g in range(G2):
                    ins = mm(bank[3][:, tok(g)], tz[:, g, :], zT[:, g, :], start=True, stop=True)
                ins.then_inc(zn_ps, 1)
            pe.wait_ge(zT_ready, PINV + 1)
            pe.wait_ge(z_ready, PINV + 1)
            for g in range(G2):
                ins = mm(bank[2][:, g * 256:(g + 1) * 256], zT[:, g, :], a3v[:, g, :], start=True, stop=True)
            ins.then_inc(m_ps, 1)
            pe.wait_ge(p1T_ready, 2)
            pe.wait_ge(m_ready, 1)
            for c in range(4):
                mm(bank[4 + c][:, :], m_bd[:, c // 2, (c % 2) * P:(c % 2 + 1) * P], p1T[:, c // 2, :],
                   start=False, stop=True, skip_group_check=True).then_inc(outT_ps, 1)
            pe.wait_ge(outw_in, 32)
            pe.wait_ge(outT_ready, 4)
            for t in range(NT):
                for c in range(4):
                    ins = mm(bank[0][:, tok(t)], outT[:, c, tok(t)], outw_sb[:, c, :], start=(c == 0), stop=(c == 3))
            ins.then_inc(xg_ps, 1)
            pe.wait_ge(enc0_ready, 1)
            transposes(lambda t: bank[1][:, tok(t)], lambda t: xn[:, t, :], NT).then_inc(encT_ps, 1)
            pe.wait_ge(qk_in, 64)
            pe.wait_ge(encT_ready, 1)
            for t in range(NT):
                ins = mm(bank[3][:, t * QK:(t + 1) * QK], encT[:, tok(t)], wk_sb[:, :], start=True, stop=True)
            ins.then_inc(k_ps, 1)
            mm(bank[2][0:NS * QK, :], wq3_sb[:, :, :].rearrange("p s q -> p (s q)"), encT[:, :], start=True,
               stop=True).then_inc(q_ps, 1)
            pe.sem_inc(kg_ps, 2)
            pe.sem_inc(g_done, 2)
            pe.wait_ge(ksp_ready, 1)
            mm(bank[4][0:NS * QK, :], zeros[:, 0:NS * QK], zeros[:, :], start=True, stop=False, skip_group_check=True)

            def gather(pair, s):
                pe.wait_ge(ohc_ready, 2 * pair + s + 1)
                pe.wait_ge(kv_ready, 2 * pair + s + 1)
                for j in range(EG):
                    for c in range(NT):
                        for n in range(NS):
                            ins = mm(bank[s][:, j * QK:(j + 1) * QK], oh_c[:, s, c, j * P:(j + 1) * P],
                                     ksp[:, c, n, :], start=(c == 0 and n == 0), stop=(c == NT - 1 and n == NS - 1))
                ins.then_inc(kg_ps, 1)

            def segment(pair, s):
                pe.wait_ge(ohr_ready, 2 * pair + s + 1)
                pe.wait_ge(kvs_ready, 2 * pair + s + 1)
                for j in range(EG):
                    ins = mm(bank[4][0:NS * QK, :], kvs[:, s, j, :, :].rearrange("p n q -> p (n q)"),
                             oh_r[:, s, j, :], start=False, stop=False, skip_group_check=True)
                ins.then_inc(g_done, 1)

            with pe.Fori(0, NG // 2) as pair:
                gather(pair, 0)
                gather(pair, 1)
                segment(pair, 0)
                segment(pair, 1)
            mm(bank[4][0:NS * QK, :], zeros[:, 0:NS * QK], zeros[:, :], start=False, stop=True,
               skip_group_check=True).then_inc(g_ps, 1)
            pe.wait_ge(prod_ready, 1)
            mm(bank[5][0:1, :], ones[0:NS * QK, 0:1], prod[:, :], start=True, stop=True).then_inc(arow_ps, 1)
            pe.wait_ge(arow_ready, 1)
            for t in range(NT):
                ins = mm(bank[6][:, t:t + 1], arow[0:1, tok(t)], ones[0:1, 0:1], start=True, stop=True)
            ins.then_inc(alpha_ps, 1)

            for b in range(B):
                pe.wait_ge(xn_ready, B + b + 1)
                if b >= 2:
                    pe.wait_ge(xnT_ready, B + b - 1)
                transposes(lambda t: bank[b % 2][:, tok(t)], lambda t: xn[:, b * NT + t, :], NT).then_inc(xnT_ps, 1)
            pe.wait_ge(comb_ready, 1)
            mm(bank[5][:, 0:E], ones[:, :], ksq[:, :], start=True, stop=True).then_inc(ksq_ps, 1)
            pe.wait_ge(xnT_ready, 2 * B)
            for t in range(T):
                ins = mm(bank[6][:, t * E:(t + 1) * E], xnT[:, tok(t)], comb[:, :], start=True, stop=True)
            ins.then_inc(logit_ps, 1)
            pe.wait_ge(chosen_ready, 1)
            pe.wait_ge(const_ready, 3)
            flat = chosen_b[:, :, :].rearrange("p t e -> p (t e)")
            mm(bank[0][:, :], upper[:, :], flat, start=True, stop=True).then_inc(prefix_ps, 1)
            mm(bank[1][:, :], ones_b[:, :], flat, start=True, stop=True).then_inc(prefix_ps, 1)
            pe.wait_ge(bexp_ready, 1)
            for c in range(2):
                ins = mm(bank[3][0:1, tok(c)], blk_exp[:, c:c + 1], ident[:, :], start=True, stop=True)
            ins.then_inc(bexp_ps, 1)
            mm(bank[2][:, 0:2 * NBLK], zeros[:, 0:P], zeros[:, 0:2 * NBLK], start=True, stop=False,
               skip_group_check=True)
            with pe.Fori(0, T // 2) as i:
                for s in range(2):
                    pe.wait_ge(hot_ready, 2 * i + s + 1)
                    for k in range(TOPK):
                        ins = mm(bank[2][:, 0:2 * NBLK], hot_lane[:, s, k, :],
                                 hot_blk[:, s, k, :, :].rearrange("p a b -> p (a b)"), start=False, stop=False,
                                 skip_group_check=True)
                    ins.then_inc(hot_used, 1)
            mm(bank[2][:, 0:2 * NBLK], zeros[:, 0:P], zeros[:, 0:2 * NBLK], start=False, stop=True,
               skip_group_check=True).then_inc(table_ps, 1)

            def rows_T(g, s):
                pe.wait_ge(xg_in[s % 4], 16 * (g + s // 4 + 1))
                freed(pe, xgT_ready, nth(g, s) - 1)
                nc.tensor.transpose(bank[slot(s)][:, 0:P], xg[:, s % 4, :], ident[:, :])\
                    .then_inc(xgT_ps, 1)

            def up(g, s, e):
                pe.wait_ge(xgT_ready, nth(g, s) + 1)
                freed(pe, hb_ready, nth(g, s) - 1)
                mm(bank[2 + slot(s)][:, :], xgT[:, slot(s), :], w1_sb[:, bass.ds(e, 1), :]
                   .rearrange("p a f -> p (a f)"), start=True, stop=True).then_inc(up_ps, 1)

            def hidden_T(g, s):
                pe.wait_ge(h_ready, nth(g, s) + 1)
                freed(pe, hT_ready, nth(g, s) - 1)
                transposes(lambda c: bank[4 + slot(s)][:, tok(c)], lambda c: hg[:, slot(s), tok(c)], FC)\
                    .then_inc(hT_ps, 1)

            def down(g, s, e):
                pe.wait_ge(hT_ready, nth(g, s) + 1)
                freed(pe, y_ready, nth(g, s) - 1)
                for c in range(FC):
                    mm(bank[6 + slot(s)][:, 0:D], hT[:, slot(s), tok(c)], w2_sb[:, bass.ds(e, 1), c, :]
                       .rearrange("p a d -> p (a d)"), start=(c == 0), stop=False)
                mm(bank[6 + slot(s)][:, 0:D], ones_b[0:NS, :], b2_parts[:, bass.ds(e, 1), :]
                   .rearrange("p a d -> p (a d)"), start=False, stop=True).then_inc(down_ps, 1)

            def pe_group(g):
                now = experts(pe, g)
                before = experts(pe, g - 1) if precedes(g, -1) else None
                for s in range(BG):
                    up(g, s, now[s])
                    if precedes(g, s - 2):
                        down(g, s - 2, now[s - 2] if s >= 2 else before[s + 2])
                    if precedes(g, s - 1):
                        hidden_T(g, s - 1)
                    if follows(g, s + 2):
                        rows_T(g, s + 2)

            pe.wait_ge(exp_ready, 1)
            pe.wait_ge(w_in, 32)
            pe.wait_ge(b2p_in, 16)
            rows_T(0, 0)
            rows_T(0, 1)
            group_loop(pe, pe_group)
            last = experts(pe, GROUPS - 1)
            hidden_T(GROUPS, -1)
            for s in (-2, -1):
                down(GROUPS, s, last[s + BG])


def kernel(**inputs):
    import numpy as np
    import concourse.bacc as bacc
    from concourse.bass_utils import run_bass_kernel_spmd

    a = {k.split("_", 2)[2]: np.asarray(v) for k, v in inputs.items()}
    E, F, D = a["w1"].shape
    P, DH = 128, 64
    H = a["qkv_w"].shape[1] // (3 * DH)
    taps = a["conv_w"].reshape(H, -1)
    K = taps.shape[1]
    conv_pad = np.zeros((H, 2 * P - 2 + K), taps.dtype)
    conv_pad[:, P - 1:P - 1 + K] = taps[:, ::-1]

    def heads(w):
        return w.reshape(D, H, DH).transpose(2, 1, 0)

    arrays = dict(
        dense=a["dense"], adj_rows=a["adj_rows"], adj_cols=a["adj_cols"], adj_vals=a["adj_vals"], wq=a["wq"],
        wk=a["wk"], wv_w=a["wv_w"], wv_b=a["wv_b"], qkv_w=a["qkv_w"], wq_t=heads(a["qkv_w"][:, :H * DH]),
        wk_t=heads(a["qkv_w"][:, H * DH:2 * H * DH]), out_w=a["out_w"], out_b=a["out_b"], conv_pad=conv_pad,
        keys_t=a["keys"].T, w1_t=a["w1"].transpose(2, 0, 1), b1=a["b1"],
        w2_t=a["w2"].reshape(E, D, F // P, P).transpose(3, 0, 2, 1), b2=a["b2"], rw_t=a["rw"].T, rb=a["rb"])
    arrays = {k: np.ascontiguousarray(v) for k, v in arrays.items()}
    nc = bacc.Bacc("TRN2", target_bir_lowering=False, num_devices=1)
    args = {k: nc.dram_tensor(f"in_{k}", v.shape, mybir.dt.from_np(v.dtype), kind="ExternalInput").ap()
            for k, v in arrays.items()}
    args["out"] = nc.dram_tensor("out_x", a["dense"].shape, mybir.dt.float32, kind="ExternalOutput").ap()
    sandwich_kernel(nc, **args)
    r = run_bass_kernel_spmd(nc, [{f"in_{k}": v for k, v in arrays.items()}], core_ids=[0])
    return r.results[0]["out_x"]
```

```python
import concourse.bass as bass
from concourse import mybir
from contextlib import ExitStack


def sandwich_kernel(nc, dense, adj_rows, adj_cols, adj_vals, wq, wk, wv_w, wv_b, qkv_w, wq_t, wk_t, out_w, out_b,
                    conv_pad, keys_t, w1_t, b1_t, w2_t, b2, rw_t, rb, out):
    fp32 = mybir.dt.float32
    bf16 = mybir.dt.bfloat16
    fp16 = mybir.dt.float16
    i32 = mybir.dt.int32
    ALU = mybir.AluOpType
    ACT = mybir.ActivationFunctionType
    AX = mybir.AxisListType

    P = 128
    B, N, D = dense.shape
    NT = N // P
    T = B * NT
    H, DH, L = 8, 64, 32
    LW = N // L
    HG = P // L
    G2 = H // HG
    PINV = 6
    KC = 33
    HALO = KC // 2
    WIN = P + 2 * HALO
    BAND_CUTS = [min(N, H * WIN - c) for c in range(0, H * WIN, N)]
    EDGES = adj_rows.shape[0]
    EC = EDGES // P
    EG = 8
    NG = EC // EG
    QK = wq.shape[1]
    NS = 3
    E, TOPK = keys_t.shape[1], 4
    F = w1_t.shape[2]
    FC = F // P
    EPS = 1e-5
    NBLK = -(-(T * P * TOPK + E * (P - 1)) // P // 8) * 8
    BG = 8
    RING = 8
    DUMP = T * P * TOPK

    ctx = ExitStack()
    with ctx:
        def sb(name, shape, dt=fp32):
            return ctx.enter_context(nc.sbuf_tensor(name, shape, dt))

        def sem(name):
            return ctx.enter_context(nc.semaphore(name))

        x = sb("x", [P, T, D])
        xn = sb("xn", [P, T, D])
        xnT = sb("xnT", [P, T * P])
        value = sb("value", [P, T, D])
        early = sb("early", [P, 3 * H * DH + 2 * H * D + NT * D + H * WIN + NT * H * DH + G2 * N])
        cursor = [0]

        def of_early(parts, width):
            cursor[0] += width
            return early[0:parts, cursor[0] - width:cursor[0]]

        wqkv_sb = of_early(P, 3 * H * DH)
        wqT_sb = of_early(DH, H * D).rearrange("p (h d) -> p h d", h=H)
        wkT_sb = of_early(DH, H * D).rearrange("p (h d) -> p h d", h=H)
        outw_sb = of_early(P, NT * D).rearrange("p (c d) -> p c d", c=NT)
        band = of_early(P, H * WIN).rearrange("p (h m) -> p h m", h=H)
        v_sb = of_early(P, NT * H * DH).rearrange("p (t n) -> p t n", t=NT)
        p1T = of_early(P, G2 * N).rearrange("p (g n) -> p g n", g=G2)
        wv_sb = sb("wv_sb", [P, D])
        wvb_row = sb("wvb_row", [P, D])
        outb_row = sb("outb_row", [P, D])
        wq_sb = sb("wq_sb", [P, QK])
        wk_sb = sb("wk_sb", [P, QK])
        keysT = sb("keysT", [P, E])
        rwT = sb("rwT", [P, E])
        rb_row = sb("rb_row", [P, E])
        b2_sb = sb("b2_sb", [P, E * D // P])
        b2_res = sb("b2_res", [P, E * D // P])
        b2_cut = sb("b2_cut", [P, NS, E * D // P], bf16)
        b2_parts = sb("b2_parts", [NS, E, D], bf16)
        b2_dram = nc.dram_tensor("b2_dram", [NS, E * D], bf16, kind="Internal").ap()

        ident = sb("ident", [P, P])
        flip = sb("flip", [P, P])
        identw = sb("identw", [P, 3, G2, P])
        blk_j = sb("blk_j", [P, HG, L])
        blk_d = sb("blk_d", [P, HG, DH])
        ones = sb("ones", [P, P])
        eps_c = sb("eps_c", [P, 1])
        zeros = sb("zeros", [P, N], bf16)
        iota_e = sb("iota_e", [P, E])
        iota_c = sb("iota_c", [P, NT])
        iota_r = sb("iota_r", [P, N], fp16)

        stats = sb("stats", [P, T, 6])
        mv = sb("mv", [P, T, 2])
        std = sb("std", [P, T])
        rstd = sb("rstd", [P, T])
        xlT = sb("xlT", [P, B * L])
        EDGE_OC, EDGE_OR = EDGES // 2, EDGES // 2 + NT * EG * P
        WB = F + FC
        shared = sb("shared", [P, max(EDGE_OR + EG * N, E * (WB + FC * D))])
        colb = shared[:, 0:EDGE_OC].bitcast(fp16)
        oh_c = shared[:, EDGE_OC:EDGE_OR].bitcast(bf16).rearrange("p (a c n) -> p a c n", a=2, c=NT)
        oh_r = shared[:, EDGE_OR:EDGE_OR + EG * N].bitcast(bf16).rearrange("p (a j n) -> p a j n", a=2, j=EG)
        qlT = shared[0:DH, EDGE_OR:EDGE_OR + H * B * L].rearrange("p (h n) -> p h n", h=H)
        klT = shared[0:DH, EDGE_OR + H * B * L:EDGE_OR + 2 * H * B * L].rearrange("p (h n) -> p h n", h=H)
        p3 = shared[:, EDGE_OC:EDGE_OC + G2 * N].rearrange("p (g n) -> p g n", g=G2)
        p3T = shared[:, EDGE_OC + G2 * N:EDGE_OC + 2 * G2 * N].rearrange("p (g t n) -> p g t n", g=G2, t=NT)
        p1 = shared[:, EDGE_OC + 2 * G2 * N:EDGE_OC + 3 * G2 * N].rearrange("p (a j) -> p a j", j=L)
        band_up = shared[:, EDGE_OC:EDGE_OC + H * WIN].rearrange("p (h m) -> p h m", h=H)
        outT = shared[:, EDGE_OR:EDGE_OR + NT * N].rearrange("p (c n) -> p c n", c=NT)
        w1_sb = shared[:, 0:E * WB].rearrange("p (e f) -> p e f", e=E)
        w2_sb = shared[:, E * WB:E * (WB + FC * D)].rearrange("p (e c d) -> p e c d", e=E, c=FC)
        xl = xnT[:, 0:2 * B * D].rearrange("p (a b d) -> p a b d", a=2, b=B)
        sg = xnT[:, 2 * B * D:4 * B * D].rearrange("p (a b d) -> p a b d", a=2, b=B)
        TE = T * E
        logits, chosen, pos_e, tmp_e, k0, k1, k2 = [
            xnT[:, i * TE:(i + 1) * TE].rearrange("p (t e) -> p t e", t=T) for i in range(7)]
        top8 = xnT[:, 7 * TE:7 * TE + T * 8].rearrange("p (t k) -> p t k", t=T)
        topi = xnT[:, 7 * TE + T * 8:8 * TE].bitcast(mybir.dt.uint32).rearrange("p (t k) -> p t k", t=T)
        att = sb("att", [P, 7, N])
        a2 = att[:, 0, :].rearrange("p (a j) -> p a j", j=L)
        a2m = sb("a2m", [P, B * G2])
        a2s = sb("a2s", [P, B * G2])
        r1, r3 = att[:, 1, 0:H * L], att[:, 1, H * L:2 * H * L]
        p3m = sb("p3m", [P, G2])
        p3s = sb("p3s", [P, G2])
        p1m = sb("p1m", [P, NT * H])
        p1s = sb("p1s", [P, NT * H])
        a3v = att[:, 2, :].rearrange("p (g n) -> p g n", g=G2)
        m_bd = att[:, 3, :].rearrange("p (g n) -> p g n", g=G2)
        pinv = sb("pinv", [P, 6, G2 * P])
        xbd, xT, z, zT, pzT, tz = [pinv[:, i, :].rearrange("p (g n) -> p g n", g=G2) for i in range(6)]
        mx2 = sb("mx2", [P, 4])
        srow = sb("srow", [1, 4])
        sinv = sb("sinv", [P, 1])
        xgb = att[:, 4, :].rearrange("p (t d) -> p t d", t=NT)
        encT = att[:, 5, :]
        q_tok = att[:, 6, 0:NT * QK].rearrange("p (t q) -> p t q", t=NT)
        araw = sb("araw", [P, NT])
        kf = sb("kf", [P, NT, QK])
        kres = sb("kres", [P, NT, QK])
        ksp = sb("ksp", [P, NT, NS, QK], bf16)

        idx_i = sb("idx_i", [P, 2, EC], i32)
        idx_f = sb("idx_f", [P, 2, EC])
        neg = sb("neg", [P, EC])
        vals = sb("vals", [P, EC])
        colT = sb("colT", [P, EC], fp16)
        col_dram = nc.dram_tensor("col_dram", [EDGES], fp16, kind="Internal").ap()
        kv, kvr = [xnT[:, i * N:(i + 1) * N].rearrange("p (a j q) -> p a j q", a=2, j=EG) for i in range(2)]
        kvs = xnT[:, 2 * N:2 * N + EG * NS * QK].bitcast(bf16).rearrange("p (a j n q) -> p a j n q", a=2, j=EG, n=NS)
        prod = xnT[:, 4 * N:4 * N + NT * NS * QK].rearrange("p (t n q) -> p t n q", t=NT, n=NS)
        arow = xnT[0:1, 5 * N:6 * N]
        asc = sb("asc", [1, 4])
        alpha = sb("alpha", [P, NT])
        nalpha = sb("nalpha", [P, NT])
        shift = sb("shift", [P, T])
        nmr = sb("nmr", [P, T])
        csum = sb("csum", [P, E])

        attf = att[:, :, :].rearrange("p a n -> p (a n)")
        taken = [0]

        def of_att(width):
            taken[0] += width
            return attf[:, taken[0] - width:taken[0]]

        k3 = of_att(TE).rearrange("p (t e) -> p t e", t=T)
        chosen_b = of_att(TE // 2).bitcast(bf16).rearrange("p (t e) -> p t e", t=T)
        pos, lane, blk, pos_i, lane_i = [of_att(T * TOPK).rearrange("p (t k) -> p t k", t=T) for _ in range(5)]
        pos_i, lane_i = pos_i.bitcast(i32), lane_i.bitcast(i32)
        src_tok, used = of_att(NBLK), of_att(NBLK)
        part_i, part_f = [of_att(2 * NBLK).rearrange("p (a n) -> p a n", a=2) for _ in range(2)]
        part_i = part_i.bitcast(i32)
        x2n = sb("x2n", [P, T])
        comb = sb("comb", [P, E])
        ksq = sb("ksq", [P, E])
        lbias = sb("lbias", [P, E])
        upper = sb("upper", [P, P], bf16)
        ones_b = sb("ones_b", [P, P], bf16)
        tot, cum = [pinv[:, 2 * i:2 * i + 2, :].rearrange("p a n -> p (a n)").rearrange("p (e t) -> p e t", e=E)
                    for i in range(2)]
        zero_r = pinv[:, 4:6, :].rearrange("p a n -> p (a n)")
        cnt = sb("cnt", [P, E])
        cnt_i = sb("cnt_i", [P, E], i32)
        pbase = sb("pbase", [P, E])
        pend = sb("pend", [P, E])
        token_of = sb("token_of", [P, T, TOPK, 2], bf16)
        iota_b = sb("iota_b", [P, NBLK], fp16)
        iota_b2 = sb("iota_b2", [P, 2])
        iota_d = sb("iota_d", [P, NBLK])
        blk_cmp = sb("blk_cmp", [P, 2, E])
        blk_exp = sb("blk_exp", [P, 2])
        exp_row = sb("exp_row", [1, 2 * P], i32)
        idx_src, idx_dst = [of_att(NBLK).bitcast(mybir.dt.uint32) for _ in range(2)]
        xd = nc.dram_tensor("xd", [P * T, D], fp32, kind="Internal").ap()
        yd = nc.dram_tensor("yd", [DUMP + NBLK * P, D], fp32, kind="Internal").ap()
        xnf = xn[:, :, :].rearrange("p t d -> p (t d)")
        hot_blk = xnf[:, 0:2 * TOPK * NBLK].rearrange("p (a k n) -> p a k n", a=2, k=TOPK)
        VK = 2
        hot_lane = early[:, 0:T * TOPK * P // 2].bitcast(bf16).rearrange("p (t k n) -> p t k n", t=T, k=TOPK)
        xg = xnf[:, 0:RING * D].rearrange("p (a d) -> p a d", a=RING)
        yg = xnf[:, RING * D:2 * RING * D].rearrange("p (a d) -> p a d", a=RING)
        vf = value[:, :, :].rearrange("p t d -> p (t d)")
        xgT = vf[:, 0:2 * D].rearrange("p (a d) -> p a d", a=2)
        hT = vf[:, 2 * D:2 * D + 2 * F].rearrange("p (a f) -> p a f", a=2)
        w1_now = vf[:, 2 * D + 2 * F:2 * D + 2 * F + 2 * WB].rearrange("p (a f) -> p a f", a=2)
        yk = shared[:, 0:TOPK * T * D].rearrange("p (k n) -> p k n", k=TOPK)
        YCUTS = [0, 2, 4, 8, 16, 24, T]
        YPOOL = 4
        khot = [k0, k1, k2, k3]
        gate, topf = [idx_f[:, a, :].rearrange("p (t k) -> p t k", t=T) for a in range(2)]
        gsum = p1m

        bank = [ctx.enter_context(nc.psum_tensor(f"bank{i}", [P, 512], fp32)) for i in range(8)]

        x_in = [sem(f"x_in{i}") for i in range(4)]
        wv_in, wqkv_in, wt_in, encw_in, band_in = [sem(s) for s in (
            "wv_in", "wqkv_in", "wt_in", "encw_in", "band_in")]
        edge_in, colw_done, colb_in, ffnc_in = [sem(s) for s in ("edge_in", "colw_done", "colb_in", "ffnc_in")]
        w_in, b2_cut_ready, b2w_done, b2p_in = [sem(s) for s in (
            "w_in", "b2_cut_ready", "b2w_done", "b2p_in")]
        const_step, const_ready = sem("const_step"), sem("const_ready")
        dve_step, act_step = sem("dve_step"), sem("act_step")
        stat_ready, std_ready, xn_ready, xnT_ps, xnT_ready, val_ps, val_ready, xl_ready = [sem(s) for s in (
            "stat_ready", "std_ready", "xn_ready", "xnT_ps", "xnT_ready", "val_ps", "val_ready", "xl_ready")]
        ql_ps, ql_ready, kl_ps, kl_ready, v_ps, v_ready = [sem(s) for s in (
            "ql_ps", "ql_ready", "kl_ps", "kl_ready", "v_ps", "v_ready")]
        a2_ps, a2_shift, a2_exp, a2_ready = [sem(s) for s in ("a2_ps", "a2_shift", "a2_exp", "a2_ready")]
        r_ps, r1_ready, r3_ready, s3_ps, s3_max, p3_ready, p3T_ps, p3T_ready, a3v_ps, a3v_ready = [sem(s) for s in (
            "r_ps", "r1_ready", "r3_ready", "s3_ps", "s3_max", "p3_ready", "p3T_ps", "p3T_ready", "a3v_ps", "a3v_ready")]
        s1_ps, s1_shift, s1_exp, p1_ready, p1T_ps, p1T_ready = [sem(s) for s in (
            "s1_ps", "s1_shift", "s1_exp", "p1_ready", "p1T_ps", "p1T_ready")]
        xT_ready = sem("xT_ready")
        band_ps, band_ready = sem("band_ps"), sem("band_ready")
        xbd_ready, xT_ps, max_ready, max_ps, sinv_row, sinv_ps = [sem(s) for s in (
            "xbd_ready", "xT_ps", "max_ready", "max_ps", "sinv_row", "sinv_ps")]
        pz_ps, t_ready, pzT_ready, tz_ps, zn_ps, z_ready, zT_ready = [sem(s) for s in (
            "pz_ps", "t_ready", "pzT_ready", "tz_ps", "zn_ps", "z_ready", "zT_ready")]
        m_ps, m_ready, outT_ps, outT_ready, xg_ps, enc0_ready, enc_ready = [sem(s) for s in (
            "m_ps", "m_ready", "outT_ps", "outT_ready", "xg_ps", "enc0_ready", "enc_ready")]
        encT_ps, encT_ready, q_ps, q_ready, k_ps, ksp_ready = [sem(s) for s in (
            "encT_ps", "encT_ready", "q_ps", "q_ready", "k_ps", "ksp_ready")]
        colT_need, colT_ps, colT_ready = [sem(s) for s in ("colT_need", "colT_ps", "colT_ready")]
        ohc_ready, ohr_ready, kg_ps, kv_ready, kvu_ready, kvr_ready, kvs_ready, g_done = [sem(s) for s in (
            "ohc_ready", "ohr_ready", "kg_ps", "kv_ready", "kvu_ready", "kvr_ready", "kvs_ready",
            "g_done")]
        g_ps, araw_ready, arow_ps, amax_ready, aexp_ready, arow_ready, alpha_ps = [sem(s) for s in (
            "g_ps", "araw_ready", "arow_ps", "amax_ready", "aexp_ready", "arow_ready", "alpha_ps")]
        alpha_ready, gated_done, sw_ready, x2_ready, norm_ready, value_sum = [sem(s) for s in (
            "alpha_ready", "gated_done", "sw_ready", "x2_ready", "norm_ready", "value_sum")]
        comb_ready, ksq_ps, logit_ps, lshift, lexp = [sem(s) for s in (
            "comb_ready", "ksq_ps", "logit_ps", "lshift", "lexp")]
        xd_done, chosen_ready, prefix_ps, bexp_ready, bexp_ps, exp_ready = [sem(s) for s in (
            "xd_done", "chosen_ready", "prefix_ps", "bexp_ready", "bexp_ps", "exp_ready")]
        hot_ready, hot_used = sem("hot_ready"), sem("hot_used")
        lane_ready, hot_lane_ready, table_ps, idx_ready = [sem(s) for s in (
            "lane_ready", "hot_lane_ready", "table_ps", "idx_ready")]
        xg_in, y_out = [[sem(f"{s}{i}") for i in range(RING)] for s in ("xg_in", "y_out")]
        xgT_ps, xgT_ready, w1_ready, up_ps, h_ready, down_ps, y_ready = [sem(s) for s in (
            "xgT_ps", "xgT_ready", "w1_ready", "up_ps", "h_ready", "down_ps", "y_ready")]
        yk_in, pool_sum = [sem(f"yk_in{i}") for i in range(len(YCUTS) - 1)], sem("pool_sum")
        out_ready, out_done = sem("out_ready"), sem("out_done")

        block = ctx.enter_context(nc.Block())

        def tok(t):
            return slice(t * P, (t + 1) * P)

        def loaded(b):
            return min(b, 2 + b // 4)

        def slot(s):
            return s % 2

        def nth(g, s):
            return BG * g + s

        def freed(eng, sem, count):
            if not (isinstance(count, int) and count <= 0):
                eng.wait_ge(sem, count)

        GROUPS = NBLK // BG

        def group_loop(eng, body):
            body(0)
            body(1)
            with eng.Fori(2, GROUPS - 1) as g:
                body(g)
            body(GROUPS - 1)

        def follows(g, s):
            return not isinstance(g, int) or BG * g + s < NBLK

        def precedes(g, s):
            return not isinstance(g, int) or BG * g + s >= 0

        def experts(eng, first, n=BG):
            _, e = nc.values_load_multi_w_load_instructions(
                exp_row[0:1, bass.ds(first, n)], engines=[eng.engine], min_val=0, max_val=E - 1,
                skip_runtime_bounds_check_because="the row is clamped to 0..E-1 when it is made")
            return e

        def over_b(ap, t):
            return ap[:, :, :].rearrange("p (b t) d -> p t b d", t=NT)[:, t, :, :]

        def of_vector(c):
            n = YCUTS[c + 1] - YCUTS[c]
            return YCUTS[c], YCUTS[c + 1] - n // YPOOL

        def of_pool(c):
            return of_vector(c)[1], YCUTS[c + 1]

        @block.sync
        def _(sp):
            for b, e in ((0, 1), (1, 2), (2, 4), (4, B)):
                sp.dma_start(x[:, b * NT:e * NT, :],
                             dense[b:e, :, :].rearrange("b (t p) d -> p (b t) d", p=P)).then_inc(x_in[loaded(b)], 16)
                if b == 0:
                    sp.dma_start(wv_sb[:, :], wv_w).then_inc(wv_in, 16)
                    sp.dma_start(wvb_row[:, :], wv_b.rearrange("(a d) -> a d", a=1).broadcast_to([P, D]))\
                      .then_inc(wv_in, 16)
            sp.dma_start(b2_sb[:, :], b2.rearrange("e (c n) -> (e c) n", c=P // E))\
              .then_inc(ffnc_in, 16)
            sp.dma_start(keysT[:, :], keys_t).then_inc(ffnc_in, 16)
            sp.dma_start(rwT[:, :], rw_t).then_inc(ffnc_in, 16)
            sp.dma_start(rb_row[:, :], rb.rearrange("(a d) -> a d", a=1).broadcast_to([P, E])).then_inc(ffnc_in, 16)
            sp.wait_ge(colT_ready, 1)
            sp.dma_start(col_dram.rearrange("(c e) -> c e", e=P), colT[:, :]).then_inc(colw_done, 16)
            sp.wait_ge(colw_done, 16)
            sp.dma_start(colb[:, :], col_dram.rearrange("(a e) -> a e", a=1).broadcast_to([P, EDGES]))\
              .then_inc(colb_in, 16)
            sp.wait_ge(b2_cut_ready, 1)
            sp.dma_start(b2_dram.rearrange("s (p n) -> p s n", p=P), b2_cut[:, :, :]).then_inc(b2w_done, 16)
            sp.wait_ge(b2w_done, 16)
            sp.dma_start(b2_parts[:, :, :].rearrange("s e d -> s (e d)"), b2_dram).then_inc(b2p_in, 16)
            sp.wait_ge(g_ps, 1)
            sp.dma_start(w1_sb[:, :, 0:F], w1_t).then_inc(w_in, 16)
            sp.dma_start(w1_sb[:, :, F:WB], b1_t).then_inc(w_in, 16)
            sp.dma_start(w2_sb, w2_t).then_inc(w_in, 16)
            for b in range(B):
                sp.wait_ge(xn_ready, B + b + 1)
                sp.dma_start(xd.rearrange("(p t) d -> p t d", p=P)[:, b * NT:(b + 1) * NT, :],
                             xn[:, b * NT:(b + 1) * NT, :]).then_inc(xd_done, 16)
            for s in range(RING):
                sp.wait_ge(y_out[s], 16 * NBLK // RING)
            for c, (t, e) in enumerate(zip(YCUTS, YCUTS[1:])):
                sp.dma_start(yk[:, :, t * D:e * D], yd[0:DUMP, :].rearrange("(k p t) d -> p k (t d)", k=TOPK, p=P)
                             [:, :, t * D:e * D]).then_inc(yk_in[c], 16)
            for b in range(B):
                sp.wait_ge(out_ready, b + 1)
                sp.dma_start(out[b, :, :].rearrange("(t p) d -> p t d", p=P), x[:, b * NT:(b + 1) * NT, :])\
                  .then_inc(out_done, 16)
            sp.wait_ge(out_done, 16 * B)

        @block.gpsimd
        def _(pool):
            steps = [0]

            def step(ins):
                steps[0] += 1
                ins.then_inc(const_step, 1)
                pool.wait_ge(const_step, steps[0])

            step(pool.memset(ident[:, :], 0.0))
            step(pool.affine_select(out=ident[:, :], in_=ident[:, :], compare_op=ALU.not_equal, fill=1.0,
                                    base=0, pattern=[[-1, P]], channel_multiplier=1))
            step(pool.memset(flip[:, :], 0.0))
            pool.affine_select(out=flip[:, :], in_=flip[:, :], compare_op=ALU.not_equal, fill=1.0,
                               base=1 - P, pattern=[[1, P]], channel_multiplier=1)
            pool.memset(eps_c[:, :], EPS)
            pool.memset(zeros[:, :], 0.0)
            pool.iota(iota_e[:, :], pattern=[[1, E]], base=0, channel_multiplier=0,
                      allow_small_or_imprecise_dtypes=True)
            pool.memset(ones[:, :], 1.0).then_inc(const_ready, 1)
            for m, w in ((blk_j, L), (blk_d, DH)):
                step(pool.memset(m[:, :, :], 1.0))
                step(pool.affine_select(out=m[:, :, :], in_=m[:, :, :], compare_op=ALU.is_ge, fill=0.0,
                                        base=0, pattern=[[-L, HG], [0, w]], channel_multiplier=1))
                step(pool.affine_select(out=m[:, :, :], in_=m[:, :, :], compare_op=ALU.is_ge, fill=0.0,
                                        base=L - 1, pattern=[[L, HG], [0, w]], channel_multiplier=-1))
            step(pool.memset(identw[:, :, :, :], 0.0))
            for n, c in enumerate((7.0, 15.0, 13.0)):
                step(pool.affine_select(out=identw[:, n, :, :], in_=identw[:, n, :, :], compare_op=ALU.not_equal,
                                        fill=c, base=0, pattern=[[0, G2], [-1, P]], channel_multiplier=1))
            pool.iota(iota_c[:, :], pattern=[[P, NT]], base=0, channel_multiplier=1,
                      allow_small_or_imprecise_dtypes=True)
            pool.iota(iota_r[:, :], pattern=[[1, N]], base=0, channel_multiplier=0,
                      allow_small_or_imprecise_dtypes=True).then_inc(const_ready, 1)
            step(pool.memset(upper[:, :], 1.0))
            pool.affine_select(out=upper[:, :], in_=upper[:, :], compare_op=ALU.is_gt, fill=0.0, base=0,
                               pattern=[[1, P]], channel_multiplier=-1)
            pool.memset(ones_b[:, :], 1.0)

            def iota(out, pattern, base, mult):
                return pool.iota(out, pattern=pattern, base=base, channel_multiplier=mult,
                                 allow_small_or_imprecise_dtypes=True)

            iota(token_of[:, :, :, 0], [[0, T], [0, TOPK]], 1, 1)
            iota(token_of[:, :, :, 1], [[1, T], [T, TOPK]], 1, 0)
            iota(iota_b[:, :], [[1, NBLK]], 0, 0)
            iota(iota_b2[:, :], [[P, 2]], 0, 1)
            iota(iota_d[:, :], [[P, NBLK]], DUMP, 1).then_inc(const_ready, 1)
            pool.wait_ge(ffnc_in, 64)
            step(pool.tensor_copy(b2_cut[:, 0, :], b2_sb[:, :]))
            step(pool.tensor_tensor(out=b2_res[:, :], in0=b2_sb[:, :], in1=b2_cut[:, 0, :], op=ALU.subtract))
            step(pool.tensor_copy(b2_cut[:, 1, :], b2_res[:, :]))
            pool.tensor_tensor(out=b2_cut[:, 2, :], in0=b2_res[:, :], in1=b2_cut[:, 1, :], op=ALU.subtract)\
                .then_inc(b2_cut_ready, 1)
            pool.wait_ge(enc0_ready, 1)
            for t in range(NT):
                e = over_b(xn, t)[:, 1:B, :]
                last = pool.tensor_tensor(out=e, in0=e, in1=xgb[:, t, :].unsqueeze(1).broadcast_to([P, B - 1, D]),
                                          op=ALU.add)
            last.then_inc(enc_ready, 1)
            pool.wait_ge(lane_ready, 1)
            pool.wait_ge(xg_ps, 1)
            for t in range(T):
                for k in range(VK, TOPK):
                    ins = pool.tensor_scalar(hot_lane[:, t, k, :], iota_r[:, 0:P], lane[:, t, k:k + 1], None,
                                             ALU.is_equal)
                ins.then_inc(hot_lane_ready, 1)
            LEAD = 6
            pool.wait_ge(idx_ready, 1)
            pool.wait_ge(xd_done, 16 * B)
            for j in range(NBLK + LEAD):
                if j < NBLK:
                    if j >= RING:
                        pool.wait_ge(xgT_ps, j - RING + 1)
                    pool.indirect_dma_start(out=xg[:, j % RING, :], out_offset=None, in_=xd[:, :],
                                            in_offset=bass.IndirectOffsetOnAxis(ap=idx_src[:, j:j + 1], axis=0))\
                        .then_inc(xg_in[j % RING], 16)
                i = j - LEAD
                if i >= 0:
                    pool.wait_ge(y_ready, i + 1)
                    pool.indirect_dma_start(out=yd[:, :],
                                            out_offset=bass.IndirectOffsetOnAxis(ap=idx_dst[:, i:i + 1], axis=0),
                                            in_=yg[:, i % RING, :], in_offset=None).then_inc(y_out[i % RING], 16)
            for c in range(len(YCUTS) - 1):
                t0, t1 = of_pool(c)
                if t0 == t1:
                    pool.sem_inc(pool_sum, 1)
                    continue
                pool.wait_ge(yk_in[c], 16)
                for k in range(1, TOPK):
                    term = yk[:, k, t0 * D:t1 * D].rearrange("p (t d) -> p t d", d=D)
                    step(pool.tensor_tensor(out=term, in0=term, in1=gate[:, t0:t1, k:k + 1]
                                            .broadcast_to([P, t1 - t0, D]), op=ALU.mult))
                pool.wait_ge(value_sum, c + 1)
                for k in range(1, TOPK):
                    term = yk[:, k, t0 * D:t1 * D].rearrange("p (t d) -> p t d", d=D)
                    ins = pool.tensor_tensor(out=value[:, t0:t1, :], in0=value[:, t0:t1, :], in1=term, op=ALU.add)
                    if k < TOPK - 1:
                        step(ins)
                ins.then_inc(pool_sum, 1)

        @block.scalar
        def _(act):
            steps = [0]

            def step(ins):
                steps[0] += 1
                ins.then_inc(act_step, 1)
                act.wait_ge(act_step, steps[0])

            act.dma_start(band_up[:, :, :], bass.AP(tensor=conv_pad.tensor, offset=0,
                                                    ap=[[1, P], [conv_pad.shape[1], H], [1, WIN]]))\
               .then_inc(band_in, 16)
            act.dma_start(wqkv_sb[:, :], qkv_w).then_inc(wqkv_in, 16)
            act.dma_start(wqT_sb[:, :, :], wq_t).then_inc(wt_in, 16)
            act.dma_start(wkT_sb[:, :, :], wk_t).then_inc(wt_in, 16)
            act.dma_start(idx_i[:, 0, :], adj_rows.rearrange("(p c) -> p c", p=P)).then_inc(edge_in, 16)
            act.dma_start(idx_i[:, 1, :], adj_cols.rearrange("(p c) -> p c", p=P)).then_inc(edge_in, 16)
            act.dma_start(vals[:, :], adj_vals.rearrange("(p c) -> p c", p=P)).then_inc(edge_in, 16)
            act.dma_start(outw_sb[:, :, :], out_w.rearrange("(c p) d -> p c d", p=P)).then_inc(encw_in, 16)
            act.dma_start(outb_row[:, :], out_b.rearrange("(a d) -> a d", a=1).broadcast_to([P, D]))\
               .then_inc(encw_in, 16)
            act.dma_start(wq_sb[:, :], wq).then_inc(encw_in, 16)
            act.dma_start(wk_sb[:, :], wk).then_inc(encw_in, 16)

            act.wait_ge(const_ready, 1)
            for c, w in enumerate(BAND_CUTS):
                act.wait_ge(band_ps, c + 1)
                act.activation(band[:, :, :].rearrange("p h m -> p (h m)")[:, c * N:c * N + w], bank[4 + c][:, 0:w],
                               ACT.Copy).then_inc(band_ready, 1)

            def deviation(b):
                act.wait_ge(stat_ready, b + 1)
                act.activation(std[:, b * NT:(b + 1) * NT], mv[:, b * NT:(b + 1) * NT, 1], ACT.Sqrt,
                               bias=eps_c[:, 0:1]).then_inc(std_ready, 1)

            def normalise(b):
                for t in range(b * NT, (b + 1) * NT):
                    ins = act.activation(xn[:, t, :], x[:, t, :], ACT.Identity, bias=nmr[:, t:t + 1],
                                         scale=rstd[:, t:t + 1])
                ins.then_inc(xn_ready, 1)

            def xnT_copy(b):
                act.wait_ge(xnT_ps, b + 1)
                act.activation(xnT[:, b * N:(b + 1) * N], bank[b % 2][:, :], ACT.Copy).then_inc(xnT_ready, 1)

            deviation(0)
            for b in range(B):
                if b + 1 < B:
                    deviation(b + 1)
                act.wait_ge(norm_ready, b + 1)
                normalise(b)
                if b >= 1:
                    xnT_copy(b - 1)
            xnT_copy(B - 1)
            act.wait_ge(colT_ps, 1)
            act.activation(colT[:, :], bank[3][:, 0:P], ACT.Copy).then_inc(colT_ready, 1)
            for t in range(NT):
                act.wait_ge(v_ps, t + 1)
                act.activation(v_sb[:, t, :], bank[4 + t][:, :], ACT.Copy).then_inc(v_ready, 1)
            for c in range(4):
                act.wait_ge(ql_ps, c + 1)
                act.activation(qlT[:, 2 * c:2 * c + 2, :].rearrange("p h n -> p (h n)"), bank[c][0:DH, :], ACT.Copy,
                               scale=DH ** -0.5 / LW).then_inc(ql_ready, 1)
            act.wait_ge(r_ps, 2)
            act.activation(r3[:, :], bank[2][:, 0:H * L], ACT.Copy).then_inc(r3_ready, 1)
            act.wait_ge(a2_shift, 1)
            act.activation(a2[:, :, :], a2[:, :, :], ACT.Exp).then_inc(a2_exp, 1)
            for g in range(G2):
                act.wait_ge(s3_max, g + 1)
                act.activation(p3[:, g, :], bank[3 - g][:, :], ACT.Exp, bias=p3m[:, g:g + 1],
                               accum_out=p3s[:, g:g + 1]).then_inc(p3_ready, 1)
            act.wait_ge(s1_shift, 1)
            act.activation(p1[:, :, :], p1[:, :, :], ACT.Exp).then_inc(s1_exp, 1)
            for g in range(G2):
                act.wait_ge(p3T_ps, g + 1)
                act.activation(p3T[:, g, :, :].rearrange("p c n -> p (c n)"), bank[3 - g][:, :], ACT.Copy)\
                   .then_inc(p3T_ready, 1)
            for g in range(G2):
                act.wait_ge(p1T_ps, g + 1)
                act.activation(p1T[:, g, :], bank[1 - g][:, :], ACT.Copy).then_inc(p1T_ready, 1)
            with act.Fori(0, PINV) as i:
                act.wait_ge(pz_ps, 2 * i + 2)
                act.activation(pzT[:, :, :].rearrange("p g n -> p (g n)"), bank[3][:, 0:G2 * P], ACT.Copy)\
                   .then_inc(pzT_ready, 1)
                act.wait_ge(zn_ps, 2 * i + 2)
                act.activation(zT[:, :, :].rearrange("p g n -> p (g n)"), bank[3][:, 0:G2 * P], ACT.Copy,
                               scale=0.25).then_inc(zT_ready, 1)
            act.wait_ge(m_ps, 1)
            act.activation(m_bd[:, :, :].rearrange("p g n -> p (g n)"), bank[2][:, :], ACT.Copy).then_inc(m_ready, 1)
            for c in range(2):
                act.wait_ge(outT_ps, 2 * c + 1)
                act.activation(outT[:, 2 * c, :], bank[4 + 2 * c][:, :], ACT.Copy).then_inc(outT_ready, 1)
            act.wait_ge(encT_ps, 1)
            act.activation(encT[:, :], bank[1][:, :], ACT.Copy).then_inc(encT_ready, 1)
            act.wait_ge(q_ps, 1)
            act.activation(q_tok[:, :, :].rearrange("p t q -> p (t q)"), bank[2][:, 0:NT * QK], ACT.Copy,
                           scale=QK ** -0.5).then_inc(q_ready, 1)
            with act.Fori(0, NG // 2) as pair:
                for s in range(2):
                    act.wait_ge(kv_ready, 2 * pair + s + 3)
                    act.activation(kvs[:, s, :, 0, :], kv[:, s, :, :], ACT.Copy).then_inc(kvu_ready, 1)
                    act.wait_ge(kvr_ready, 2 * pair + s + 1)
                    act.activation(kvs[:, s, :, 1, :], kvr[:, s, :, :], ACT.Copy).then_inc(kvu_ready, 1)
            act.wait_ge(amax_ready, 1)
            act.activation(arow[:, :], bank[5][0:1, :], ACT.Exp, bias=asc[0:1, 0:1],
                           accum_out=asc[0:1, 1:2]).then_inc(aexp_ready, 1)
            for t in range(NT):
                if t == 0:
                    act.wait_ge(alpha_ready, 1)
                if t >= 2:
                    act.wait_ge(gated_done, t - 1)
                step(act.activation(sg[:, t % 2, :, :], over_b(value, t), ACT.Sigmoid, scale=nalpha[:, t:t + 1]))
                act.activation(sg[:, t % 2, :, :], sg[:, t % 2, :, :], ACT.Square).then_inc(sw_ready, 1)
            act.wait_ge(stat_ready, B + 1)
            act.activation(std[:, :], mv[:, :, 1], ACT.Sqrt, bias=eps_c[:, 0:1], scale=4.0).then_inc(std_ready, 1)
            for b in range(B):
                act.wait_ge(xnT_ps, B + b + 1)
                act.activation(xnT[:, b * N:(b + 1) * N], bank[b % 2][:, :], ACT.Copy).then_inc(xnT_ready, 1)
            act.wait_ge(stat_ready, B + 2)
            act.activation(std[:, :], mv[:, :, 1], ACT.Sqrt, bias=eps_c[:, 0:1]).then_inc(std_ready, 1)
            act.wait_ge(norm_ready, B + 1)
            for b in range(B):
                normalise(b)
            act.wait_ge(lshift, 1)
            act.activation(gate[:, :, :], gate[:, :, :], ACT.Exp).then_inc(lexp, 1)

            def gelu(g, s):
                act.wait_ge(up_ps, nth(g, s) + 1)
                for c in range(FC):
                    ins = act.activation(hT[:, slot(s), tok(c)], bank[2 + slot(s)][:, tok(c)], ACT.Gelu,
                                         bias=w1_now[:, slot(s), F + c:F + c + 1])
                ins.then_inc(h_ready, 1)

            def act_group(g):
                for s in range(BG):
                    gelu(g, s)

            group_loop(act, act_group)
            for c, (t0, t1) in enumerate(zip(YCUTS, YCUTS[1:])):
                act.wait_ge(yk_in[c], 16)
                for t in range(t0, t1):
                    ins = act.activation(value[:, t, :], yk[:, 0, t * D:(t + 1) * D], ACT.Copy, scale=gate[:, t, 0:1])
                ins.then_inc(value_sum, 1)
            act.wait_ge(stat_ready, B + 3)
            act.activation(std[:, :], mv[:, :, 1], ACT.Sqrt, bias=eps_c[:, 0:1]).then_inc(std_ready, 1)
            act.wait_ge(norm_ready, B + 2)
            for b in range(2, B):
                for t in range(b * NT, (b + 1) * NT):
                    ins = act.activation(value[:, t, :], value[:, t, :], ACT.Identity, bias=nmr[:, t:t + 1],
                                         scale=rstd[:, t:t + 1])
                ins.then_inc(value_sum, 1)

        @block.vector
        def _(dve):
            steps = [0]
            v = nc.vector

            def step(ins):
                steps[0] += 1
                ins.then_inc(dve_step, 1)
                dve.wait_ge(dve_step, steps[0])

            def row_stats(src, t, last):
                for i in t:
                    ins = v.bn_stats(stats[:, i, :], src[:, i, :])
                step(ins)
                for i in t:
                    ins = v.bn_aggr(mv[:, i, :], stats[:, i, :])
                ins.then_inc(last, 1)

            def batch(b):
                return range(b * NT, (b + 1) * NT)

            def norm(sl):
                step(v.reciprocal(rstd[:, sl], std[:, sl]))
                return v.scalar_tensor_tensor(out=nmr[:, sl], in0=mv[:, sl, 0], scalar=-1.0, in1=rstd[:, sl],
                                              op0=ALU.mult, op1=ALU.mult)

            def batch_norm(b):
                dve.wait_ge(std_ready, b + 1)
                norm(slice(b * NT, (b + 1) * NT)).then_inc(norm_ready, 1)

            def values(b):
                dve.wait_ge(xnT_ready, b + 1)
                v.tensor_reduce(out=xlT[:, b * L:(b + 1) * L],
                                in_=xnT[:, b * N:(b + 1) * N].rearrange("p (l w) -> p l w", w=LW),
                                axis=AX.X, op=ALU.add).then_inc(xl_ready, 1)
                if b == 0:
                    dve.wait_ge(wv_in, 32)
                dve.wait_ge(val_ps, b + 1)
                v.tensor_tensor(out=value[:, b * NT:(b + 1) * NT, :],
                                in0=bank[2 + b % 2][:, :].rearrange("p (t d) -> p t d", t=NT),
                                in1=wvb_row[:, :].unsqueeze(1).broadcast_to([P, NT, D]), op=ALU.add)\
                 .then_inc(val_ready, 1)

            for b in range(B):
                dve.wait_ge(x_in[loaded(b)], 16)
                row_stats(x, batch(b), stat_ready)
                if b >= 1:
                    batch_norm(b - 1)
                if b >= 3:
                    values(b - 3)
            batch_norm(B - 1)
            dve.wait_ge(edge_in, 48)
            step(v.tensor_copy(idx_f[:, :, :], idx_i[:, :, :]))
            step(v.tensor_scalar(neg[:, :], idx_f[:, 1, :], 0.0, float(N), ALU.is_lt, ALU.mult))
            step(v.tensor_tensor(out=idx_f[:, 1, :], in0=idx_f[:, 1, :], in1=neg[:, :], op=ALU.add))
            v.tensor_scalar(idx_f[:, 1, :], idx_f[:, 1, :], 0.0, float(N - 1), ALU.max, ALU.min)\
             .then_inc(colT_need, 1)
            for b in range(B - 3, B):
                values(b)

            dve.wait_ge(const_ready, 2)
            for c in range(4):
                dve.wait_ge(kl_ps, c + 1)
                v.tensor_scalar(klT[:, 2 * c:2 * c + 2, :].rearrange("p h n -> p (h n)"), bank[c][0:DH, :],
                                1.0 / LW, None, ALU.mult).then_inc(kl_ready, 1)
            dve.wait_ge(r_ps, 1)
            v.tensor_scalar(r1[:, :], bank[1][:, 0:H * L], DH ** -0.5, None, ALU.mult).then_inc(r1_ready, 1)

            def shift_max(ps, dst, mx, out_sem):
                step(v.tensor_reduce(out=mx, in_=ps, axis=AX.X, op=ALU.max))
                v.tensor_tensor(out=dst, in0=ps, in1=mx.unsqueeze(2).broadcast_to(list(dst.shape)),
                                op=ALU.subtract).then_inc(out_sem, 1)

            def normalise_rows(p, s):
                step(v.tensor_reduce(out=s, in_=p, axis=AX.X, op=ALU.add))
                step(v.reciprocal(s, s))
                return v.tensor_tensor(out=p, in0=p, in1=s.unsqueeze(2).broadcast_to(list(p.shape)), op=ALU.mult)

            dve.wait_ge(a2_ps, 1)
            shift_max(bank[0][:, :].rearrange("p (a j) -> p a j", j=L), a2[:, :, :], a2m[:, :], a2_shift)
            for g in range(G2):
                dve.wait_ge(s3_ps, g + 1)
                v.tensor_reduce(out=p3m[:, g:g + 1], in_=bank[3 - g][:, :], axis=AX.X, op=ALU.max, negate=True)\
                 .then_inc(s3_max, 1)
            dve.wait_ge(a2_exp, 1)
            normalise_rows(a2[:, :, :], a2s[:, :]).then_inc(a2_ready, 1)
            dve.wait_ge(a2_ready, 1)
            step(v.tensor_tensor(out=xbd[:, :, :].rearrange("p g (h j) -> p g h j", h=HG),
                                 in0=a2[:, 0:G2, :].unsqueeze(2).broadcast_to([P, G2, HG, L]),
                                 in1=blk_j[:, :, :].unsqueeze(1).broadcast_to([P, G2, HG, L]), op=ALU.mult))
            step(v.tensor_reduce(out=a2s[:, :], in_=a2[:, :, :], axis=AX.X, op=ALU.add))
            v.tensor_reduce(out=mx2[:, 0:1], in_=a2s[:, :], axis=AX.X, op=ALU.max).then_inc(xbd_ready, 1)
            dve.wait_ge(s1_ps, 1)
            for h in range(2):
                sl = slice(h * 16, (h + 1) * 16)
                step(v.tensor_reduce(out=p1m[:, sl], in_=bank[1 - h][:, :].rearrange("p (a j) -> p a j", j=L),
                                     axis=AX.X, op=ALU.max))
                ins = v.tensor_tensor(out=p1[:, sl, :], in0=bank[1 - h][:, :].rearrange("p (a j) -> p a j", j=L),
                                      in1=p1m[:, sl].unsqueeze(2).broadcast_to([P, 16, L]), op=ALU.subtract)
            ins.then_inc(s1_shift, 1)
            dve.wait_ge(xT_ps, 1)
            v.tensor_reduce(out=mx2[:, 1:2], in_=bank[0][:, :], axis=AX.X, op=ALU.max).then_inc(max_ready, 1)
            v.tensor_copy(xT[:, :, :].rearrange("p g n -> p (g n)"), bank[7][:, 0:G2 * P]).then_inc(xT_ready, 1)
            dve.wait_ge(s1_exp, 1)
            normalise_rows(p1[:, :, :], p1s[:, :]).then_inc(p1_ready, 1)
            dve.wait_ge(max_ps, 1)
            step(v.tensor_reduce(out=srow[0:1, 0:2], in_=bank[7][0:1, 0:2 * P].rearrange("p (a n) -> p a n", a=2),
                                 axis=AX.X, op=ALU.max))
            step(v.tensor_tensor(out=srow[0:1, 2:3], in0=srow[0:1, 0:1], in1=srow[0:1, 1:2], op=ALU.mult))
            v.reciprocal(srow[0:1, 3:4], srow[0:1, 2:3]).then_inc(sinv_row, 1)
            dve.wait_ge(sinv_ps, 1)
            step(v.tensor_copy(sinv[:, :], bank[7][:, 0:1]))
            v.tensor_scalar(z[:, :, :], xT[:, :, :], sinv[:, 0:1], None, ALU.mult).then_inc(z_ready, 1)
            v.tensor_scalar(zT[:, :, :], xbd[:, :, :], sinv[:, 0:1], None, ALU.mult).then_inc(zT_ready, 1)
            dve.wait_ge(a3v_ps, 1)
            step(v.reciprocal(p3s[:, :], p3s[:, :]))
            for g in range(G2):
                ins = v.scalar_tensor_tensor(out=a3v[:, g, :], in0=bank[3][:, g * 256:(g + 1) * 256],
                                             scalar=p3s[:, g:g + 1],
                                             in1=blk_d[:, :, :].rearrange("p h d -> p (h d)"),
                                             op0=ALU.mult, op1=ALU.mult)
            ins.then_inc(a3v_ready, 1)
            with dve.Fori(0, PINV) as i:
                for n in range(3):
                    if n == 0:
                        dve.wait_ge(pz_ps, 2 * i + 1)
                    else:
                        dve.wait_ge(tz_ps, 2 * i + n)
                    v.scalar_tensor_tensor(out=tz[:, :, :], in0=bank[2 + (n == 2)][:, 0:G2 * P]
                                           .rearrange("p (g n) -> p g n", g=G2), scalar=-1.0,
                                           in1=identw[:, n, :, :], op0=ALU.mult, op1=ALU.add).then_inc(t_ready, 1)
                dve.wait_ge(zn_ps, 2 * i + 1)
                v.tensor_scalar(z[:, :, :].rearrange("p g n -> p (g n)"), bank[2][:, 0:G2 * P], 0.25, None,
                                ALU.mult).then_inc(z_ready, 1)
            for c in range(2):
                dve.wait_ge(outT_ps, 2 * c + 2)
                v.tensor_copy(outT[:, 2 * c + 1, :], bank[5 + 2 * c][:, :]).then_inc(outT_ready, 1)
            dve.wait_ge(encw_in, 64)
            dve.wait_ge(xg_ps, 1)
            step(v.tensor_tensor(out=xgb[:, :, :], in0=bank[0][:, :].rearrange("p (t d) -> p t d", t=NT),
                                 in1=outb_row[:, :].unsqueeze(1).broadcast_to([P, NT, D]), op=ALU.add))
            v.tensor_tensor(out=xn[:, 0:NT, :], in0=xn[:, 0:NT, :], in1=xgb[:, :, :], op=ALU.add)\
             .then_inc(enc0_ready, 1)
            dve.wait_ge(k_ps, 1)
            step(v.tensor_copy(kf[:, :, :].rearrange("p c q -> p (c q)"), bank[3][:, 0:NT * QK]))
            step(v.tensor_copy(ksp[:, :, 0, :], kf[:, :, :]))
            step(v.tensor_tensor(out=kres[:, :, :], in0=kf[:, :, :], in1=ksp[:, :, 0, :], op=ALU.subtract))
            step(v.tensor_copy(ksp[:, :, 1, :], kres[:, :, :]))
            v.tensor_tensor(out=ksp[:, :, 2, :], in0=kres[:, :, :], in1=ksp[:, :, 1, :], op=ALU.subtract)\
             .then_inc(ksp_ready, 1)
            dve.wait_ge(colb_in, 16)

            def one_hot_cols(pair, s):
                g = 2 * pair + s
                dve.wait_ge(kg_ps, 2 * pair + s + 1)
                for c in range(NT):
                    ins = v.tensor_scalar(oh_c[:, s, c, :], colb[:, bass.ds(g * (EG * P), EG * P)],
                                          iota_c[:, c:c + 1], None, ALU.is_equal)
                ins.then_inc(ohc_ready, 1)

            def one_hot_rows(pair, s):
                g = 2 * pair + s
                dve.wait_ge(g_done, 2 * pair + s + 1)
                for j in range(EG):
                    ins = v.tensor_scalar(oh_r[:, s, j, :], iota_r[:, :], idx_f[:, 0, bass.ds(g * EG + j, 1)], None,
                                          ALU.is_equal)
                ins.then_inc(ohr_ready, 1)

            def product(pair, s):
                g = 2 * pair + s
                dve.wait_ge(kg_ps, 2 * pair + s + 3)
                v.tensor_tensor(out=kv[:, s, :, :],
                                in0=bank[s][:, 0:EG * QK].rearrange("p (j q) -> p j q", j=EG),
                                in1=vals[:, bass.ds(g * EG, EG)].unsqueeze(2).broadcast_to([P, EG, QK]),
                                op=ALU.mult).then_inc(kv_ready, 1)

            def middle(pair, s):
                dve.wait_ge(kvu_ready, 2 * (2 * pair + s) + 1)
                v.tensor_tensor(out=kvr[:, s, :, :], in0=kv[:, s, :, :], in1=kvs[:, s, :, 0, :], op=ALU.subtract)\
                 .then_inc(kvr_ready, 1)

            def lower(pair, s):
                dve.wait_ge(kvu_ready, 2 * (2 * pair + s) + 2)
                v.tensor_tensor(out=kvs[:, s, :, 2, :], in0=kvr[:, s, :, :], in1=kvs[:, s, :, 1, :],
                                op=ALU.subtract).then_inc(kvs_ready, 1)

            def group(pair, s, last=False):
                after = (pair + (s + 1) // 2, (s + 1) % 2)
                product(pair, s)
                if not last:
                    one_hot_cols(*after)
                middle(pair, s)
                if not last:
                    one_hot_rows(*after)
                lower(pair, s)

            dve.sem_inc(kv_ready, 2)
            one_hot_cols(0, 0)
            one_hot_rows(0, 0)
            with dve.Fori(0, NG // 2 - 1) as pair:
                group(pair, 0)
                group(pair, 1)
            group(NG // 2 - 1, 0)
            group(NG // 2 - 1, 1, True)
            dve.wait_ge(g_ps, 1)
            dve.wait_ge(q_ready, 1)
            step(v.tensor_tensor(out=prod[:, :, :, :], in0=bank[4][:, 0:NT * NS * QK]
                                 .rearrange("p (t n q) -> p t n q", t=NT, n=NS),
                                 in1=q_tok[:, :, :].unsqueeze(2).broadcast_to([P, NT, NS, QK]), op=ALU.mult))
            v.tensor_reduce(out=araw[:, :], in_=prod[:, :, :, :].rearrange("p t n q -> p t (n q)"), axis=AX.X,
                            op=ALU.add).then_inc(araw_ready, 1)
            dve.wait_ge(arow_ps, 1)
            v.tensor_reduce(out=asc[0:1, 0:1], in_=bank[5][0:1, :], axis=AX.X, op=ALU.max, negate=True)\
             .then_inc(amax_ready, 1)
            dve.wait_ge(aexp_ready, 1)
            step(v.reciprocal(asc[0:1, 2:3], asc[0:1, 1:2]))
            v.tensor_scalar(arow[:, :], arow[:, :], asc[0:1, 2:3], None, ALU.mult).then_inc(arow_ready, 1)
            dve.wait_ge(alpha_ps, 1)
            v.tensor_scalar(nalpha[:, :], bank[6][:, 0:NT], -1.0, None, ALU.mult).then_inc(alpha_ready, 1)
            step(v.tensor_copy(alpha[:, :], bank[6][:, 0:NT]))
            dve.wait_ge(ffnc_in, 64)
            v.tensor_tensor(out=ksq[:, :], in0=keysT[:, :], in1=keysT[:, :], op=ALU.mult)
            v.scalar_tensor_tensor(out=comb[:, :], in0=keysT[:, :], scalar=2.0, in1=rwT[:, :],
                                   op0=ALU.mult, op1=ALU.add).then_inc(comb_ready, 1)
            dve.wait_ge(enc_ready, 1)

            def gated(t):
                step(v.scalar_tensor_tensor(out=xl[:, t % 2, :, :], in0=over_b(value, t), scalar=alpha[:, t:t + 1],
                                            in1=over_b(xn, t), op0=ALU.mult, op1=ALU.subtract))
                dve.wait_ge(sw_ready, t + 1)
                step(v.tensor_tensor(out=xl[:, t % 2, :, :], in0=xl[:, t % 2, :, :], in1=sg[:, t % 2, :, :],
                                     op=ALU.mult))
                v.tensor_tensor(out=over_b(xn, t), in0=over_b(xn, t), in1=xl[:, t % 2, :, :], op=ALU.add)\
                 .then_inc(gated_done, 1)

            for t in range(NT):
                gated(t)
            dve.wait_ge(gated_done, NT)
            row_stats(xn, range(T), stat_ready)
            dve.wait_ge(std_ready, B + 1)
            step(v.reciprocal(rstd[:, :], std[:, :]))
            step(v.tensor_scalar(rstd[:, :], rstd[:, :], 2.0, None, ALU.mult))
            v.tensor_tensor(out=shift[:, :], in0=mv[:, :, 0], in1=rstd[:, :], op=ALU.mult)
            for b in range(B):
                for t in batch(b):
                    ins = v.scalar_tensor_tensor(out=x[:, t, :], in0=xn[:, t, :], scalar=rstd[:, t:t + 1],
                                                 in1=x[:, t, :], op0=ALU.mult, op1=ALU.add)
                ins.then_inc(x2_ready, 1)
            dve.wait_ge(x2_ready, B)
            row_stats(x, range(T), stat_ready)

            dve.wait_ge(std_ready, B + 2)
            norm(slice(0, T)).then_inc(norm_ready, 1)
            dve.wait_ge(norm_ready, B + 1)
            dve.wait_ge(ksq_ps, 1)
            v.tensor_copy(csum[:, :], bank[5][:, E:2 * E])
            step(v.tensor_tensor(out=lbias[:, :], in0=rb_row[:, :], in1=bank[5][:, 0:E], op=ALU.subtract))
            dve.wait_ge(logit_ps, 1)
            step(v.tensor_tensor(out=logits[:, :, :], in0=bank[6][:, :].rearrange("p (t e) -> p t e", t=T),
                                 in1=rstd[:, :].unsqueeze(2).broadcast_to([P, T, E]), op=ALU.mult))
            step(v.tensor_tensor(out=tmp_e[:, :, :], in0=nmr[:, :].unsqueeze(2).broadcast_to([P, T, E]),
                                 in1=csum[:, :].unsqueeze(1).broadcast_to([P, T, E]), op=ALU.mult))
            step(v.tensor_tensor(out=logits[:, :, :], in0=logits[:, :, :], in1=tmp_e[:, :, :], op=ALU.add))
            step(v.tensor_tensor(out=logits[:, :, :], in0=logits[:, :, :],
                                 in1=lbias[:, :].unsqueeze(1).broadcast_to([P, T, E]), op=ALU.add))
            step(v.tensor_tensor(out=x2n[:, :], in0=rstd[:, :], in1=rstd[:, :], op=ALU.mult))
            step(v.tensor_tensor(out=x2n[:, :], in0=x2n[:, :], in1=mv[:, :, 1], op=ALU.mult))
            step(v.tensor_scalar(x2n[:, :], x2n[:, :], float(D), None, ALU.mult))
            step(v.tensor_tensor(out=logits[:, :, :], in0=logits[:, :, :],
                                 in1=x2n[:, :].unsqueeze(2).broadcast_to([P, T, E]), op=ALU.subtract))
            for t in range(T):
                ins = v.max(out=top8[:, t, :], in_=logits[:, t, :])
            step(ins)
            v.tensor_tensor(out=gate[:, :, :], in0=top8[:, :, 0:TOPK],
                            in1=top8[:, :, 0:1].broadcast_to([P, T, TOPK]), op=ALU.subtract).then_inc(lshift, 1)
            dve.wait_ge(const_ready, 3)
            for t in range(T):
                ins = v.max_index(out=topi[:, t, :], in_max=top8[:, t, :], in_values=logits[:, t, :])
            step(ins)
            step(v.tensor_copy(topf[:, :, :], topi[:, :, 0:TOPK]))
            for k in range(TOPK):
                ins = v.tensor_tensor(out=khot[k][:, :, :], in0=iota_e[:, :].unsqueeze(1).broadcast_to([P, T, E]),
                                      in1=topf[:, :, k:k + 1].broadcast_to([P, T, E]), op=ALU.is_equal)
            step(ins)
            step(v.tensor_tensor(out=chosen[:, :, :], in0=khot[0][:, :, :], in1=khot[1][:, :, :], op=ALU.add))
            step(v.tensor_tensor(out=tmp_e[:, :, :], in0=khot[2][:, :, :], in1=khot[3][:, :, :], op=ALU.add))
            v.tensor_tensor(out=chosen_b[:, :, :], in0=chosen[:, :, :], in1=tmp_e[:, :, :], op=ALU.add)\
             .then_inc(chosen_ready, 1)
            v.memset(zero_r[:, :], 0.0)
            dve.wait_ge(prefix_ps, 2)
            step(v.tensor_copy(tot[:, :, :], bank[1][:, :].rearrange("p (t e) -> p e t", t=T)))
            step(v.tensor_tensor_scan(out=cum[:, :, :].rearrange("p e t -> p (e t)"),
                                      data0=tot[:, :, :].rearrange("p e t -> p (e t)"), data1=zero_r[:, :],
                                      initial=0.0, op0=ALU.add, op1=ALU.add))
            step(v.tensor_tensor(out=tot[:, :, :], in0=cum[:, :, :], in1=tot[:, :, :], op=ALU.subtract))
            step(v.tensor_tensor(out=cnt[:, :], in0=cum[:, :, T - 1], in1=tot[:, :, 0], op=ALU.subtract))
            step(v.tensor_scalar(cnt_i[:, :], cnt[:, :], float(P - 1), None, ALU.add))
            step(v.tensor_scalar(cnt_i[:, :], cnt_i[:, :], 7, 7, ALU.logical_shift_right, ALU.logical_shift_left))
            step(v.tensor_copy(cnt[:, :], cnt_i[:, :]))
            step(v.tensor_tensor_scan(out=pend[:, :], data0=cnt[:, :], data1=zero_r[:, 0:E], initial=0.0,
                                      op0=ALU.add, op1=ALU.add))
            step(v.tensor_tensor(out=pbase[:, :], in0=pend[:, :], in1=cnt[:, :], op=ALU.subtract))
            step(v.tensor_scalar(pend[:, :], pend[:, :], 1.0 / P, None, ALU.mult))
            step(v.tensor_tensor(out=blk_cmp[:, :, :], in0=pend[:, :].unsqueeze(1).broadcast_to([P, 2, E]),
                                 in1=iota_b2[:, :].unsqueeze(2).broadcast_to([P, 2, E]), op=ALU.is_le))
            step(v.tensor_reduce(out=blk_exp[:, :], in_=blk_cmp[:, :, :], axis=AX.X, op=ALU.add))
            v.tensor_scalar(blk_exp[:, :], blk_exp[:, :], float(E - 1), None, ALU.min).then_inc(bexp_ready, 1)
            step(v.tensor_tensor(out=pbase[:, :], in0=pbase[:, :], in1=tot[:, :, 0], op=ALU.subtract))
            step(v.tensor_tensor(out=tot[:, :, :], in0=tot[:, :, :],
                                 in1=pbase[:, :].unsqueeze(2).broadcast_to([P, E, T]), op=ALU.add))
            step(v.tensor_tensor(out=pos_e[:, :, :], in0=bank[0][:, :].rearrange("p (t e) -> p t e", t=T),
                                 in1=tot[:, :, :].rearrange("p e t -> p t e"), op=ALU.add))
            for k in range(TOPK):
                step(v.tensor_tensor(out=khot[k][:, :, :], in0=khot[k][:, :, :], in1=pos_e[:, :, :], op=ALU.mult))
                ins = v.tensor_reduce(out=pos[:, :, k], in_=khot[k][:, :, :], axis=AX.X, op=ALU.add)
            step(ins)
            step(v.tensor_copy(pos_i[:, :, :], pos[:, :, :]))
            v.tensor_scalar(lane_i[:, :, :], pos_i[:, :, :], P - 1, None, ALU.bitwise_and)
            step(v.tensor_scalar(pos_i[:, :, :], pos_i[:, :, :], 7, None, ALU.logical_shift_right))
            v.tensor_copy(lane[:, :, :], lane_i[:, :, :]).then_inc(lane_ready, 1)
            step(v.tensor_copy(blk[:, :, :], pos_i[:, :, :]))
            lane_f, blk_f = [a[:, :, :].rearrange("p t k -> p (t k)") for a in (lane, blk)]
            tk_f = token_of[:, :, :, :].rearrange("p t k a -> p (t k a)").bitcast(fp32)
            dve.sem_inc(hot_used, 2)
            dve.wait_ge(xd_done, 16 * B)
            with dve.Fori(0, T // 4) as i:
                for s in range(4):
                    dve.wait_ge(hot_used, 4 * i + s + 1)
                    for k in range(TOPK):
                        at = bass.ds((4 * i + s) * TOPK + k, 1)
                        if k < VK:
                            v.tensor_scalar(hot_lane[:, bass.ds(4 * i + s, 1), k, :].rearrange("p t n -> p (t n)"),
                                            iota_r[:, 0:P], lane_f[:, at], None, ALU.is_equal)
                        ins = v.tensor_scalar(hot_blk[:, s % 2, k, :], iota_b[:, :], blk_f[:, at], tk_f[:, at],
                                              ALU.is_equal, ALU.mult)
                    ins.then_inc(hot_ready, 1)
            dve.wait_ge(bexp_ps, 1)
            v.tensor_copy(exp_row[:, :], bank[3][0:1, 0:2 * P]).then_inc(exp_ready, 1)
            dve.wait_ge(table_ps, 1)
            found_p, found_tk = [bank[2][:, 0:2 * NBLK].rearrange("p (b a) -> p a b", a=2)[:, a, :] for a in range(2)]
            v.tensor_scalar(used[:, :], found_p, 0.0, None, ALU.is_gt)
            v.tensor_scalar(src_tok[:, :], found_p, 1.0, float(T), ALU.subtract, ALU.mult)
            step(v.tensor_scalar(part_i[:, 0, :], found_tk, 1.0, 0.0, ALU.subtract, ALU.max))
            v.tensor_scalar(part_i[:, 1, :], part_i[:, 0, :], 5, 12, ALU.logical_shift_right, ALU.logical_shift_left)
            step(v.tensor_scalar(part_i[:, 0, :], part_i[:, 0, :], T - 1, None, ALU.bitwise_and))
            step(v.tensor_copy(part_f[:, :, :], part_i[:, :, :]))
            step(v.tensor_tensor(out=src_tok[:, :], in0=src_tok[:, :], in1=part_f[:, 0, :], op=ALU.add))
            step(v.tensor_tensor(out=part_f[:, 1, :], in0=src_tok[:, :], in1=part_f[:, 1, :], op=ALU.add))
            step(v.tensor_tensor(out=part_f[:, 1, :], in0=part_f[:, 1, :], in1=iota_d[:, :], op=ALU.subtract))
            step(v.tensor_tensor(out=part_f[:, 1, :], in0=part_f[:, 1, :], in1=used[:, :], op=ALU.mult))
            step(v.tensor_tensor(out=idx_dst[:, :], in0=part_f[:, 1, :], in1=iota_d[:, :], op=ALU.add))
            v.tensor_scalar(idx_src[:, :], src_tok[:, :], 0.0, None, ALU.max).then_inc(idx_ready, 1)
            dve.wait_ge(lexp, 1)
            step(normalise_rows(gate[:, :, :], gsum[:, :]))

            def weights(g, s, e):
                freed(dve, up_ps, nth(g, s) - 1)
                freed(dve, h_ready, nth(g, s) - 1)
                v.tensor_scalar(w1_now[:, slot(s), :], w1_sb[:, bass.ds(e, 1), :].rearrange("p a f -> p (a f)"), 1.0,
                                None, ALU.mult).then_inc(w1_ready, 1)

            def xT_copy(g, s):
                dve.wait_ge(xgT_ps, nth(g, s) + 1)
                v.tensor_copy(xgT[:, slot(s), :], bank[slot(s)][:, 0:P]).then_inc(xgT_ready, 1)

            def y_copy(g, s):
                dve.wait_ge(down_ps, nth(g, s) + 1)
                freed(dve, y_out[s % RING], 16 * (g * (BG // RING) + s // RING))
                v.tensor_copy(yg[:, s % RING, :], bank[6 + slot(s)][:, 0:P]).then_inc(y_ready, 1)

            def dve_group(g):
                e = experts(dve, BG * g + 1)
                for s in range(BG):
                    if follows(g, s + 1):
                        weights(g, s + 1, e[s])
                    if follows(g, s + 1):
                        xT_copy(g, s + 1)
                    if precedes(g, s - 2):
                        y_copy(g, s - 2)

            dve.wait_ge(w_in, 48)
            dve.wait_ge(exp_ready, 1)
            weights(0, 0, experts(dve, 0, 1)[0])
            xT_copy(0, 0)
            group_loop(dve, dve_group)
            y_copy(GROUPS, -2)
            y_copy(GROUPS, -1)
            def cut_stats(c):
                dve.wait_ge(pool_sum, c + 1)
                for t in range(YCUTS[c], YCUTS[c + 1]):
                    ins = v.bn_stats(stats[:, t, :], value[:, t, :])
                step(ins)
                for t in range(YCUTS[c], YCUTS[c + 1]):
                    ins = v.bn_aggr(mv[:, t, :], stats[:, t, :])
                return ins

            CUTS = len(YCUTS) - 1
            for c in range(CUTS):
                dve.wait_ge(yk_in[c], 16)
                dve.wait_ge(value_sum, c + 1)
                for k in range(1, TOPK):
                    for t in range(*of_vector(c)):
                        ins = v.scalar_tensor_tensor(out=value[:, t, :], in0=yk[:, k, t * D:(t + 1) * D],
                                                     scalar=gate[:, t, k:k + 1], in1=value[:, t, :],
                                                     op0=ALU.mult, op1=ALU.add)
                    step(ins)
                if c >= 1:
                    cut_stats(c - 1)
            cut_stats(CUTS - 1).then_inc(stat_ready, 1)
            dve.wait_ge(std_ready, B + 3)
            step(norm(slice(0, T)))
            v.tensor_tensor(out=nmr[:, :], in0=nmr[:, :], in1=shift[:, :], op=ALU.subtract).then_inc(norm_ready, 1)
            dve.wait_ge(norm_ready, B + 2)
            for b in range(B):
                sl = slice(b * NT, (b + 1) * NT)
                if b < 2:
                    for t in batch(b):
                        ins = v.tensor_scalar(value[:, t, :], value[:, t, :], rstd[:, t:t + 1], nmr[:, t:t + 1],
                                              ALU.mult, ALU.add)
                    step(ins)
                else:
                    dve.wait_ge(value_sum, CUTS + b - 1)
                v.tensor_tensor(out=x[:, sl, :], in0=x[:, sl, :], in1=value[:, sl, :], op=ALU.add)\
                 .then_inc(out_ready, 1)

        @block.tensor
        def _(pe):
            mm = nc.tensor.matmul

            def transposes(dst, src, n, width=P):
                for t in range(n):
                    ins = nc.tensor.transpose(dst(t), src(t), ident[:, :])
                return ins

            pe.wait_ge(const_ready, 1)
            pe.wait_ge(band_in, 16)
            for c, w in enumerate(BAND_CUTS):
                mm(bank[4 + c][:, 0:w], flip[:, :], band_up[:, :, :].rearrange("p h m -> p (h m)")[:, c * N:c * N + w],
                   start=True, stop=True).then_inc(band_ps, 1)

            def value_product(b):
                if b == 0:
                    pe.wait_ge(wv_in, 32)
                pe.wait_ge(xnT_ready, b + 1)
                if b >= 2:
                    pe.wait_ge(val_ready, b - 1)
                for t in range(NT):
                    ins = mm(bank[2 + b % 2][:, tok(t)], xnT[:, tok(b * NT + t)], wv_sb[:, :], start=True, stop=True)
                ins.then_inc(val_ps, 1)

            for b in range(B):
                pe.wait_ge(xn_ready, b + 1)
                if b >= 2:
                    pe.wait_ge(xnT_ready, b - 1)
                transposes(lambda t: bank[b % 2][:, tok(t)], lambda t: xn[:, b * NT + t, :], NT).then_inc(xnT_ps, 1)
                if b >= 1:
                    value_product(b - 1)
            value_product(B - 1)
            pe.wait_ge(val_ready, B)
            pe.wait_ge(colT_need, 1)
            nc.tensor.transpose(bank[3][:, 0:P], idx_f[:, 1, :], ident[:, :]).then_inc(colT_ps, 1)
            pe.wait_ge(wqkv_in, 16)
            pe.wait_ge(band_ready, len(BAND_CUTS))
            for t in range(NT):
                mm(bank[4 + t][:, :], xnT[:, tok(t)], wqkv_sb[:, 2 * H * DH:3 * H * DH], start=True, stop=True)\
                    .then_inc(v_ps, 1)
            pe.wait_ge(xl_ready, B)
            for c in range(4):
                if c == 3:
                    pe.wait_ge(colT_ready, 1)
                for h in (2 * c, 2 * c + 1):
                    ins = mm(bank[c][0:DH, (h % 2) * 256:(h % 2) * 256 + B * L], wqkv_sb[:, h * DH:(h + 1) * DH],
                             xlT[:, :], start=True, stop=True)
                ins.then_inc(ql_ps, 1)
            for c in range(4):
                pe.wait_ge(ql_ready, c + 1)
                for h in (2 * c, 2 * c + 1):
                    ins = mm(bank[c][0:DH, (h % 2) * 256:(h % 2) * 256 + B * L],
                             wqkv_sb[:, (H + h) * DH:(H + h + 1) * DH], xlT[:, :], start=True, stop=True)
                ins.then_inc(kl_ps, 1)
            pe.wait_ge(wt_in, 32)
            pe.wait_ge(kl_ready, 4)
            for h in range(H):
                ins = mm(bank[1][:, h * L:(h + 1) * L], wqT_sb[:, h, :], klT[:, h, 0:L], start=True, stop=True)
            ins.then_inc(r_ps, 1)
            for h in range(H):
                ins = mm(bank[2][:, h * L:(h + 1) * L], wkT_sb[:, h, :], qlT[:, h, 0:L], start=True, stop=True)
            ins.then_inc(r_ps, 1)
            for b in range(B):
                for h in range(H):
                    col = (b * G2 + h // HG) * L
                    ins = mm(bank[0][(h % HG) * L:(h % HG + 1) * L, col:col + L], qlT[:, h, b * L:(b + 1) * L],
                             klT[:, h, b * L:(b + 1) * L], start=True, stop=True)
            ins.then_inc(a2_ps, 1)
            pe.wait_ge(r3_ready, 1)
            for g in range(G2):
                mm(bank[3 - g][:, :], r3[:, g * P:(g + 1) * P], xnT[:, 0:N], start=True, stop=True)\
                    .then_inc(s3_ps, 1)
            pe.wait_ge(r1_ready, 1)
            pe.wait_ge(a2_shift, 1)
            for t in range(NT):
                ins = mm(bank[1 - t // 2][:, (t % 2) * 256:(t % 2) * 256 + H * L], xnT[:, tok(t)], r1[:, :],
                         start=True, stop=True)
            ins.then_inc(s1_ps, 1)
            pe.wait_ge(v_ready, NT)

            def conv(c):
                for h in (2 * c, 2 * c + 1):
                    lo = (h % 2) * DH
                    for o in range(NT):
                        ins = mm(bank[4 + c][lo:lo + DH, tok(o)], v_sb[:, o, h * DH:(h + 1) * DH],
                                 band[:, h, HALO:HALO + P], start=(o == 0), stop=False, skip_group_check=True)
                    for o in range(NT):
                        if o > 0:
                            ins = mm(bank[4 + c][lo:lo + DH, o * P:o * P + HALO], v_sb[:, o - 1, h * DH:(h + 1) * DH],
                                     band[:, h, HALO + P:WIN], start=False, stop=False, skip_group_check=True)
                        if o < NT - 1:
                            ins = mm(bank[4 + c][lo:lo + DH, (o + 1) * P - HALO:(o + 1) * P],
                                     v_sb[:, o + 1, h * DH:(h + 1) * DH],
                                     band[:, h, 0:HALO], start=False, stop=False, skip_group_check=True)

            for c in range(3):
                conv(c)
            pe.wait_ge(xbd_ready, 1)
            pe.wait_ge(const_ready, 2)
            pe.wait_ge(s1_shift, 1)
            mm(bank[0][:, :], blk_j[:, :, :].rearrange("p h j -> p (h j)"), a2[:, :, :].rearrange("p a j -> p (a j)"), start=True, stop=True)
            transposes(lambda g: bank[7][:, tok(g)], lambda g: xbd[:, g, :], G2).then_inc(xT_ps, 1)
            for g in range(G2):
                pe.wait_ge(p3_ready, g + 1)
                transposes(lambda t: bank[3 - g][:, tok(t)], lambda t: p3[:, g, tok(t)], NT).then_inc(p3T_ps, 1)
            pe.wait_ge(max_ready, 1)
            pe.wait_ge(xT_ready, 1)
            mm(bank[7][0:1, 0:P], mx2[:, 0:1], ident[:, :], start=True, stop=True)
            mm(bank[7][0:1, P:2 * P], mx2[:, 1:2], ident[:, :], start=True, stop=True).then_inc(max_ps, 1)
            pe.wait_ge(p1_ready, 1)
            for g in range(G2):
                transposes(lambda t: bank[1 - g][:, tok(t)],
                           lambda t: p1[:, t * H + g * HG:t * H + (g + 1) * HG, :].rearrange("p h j -> p (h j)"), NT)\
                    .then_inc(p1T_ps, 1)
            pe.wait_ge(sinv_row, 1)
            mm(bank[7][:, 0:1], ones[0:1, :], srow[0:1, 3:4], start=True, stop=True).then_inc(sinv_ps, 1)
            pe.wait_ge(p3T_ready, 2)
            for g in range(G2):
                for t in range(NT):
                    ins = mm(bank[3][:, g * 256:(g + 1) * 256], p3T[:, g, t, :],
                             v_sb[:, t, g * 256:(g + 1) * 256], start=(t == 0), stop=(t == NT - 1))
            ins.then_inc(a3v_ps, 1)
            pe.wait_ge(z_ready, 1)
            conv(3)
            pe.wait_ge(a3v_ready, 1)
            with pe.Fori(0, PINV) as i:
                pe.wait_ge(z_ready, i + 1)
                pe.wait_ge(zT_ready, i + 1)
                for g in range(G2):
                    ins = mm(bank[2][:, tok(g)], xT[:, g, :], z[:, g, :], start=True, stop=True)
                ins.then_inc(pz_ps, 1)
                for g in range(G2):
                    ins = mm(bank[3][:, tok(g)], z[:, g, :], xT[:, g, :], start=True, stop=True)
                ins.then_inc(pz_ps, 1)
                pe.wait_ge(pzT_ready, i + 1)
                for n in range(2):
                    pe.wait_ge(t_ready, 3 * i + n + 1)
                    for g in range(G2):
                        ins = mm(bank[2 + n][:, tok(g)], pzT[:, g, :], tz[:, g, :], start=True, stop=True)
                    ins.then_inc(tz_ps, 1)
                pe.wait_ge(t_ready, 3 * i + 3)
                for g in range(G2):
                    ins = mm(bank[2][:, tok(g)], zT[:, g, :], tz[:, g, :], start=True, stop=True)
                ins.then_inc(zn_ps, 1)
                for g in range(G2):
                    ins = mm(bank[3][:, tok(g)], tz[:, g, :], zT[:, g, :], start=True, stop=True)
                ins.then_inc(zn_ps, 1)
            pe.wait_ge(zT_ready, PINV + 1)
            pe.wait_ge(z_ready, PINV + 1)
            for g in range(G2):
                ins = mm(bank[2][:, g * 256:(g + 1) * 256], zT[:, g, :], a3v[:, g, :], start=True, stop=True)
            ins.then_inc(m_ps, 1)
            pe.wait_ge(p1T_ready, 2)
            pe.wait_ge(m_ready, 1)
            for c in range(4):
                mm(bank[4 + c][:, :], m_bd[:, c // 2, (c % 2) * P:(c % 2 + 1) * P], p1T[:, c // 2, :],
                   start=False, stop=True, skip_group_check=True).then_inc(outT_ps, 1)
            pe.wait_ge(encw_in, 64)
            pe.wait_ge(outT_ready, 4)
            for t in range(NT):
                for c in range(4):
                    ins = mm(bank[0][:, tok(t)], outT[:, c, tok(t)], outw_sb[:, c, :], start=(c == 0), stop=(c == 3))
            ins.then_inc(xg_ps, 1)
            pe.wait_ge(enc0_ready, 1)
            transposes(lambda t: bank[1][:, tok(t)], lambda t: xn[:, t, :], NT).then_inc(encT_ps, 1)
            pe.wait_ge(encT_ready, 1)
            for t in range(NT):
                ins = mm(bank[3][:, t * QK:(t + 1) * QK], encT[:, tok(t)], wk_sb[:, :], start=True, stop=True)
            ins.then_inc(k_ps, 1)
            for t in range(NT):
                ins = mm(bank[2][:, t * QK:(t + 1) * QK], encT[:, tok(t)], wq_sb[:, :], start=True, stop=True)
            ins.then_inc(q_ps, 1)
            pe.sem_inc(kg_ps, 2)
            pe.sem_inc(g_done, 2)
            pe.wait_ge(ksp_ready, 1)
            mm(bank[4][:, 0:NT * NS * QK], zeros[:, 0:P], zeros[:, 0:NT * NS * QK], start=True, stop=False,
               skip_group_check=True)

            def gather(pair, s):
                pe.wait_ge(ohc_ready, 2 * pair + s + 1)
                pe.wait_ge(kv_ready, 2 * pair + s + 1)
                for j in range(EG):
                    for c in range(NT):
                        for n in range(NS):
                            ins = mm(bank[s][:, j * QK:(j + 1) * QK], oh_c[:, s, c, j * P:(j + 1) * P],
                                     ksp[:, c, n, :], start=(c == 0 and n == 0), stop=(c == NT - 1 and n == NS - 1))
                ins.then_inc(kg_ps, 1)

            def segment(pair, s):
                pe.wait_ge(ohr_ready, 2 * pair + s + 1)
                pe.wait_ge(kvs_ready, 2 * pair + s + 1)
                for j in range(EG):
                    for c in range(NT):
                        ins = mm(bank[4][:, c * NS * QK:(c + 1) * NS * QK], oh_r[:, s, j, tok(c)],
                                 kvs[:, s, j, :, :].rearrange("p n q -> p (n q)"), start=False, stop=False,
                                 skip_group_check=True)
                ins.then_inc(g_done, 1)

            gather(0, 0)
            with pe.Fori(0, NG // 2 - 1) as pair:
                gather(pair, 1)
                segment(pair, 0)
                gather(pair + 1, 0)
                segment(pair, 1)
            gather(NG // 2 - 1, 1)
            segment(NG // 2 - 1, 0)
            segment(NG // 2 - 1, 1)
            mm(bank[4][:, 0:NT * NS * QK], zeros[:, 0:P], zeros[:, 0:NT * NS * QK], start=False, stop=True,
               skip_group_check=True).then_inc(g_ps, 1)
            pe.wait_ge(araw_ready, 1)
            for t in range(NT):
                ins = mm(bank[5][0:1, tok(t)], araw[:, t:t + 1], ident[:, :], start=True, stop=True)
            ins.then_inc(arow_ps, 1)
            pe.wait_ge(arow_ready, 1)
            for t in range(NT):
                ins = mm(bank[6][:, t:t + 1], arow[0:1, tok(t)], ones[0:1, 0:1], start=True, stop=True)
            ins.then_inc(alpha_ps, 1)

            pe.wait_ge(comb_ready, 1)
            mm(bank[5][:, 0:E], ones[:, :], ksq[:, :], start=True, stop=True)
            mm(bank[5][:, E:2 * E], ones[:, :], comb[:, :], start=True, stop=True).then_inc(ksq_ps, 1)

            def router(b):
                pe.wait_ge(xnT_ready, B + b + 1)
                for t in range(b * NT, (b + 1) * NT):
                    ins = mm(bank[6][:, t * E:(t + 1) * E], xnT[:, tok(t)], comb[:, :], start=True, stop=True)
                return ins

            for b in range(B):
                pe.wait_ge(x2_ready, b + 1)
                transposes(lambda t: bank[b % 2][:, tok(t)], lambda t: x[:, b * NT + t, :], NT).then_inc(xnT_ps, 1)
                if b >= 1:
                    router(b - 1)
            router(B - 1).then_inc(logit_ps, 1)
            pe.wait_ge(chosen_ready, 1)
            pe.wait_ge(const_ready, 3)
            flat = chosen_b[:, :, :].rearrange("p t e -> p (t e)")
            mm(bank[0][:, :], upper[:, :], flat, start=True, stop=True).then_inc(prefix_ps, 1)
            mm(bank[1][:, :], ones_b[:, :], flat, start=True, stop=True).then_inc(prefix_ps, 1)
            pe.wait_ge(bexp_ready, 1)
            for c in range(2):
                ins = mm(bank[3][0:1, tok(c)], blk_exp[:, c:c + 1], ident[:, :], start=True, stop=True)
            ins.then_inc(bexp_ps, 1)
            mm(bank[2][:, 0:2 * NBLK], zeros[:, 0:P], zeros[:, 0:2 * NBLK], start=True, stop=False,
               skip_group_check=True)
            with pe.Fori(0, T // 4) as i:
                for s in range(4):
                    pe.wait_ge(hot_lane_ready, 4 * i + s + 1)
                    pe.wait_ge(hot_ready, 4 * i + s + 1)
                    for k in range(TOPK):
                        ins = mm(bank[2][:, 0:2 * NBLK], hot_lane[:, bass.ds(4 * i + s, 1), k, :]
                                 .rearrange("p t n -> p (t n)"), hot_blk[:, s % 2, k, :].bitcast(bf16), start=False,
                                 stop=False, skip_group_check=True)
                    ins.then_inc(hot_used, 1)
            mm(bank[2][:, 0:2 * NBLK], zeros[:, 0:P], zeros[:, 0:2 * NBLK], start=False, stop=True,
               skip_group_check=True).then_inc(table_ps, 1)

            def rows_T(g, s):
                pe.wait_ge(xg_in[s % RING], 16 * (g * (BG // RING) + s // RING + 1))
                freed(pe, xgT_ready, nth(g, s) - 1)
                nc.tensor.transpose(bank[slot(s)][:, 0:P], xg[:, s % RING, :], ident[:, :]).then_inc(xgT_ps, 1)

            def up(g, s):
                pe.wait_ge(xgT_ready, nth(g, s) + 1)
                pe.wait_ge(w1_ready, nth(g, s) + 1)
                for c in range(FC):
                    ins = mm(bank[2 + slot(s)][:, tok(c)], w1_now[:, slot(s), tok(c)], xgT[:, slot(s), :],
                             start=True, stop=True)
                ins.then_inc(up_ps, 1)

            def down(g, s, e):
                pe.wait_ge(h_ready, nth(g, s) + 1)
                freed(pe, y_ready, nth(g, s) - 1)
                for c in range(FC):
                    mm(bank[6 + slot(s)][:, 0:D], hT[:, slot(s), tok(c)], w2_sb[:, bass.ds(e, 1), c, :]
                       .rearrange("p a d -> p (a d)"), start=(c == 0), stop=False)
                mm(bank[6 + slot(s)][:, 0:D], ones_b[0:NS, :], b2_parts[:, bass.ds(e, 1), :]
                   .rearrange("p a d -> p (a d)"), start=False, stop=True).then_inc(down_ps, 1)

            def pe_group(g):
                e = experts(pe, BG * g - 1) if precedes(g, -1) else [None, *experts(pe, 0, BG - 1)]
                for s in range(BG):
                    up(g, s)
                    if follows(g, s + 1):
                        rows_T(g, s + 1)
                    if precedes(g, s - 1):
                        down(g, s - 1, e[s])

            pe.wait_ge(exp_ready, 1)
            pe.wait_ge(w_in, 48)
            pe.wait_ge(b2p_in, 16)
            rows_T(0, 0)
            group_loop(pe, pe_group)
            down(GROUPS, -1, experts(pe, NBLK - 1, 1)[0])


def kernel(**inputs):
    import numpy as np
    import concourse.bacc as bacc
    from concourse.bass_utils import run_bass_kernel_spmd

    a = {k.split("_", 2)[2]: np.asarray(v) for k, v in inputs.items()}
    E, F, D = a["w1"].shape
    P, DH = 128, 64
    H = a["qkv_w"].shape[1] // (3 * DH)
    taps = a["conv_w"].reshape(H, -1)
    K = taps.shape[1]
    conv_pad = np.zeros((H, 2 * P - 2 + K), taps.dtype)
    conv_pad[:, P - 1:P - 1 + K] = taps[:, ::-1]

    def heads(w):
        return w.reshape(D, H, DH).transpose(2, 1, 0)

    arrays = dict(
        dense=a["dense"], adj_rows=a["adj_rows"], adj_cols=a["adj_cols"], adj_vals=a["adj_vals"], wq=a["wq"],
        wk=a["wk"], wv_w=a["wv_w"], wv_b=a["wv_b"], qkv_w=a["qkv_w"], wq_t=heads(a["qkv_w"][:, :H * DH]),
        wk_t=heads(a["qkv_w"][:, H * DH:2 * H * DH]), out_w=a["out_w"], out_b=a["out_b"], conv_pad=conv_pad,
        keys_t=a["keys"].T, w1_t=a["w1"].transpose(2, 0, 1), b1_t=a["b1"].reshape(E, F // P, P).transpose(2, 0, 1),
        w2_t=a["w2"].reshape(E, D, F // P, P).transpose(3, 0, 2, 1), b2=a["b2"], rw_t=a["rw"].T, rb=a["rb"])
    arrays = {k: np.ascontiguousarray(v) for k, v in arrays.items()}
    nc = bacc.Bacc("TRN2", target_bir_lowering=False, num_devices=1)
    args = {k: nc.dram_tensor(f"in_{k}", v.shape, mybir.dt.from_np(v.dtype), kind="ExternalInput").ap()
            for k, v in arrays.items()}
    args["out"] = nc.dram_tensor("out_x", a["dense"].shape, mybir.dt.float32, kind="ExternalOutput").ap()
    sandwich_kernel(nc, **args)
    r = run_bass_kernel_spmd(nc, [{f"in_{k}": v for k, v in arrays.items()}], core_ids=[0])
    return r.results[0]["out_x"]
```
